# Optimizing a Trainium2 kernel written in Bass

```python
import numpy as np
import jax
import jax.numpy as jnp

def _softmax(x, axis=-1):
    return jax.nn.softmax(x, axis=axis)

def _gelu(x):
    return jax.nn.gelu(x, approximate=True)

def _silu(x):
    return jax.nn.silu(x)

def _sigmoid(x):
    return jax.nn.sigmoid(x)

def _layernorm(x, axis=-1, eps=1e-05):
    m = jnp.mean(x, axis=axis, keepdims=True)
    v = jnp.var(x, axis=axis, keepdims=True)
    return (x - m) / jnp.sqrt(v + eps)

def _scatter_add(tgt, idx, src, axis=0):
    return tgt.at[idx].add(src)

def _segment_sum(src, seg, n):
    return jax.ops.segment_sum(src, seg, n)
kernel_name = 'mk_seq_postln_d2_jaxref_r8_ade646'

def setup_inputs(seed: int=0):
    np.random.seed(seed)
    _w = jnp.asarray

    def _L0_attn_setup():
        import jax, jax.numpy as jnp
        import numpy as np
        import math
        B, S, D = (4, 256, 128)
        H, KV = (16, 4)
        HD = D // H
        GROUPS = H // KV

        def _alibi_slopes(n):
            start = 2.0 ** (-2.0 ** (-(math.log2(n) - 3)))
            return np.array([start * start ** i for i in range(n)], dtype=np.float32)
        key = jax.random.key(seed)
        ks = jax.random.split(key, 5)
        sc = 0.02
        return {'x': jax.random.normal(ks[0], (B, S, D), jnp.float32), 'Wq': jax.random.normal(ks[1], (D, H * HD), jnp.float32) * sc, 'Wk': jax.random.normal(ks[2], (D, KV * HD), jnp.float32) * sc, 'Wv': jax.random.normal(ks[3], (D, KV * HD), jnp.float32) * sc, 'Wo': jax.random.normal(ks[4], (H * HD, D), jnp.float32) * sc}
    _L0_attn_in = _L0_attn_setup()

    def _L0_ffn_setup():
        import jax, jax.numpy as jnp
        import numpy as np
        B, N, D = (4, 256, 128)
        SPARSITY = 0.01
        key = jax.random.key(seed)
        k1, k2, k3 = jax.random.split(key, 3)
        x = jax.random.normal(k1, (B, N, D), dtype=jnp.float32)
        spatial = jax.random.normal(k2, (D, D), dtype=jnp.float32) * 0.02
        freq = jnp.fft.fft(spatial, axis=-1)
        k = int(D * SPARSITY)
        mag = jnp.abs(freq)
        kth = jax.lax.top_k(mag, k)[0][:, -1:]
        w_sparse = jnp.where(mag >= kth, freq, 0.0 + 0j)
        bias = jax.random.normal(k3, (D,), dtype=jnp.float32) * 0.01
        return {'x': x, 'w_freq_real': jnp.real(w_sparse).astype(jnp.float32), 'w_freq_imag': jnp.imag(w_sparse).astype(jnp.float32), 'bias': bias}
    _L0_ffn_in = _L0_ffn_setup()

    def _L1_attn_setup():
        import jax, jax.numpy as jnp
        import numpy as np
        import math
        NUM_HEADS = 16
        SEGMENT_SIZE = 128
        DILATION = 2

        def hilbert_map(seq_len: int) -> np.ndarray:
            if seq_len <= 64:
                return np.arange(seq_len, dtype=np.int64)
            g = int(math.ceil(math.sqrt(seq_len)))
            fm = np.zeros(seq_len, dtype=np.int64)
            idx = 0
            for row in range(g):
                cols = range(g) if row % 2 == 0 else range(g - 1, -1, -1)
                for col in cols:
                    lp = row * g + col
                    if lp < seq_len and idx < seq_len:
                        fm[lp] = idx
                        idx += 1
            return fm
        key = jax.random.key(seed)
        k1, k2, k3 = jax.random.split(key, 3)
        B, S, D = (2, 1024, 128)
        x = jax.random.normal(k1, (B, S, D), dtype=jnp.float32)
        W_qkv = jax.random.normal(k2, (D, 3 * D), dtype=jnp.float32) * 0.02
        W_out = jax.random.normal(k3, (D, D), dtype=jnp.float32) * 0.02
        return {'x': x, 'W_qkv': W_qkv, 'W_out': W_out}
    _L1_attn_in = _L1_attn_setup()

    def _L1_ffn_setup():
        import jax, jax.numpy as jnp
        import numpy as np
        B, T, C, H, E, MIN_E = (4, 256, 128, 128, 16, 2)
        IS_CAUSAL = False

        def _forward(hidden_states, sim_matrix, gates, q_proj, k_proj, v_proj, o_proj):
            b, t, c = hidden_states.shape
            n = b * t
            x = hidden_states.reshape(n, c)
            xn = x / jnp.maximum(jnp.linalg.norm(x, axis=-1, keepdims=True), 1e-12)
            sn = sim_matrix / jnp.maximum(jnp.linalg.norm(sim_matrix, axis=0, keepdims=True), 1e-12)
            logits = xn @ sn - jax.nn.sigmoid(gates)
            gated = jax.nn.relu(logits)
            hard = (gated > 0).astype(gated.dtype)
            mask = gated + jax.lax.stop_gradient(hard - gated)
            inactive = jnp.sum(hard, axis=1) == 0
            _, fb_idx = jax.lax.top_k(logits, MIN_E)
            fb = jnp.zeros((n, logits.shape[1]), gated.dtype).at[jnp.arange(n)[:, None], fb_idx].set(1.0)
            put = jax.lax.stop_gradient(inactive[:, None].astype(gated.dtype) * fb)
            mask = mask * (1.0 - put) + put
            masked = jnp.where(mask > 0, gated, -jnp.inf)
            w = jax.nn.softmax(masked, axis=-1)

            def moe_proj(p):
                y = jnp.einsum('nc,ech->neh', x, p)
                return jnp.einsum('ne,neh->nh', w, y)
            q = moe_proj(q_proj).reshape(b, t, -1)
            k = moe_proj(k_proj).reshape(b, t, -1)
            v = moe_proj(v_proj).reshape(b, t, -1)
            h = q.shape[-1]
            scores = jnp.einsum('bth,bsh->bts', q, k) / jnp.sqrt(jnp.asarray(h, q.dtype))
            if IS_CAUSAL and t > 1:
                causal = jnp.tril(jnp.ones((t, t), bool))
                scores = jnp.where(causal[None], scores, -jnp.inf)
            attn = jax.nn.softmax(scores, axis=-1)
            o = jnp.einsum('bts,bsh->bth', attn, v).reshape(n, h)
            z = jnp.einsum('ne,nh->enh', w, o)
            out = jnp.einsum('enh,ehc->nc', z, o_proj)
            return out.reshape(b, t, c)
        key = jax.random.key(seed)
        ks = jax.random.split(key, 6)
        lim_qkv = float(np.sqrt(6.0 / (C + H)))
        inp = {'hidden_states': jax.random.normal(ks[0], (B, T, C), jnp.float32), 'sim_matrix': jax.random.normal(ks[1], (C, E), jnp.float32), 'gates': jnp.zeros((E,), jnp.float32), 'q_proj': jax.random.uniform(ks[2], (E, C, H), jnp.float32, -lim_qkv, lim_qkv), 'k_proj': jax.random.uniform(ks[3], (E, C, H), jnp.float32, -lim_qkv, lim_qkv), 'v_proj': jax.random.uniform(ks[4], (E, C, H), jnp.float32, -lim_qkv, lim_qkv), 'o_proj': jax.random.uniform(ks[5], (E, H, C), jnp.float32, -lim_qkv, lim_qkv)}
        return inp
    _L1_ffn_in = _L1_ffn_setup()
    _d = {'L0_attn_x': _L0_attn_in['x'], 'L0_attn_Wq': _L0_attn_in['Wq'], 'L0_attn_Wk': _L0_attn_in['Wk'], 'L0_attn_Wv': _L0_attn_in['Wv'], 'L0_attn_Wo': _L0_attn_in['Wo'], 'L0_ffn_w_freq_real': _L0_ffn_in['w_freq_real'], 'L0_ffn_w_freq_imag': _L0_ffn_in['w_freq_imag'], 'L0_ffn_bias': _L0_ffn_in['bias'], 'L1_attn_W_qkv': _L1_attn_in['W_qkv'], 'L1_attn_W_out': _L1_attn_in['W_out'], 'L1_ffn_sim_matrix': _L1_ffn_in['sim_matrix'], 'L1_ffn_gates': _L1_ffn_in['gates'], 'L1_ffn_q_proj': _L1_ffn_in['q_proj'], 'L1_ffn_k_proj': _L1_ffn_in['k_proj'], 'L1_ffn_v_proj': _L1_ffn_in['v_proj'], 'L1_ffn_o_proj': _L1_ffn_in['o_proj']}
    _x0 = _d['L0_attn_x']
    _d['L0_attn_x'] = jax.random.normal(jax.random.fold_in(jax.random.key(seed), 1), (2, 1024, 128), dtype=_x0.dtype)
    del _x0
    return _d

def reference(L0_attn_x, L0_attn_Wq, L0_attn_Wk, L0_attn_Wv, L0_attn_Wo, L0_ffn_w_freq_real, L0_ffn_w_freq_imag, L0_ffn_bias, L1_attn_W_qkv, L1_attn_W_out, L1_ffn_sim_matrix, L1_ffn_gates, L1_ffn_q_proj, L1_ffn_k_proj, L1_ffn_v_proj, L1_ffn_o_proj):

    def _L0_attn_ref(x, Wq, Wk, Wv, Wo):
        import jax, jax.numpy as jnp
        import numpy as np
        import math
        B, S, D = (4, 256, 128)
        H, KV = (16, 4)
        HD = D // H
        GROUPS = H // KV

        def _alibi_slopes(n):
            start = 2.0 ** (-2.0 ** (-(math.log2(n) - 3)))
            return np.array([start * start ** i for i in range(n)], dtype=np.float32)
        b, s, _ = x.shape
        scale = HD ** (-0.5)
        q = (x @ Wq).reshape(b, s, H, HD).transpose(0, 2, 1, 3)
        k = (x @ Wk).reshape(b, s, KV, HD).transpose(0, 2, 1, 3)
        v = (x @ Wv).reshape(b, s, KV, HD).transpose(0, 2, 1, 3)
        k = jnp.repeat(k, GROUPS, axis=1)
        v = jnp.repeat(v, GROUPS, axis=1)
        attn = jnp.einsum('bhqd,bhkd->bhqk', q, k) * scale
        slopes = jnp.asarray(_alibi_slopes(H))
        pos = jnp.arange(s, dtype=jnp.float32)
        rel = pos[None, :] - pos[:, None]
        attn = attn + slopes[None, :, None, None] * rel[None, None, :, :]
        attn = jax.nn.softmax(attn, axis=-1)
        out = jnp.einsum('bhqk,bhkd->bhqd', attn, v)
        out = out.transpose(0, 2, 1, 3).reshape(b, s, H * HD)
        return out @ Wo

    def _L0_ffn_ref(x, w_freq_real, w_freq_imag, bias):
        import jax, jax.numpy as jnp
        import numpy as np
        B, N, D = (4, 256, 128)
        SPARSITY = 0.01
        w = jax.lax.complex(w_freq_real, w_freq_imag)
        x_freq = jnp.fft.fft(x, axis=-1)
        y_freq = jnp.einsum('bnd,do->bno', x_freq, w)
        y = jnp.real(jnp.fft.ifft(y_freq, axis=-1))
        return y + bias

    def _L1_attn_ref(x, W_qkv, W_out):
        import jax, jax.numpy as jnp
        import numpy as np
        import math
        NUM_HEADS = 16
        SEGMENT_SIZE = 128
        DILATION = 2

        def hilbert_map(seq_len: int) -> np.ndarray:
            if seq_len <= 64:
                return np.arange(seq_len, dtype=np.int64)
            g = int(math.ceil(math.sqrt(seq_len)))
            fm = np.zeros(seq_len, dtype=np.int64)
            idx = 0
            for row in range(g):
                cols = range(g) if row % 2 == 0 else range(g - 1, -1, -1)
                for col in cols:
                    lp = row * g + col
                    if lp < seq_len and idx < seq_len:
                        fm[lp] = idx
                        idx += 1
            return fm
        B, S, Dm = x.shape
        H, Dh = (NUM_HEADS, Dm // NUM_HEADS)
        seg, dil = (SEGMENT_SIZE, DILATION)
        scale = Dh ** (-0.5)
        qkv = (x @ W_qkv).reshape(B, S, 3, H, Dh)
        q = jnp.transpose(qkv[:, :, 0], (0, 2, 1, 3))
        k = jnp.transpose(qkv[:, :, 1], (0, 2, 1, 3))
        v = jnp.transpose(qkv[:, :, 2], (0, 2, 1, 3))
        m = jnp.asarray(hilbert_map(S))
        q, k, v = (q[:, :, m], k[:, :, m], v[:, :, m])
        nseg = S // seg
        qs = q.reshape(B, H, nseg, seg, Dh)
        ks = k.reshape(B, H, nseg, seg, Dh)[:, :, :, ::dil]
        vs = v.reshape(B, H, nseg, seg, Dh)[:, :, :, ::dil]
        scores = jnp.einsum('bhnqd,bhnkd->bhnqk', qs, ks) * scale
        attn = jax.nn.softmax(scores, axis=-1)
        out = jnp.einsum('bhnqk,bhnkd->bhnqd', attn, vs).reshape(B, H, S, Dh)
        inv = jnp.argsort(m)
        out = out[:, :, inv]
        out = jnp.transpose(out, (0, 2, 1, 3)).reshape(B, S, Dm)
        return out @ W_out

    def _L1_ffn_ref(hidden_states, sim_matrix, gates, q_proj, k_proj, v_proj, o_proj):
        import jax, jax.numpy as jnp
        import numpy as np
        B, T, C, H, E, MIN_E = (4, 256, 128, 128, 16, 2)
        IS_CAUSAL = False

        def _forward(hidden_states, sim_matrix, gates, q_proj, k_proj, v_proj, o_proj):
            b, t, c = hidden_states.shape
            n = b * t
            x = hidden_states.reshape(n, c)
            xn = x / jnp.maximum(jnp.linalg.norm(x, axis=-1, keepdims=True), 1e-12)
            sn = sim_matrix / jnp.maximum(jnp.linalg.norm(sim_matrix, axis=0, keepdims=True), 1e-12)
            logits = xn @ sn - jax.nn.sigmoid(gates)
            gated = jax.nn.relu(logits)
            hard = (gated > 0).astype(gated.dtype)
            mask = gated + jax.lax.stop_gradient(hard - gated)
            inactive = jnp.sum(hard, axis=1) == 0
            _, fb_idx = jax.lax.top_k(logits, MIN_E)
            fb = jnp.zeros((n, logits.shape[1]), gated.dtype).at[jnp.arange(n)[:, None], fb_idx].set(1.0)
            put = jax.lax.stop_gradient(inactive[:, None].astype(gated.dtype) * fb)
            mask = mask * (1.0 - put) + put
            masked = jnp.where(mask > 0, gated, -jnp.inf)
            w = jax.nn.softmax(masked, axis=-1)

            def moe_proj(p):
                y = jnp.einsum('nc,ech->neh', x, p)
                return jnp.einsum('ne,neh->nh', w, y)
            q = moe_proj(q_proj).reshape(b, t, -1)
            k = moe_proj(k_proj).reshape(b, t, -1)
            v = moe_proj(v_proj).reshape(b, t, -1)
            h = q.shape[-1]
            scores = jnp.einsum('bth,bsh->bts', q, k) / jnp.sqrt(jnp.asarray(h, q.dtype))
            if IS_CAUSAL and t > 1:
                causal = jnp.tril(jnp.ones((t, t), bool))
                scores = jnp.where(causal[None], scores, -jnp.inf)
            attn = jax.nn.softmax(scores, axis=-1)
            o = jnp.einsum('bts,bsh->bth', attn, v).reshape(n, h)
            z = jnp.einsum('ne,nh->enh', w, o)
            out = jnp.einsum('enh,ehc->nc', z, o_proj)
            return out.reshape(b, t, c)
        return _forward(hidden_states, sim_matrix, gates, q_proj, k_proj, v_proj, o_proj)
    x = L0_attn_x
    x = _layernorm(x + _L0_attn_ref(x, L0_attn_Wq, L0_attn_Wk, L0_attn_Wv, L0_attn_Wo), axis=-1)
    x = _layernorm(x + _L0_ffn_ref(x, L0_ffn_w_freq_real, L0_ffn_w_freq_imag, L0_ffn_bias), axis=-1)
    x = _layernorm(x + _L1_attn_ref(x, L1_attn_W_qkv, L1_attn_W_out), axis=-1)
    x = _layernorm(x + _L1_ffn_ref(x, L1_ffn_sim_matrix, L1_ffn_gates, L1_ffn_q_proj, L1_ffn_k_proj, L1_ffn_v_proj, L1_ffn_o_proj), axis=-1)
    return x

_drawn_inputs = setup_inputs


def setup_inputs(seed=0):
    import zlib

    import numpy as np

    out = dict(_drawn_inputs(seed))
    spreads = {'L1_ffn_gates': (0.0, 0.309)}
    factors = {'L0_attn_Wq': 8.0,
     'L0_attn_Wk': 8.0,
     'L0_attn_Wv': 3.909,
     'L0_attn_Wo': 4.758,
     'L0_ffn_bias': 5.677,
     'L1_attn_W_qkv': 7.988,
     'L1_attn_W_out': 7.992,
     'L1_ffn_q_proj': 5.269,
     'L1_ffn_k_proj': 5.233}
    for name, (base, spread) in spreads.items():
        noise = np.random.default_rng([zlib.crc32(name.encode()), seed]).standard_normal(out[name].shape)
        drawn = base * np.exp(spread * noise) if base else spread * noise
        out[name] = jnp.asarray(drawn.astype(out[name].dtype))
    for name, factor in factors.items():
        out[name] = (out[name] * factor).astype(out[name].dtype)
    return out
```

```python
from contextlib import ExitStack

import numpy as np

import concourse.bass as bass
from concourse import mybir

F32 = mybir.dt.float32
BF16 = mybir.dt.bfloat16
ALU = mybir.AluOpType
ACT = mybir.ActivationFunctionType
AX_X = mybir.AxisListType.X

P = 128
D = 128
NB, S = 2, 1024
NT = NB * S // P
QUAD = 4
NQ = NT // QUAD
QN = QUAD * P
H, DH = 16, 8
G, HG = 4, 4
NS = NB * G
KB = S // P
SEG, KSEG = 128, 64
PARTS = 3
ROWS = PARTS * PARTS * DH
BIAS_ROW = ROWS
N_BIAS = 6
MAX_ROW = 96
K_MAX = 96
K_EXP = 98
RING = 4
LEAD = 4
STEPS = KB * HG
E = 16
EPS = 1e-5
W3 = 3 * D
YR = 4


def build(nc, x, wq, wk, wv, wo, w_re, w_im, bias, w_qkv, w_out, sim, gates, p_q, p_k, p_v, p_o,
          ident, c_cos, c_sin, c_nsin, slopes, kpos, rank, out):
    scale = float(DH) ** -0.5
    scale_moe = float(D) ** -0.5
    dq = [nc.dram_tensor(f"q_parts_{n}", [NB * H, PARTS * DH, S], BF16).ap() for n in range(2)]
    dk0 = nc.dram_tensor("k_parts_0", [NS, ROWS, S], BF16).ap()
    dk1 = nc.dram_tensor("k_parts_1", [NB * H, ROWS, S // 2], BF16).ap()

    with ExitStack() as ctx:
        def sb(name, shape, dt=F32):
            return ctx.enter_context(nc.sbuf_tensor(name, shape, dt))

        def sem(name):
            return ctx.enter_context(nc.semaphore(name))

        ident_sb = sb("ident_sb", [P, P])
        ones = sb("ones", [P, P])
        cos_sb, sin_sb, nsin_sb = sb("cos_sb", [P, P]), sb("sin_sb", [P, P]), sb("nsin_sb", [P, P])
        w_qkv0 = sb("w_qkv0", [P, 3, P])
        wo_sb = sb("wo_sb", [P, P])
        wre_sb, wim_sb = sb("wre_sb", [P, P]), sb("wim_sb", [P, P])
        a_re, a_im, m_sb = sb("a_re", [P, P]), sb("a_im", [P, P]), sb("m_sb", [P, P])
        bias_sb = sb("bias_sb", [P, P])
        w_qkv1 = sb("w_qkv1", [P, W3])
        wout_sb = sb("wout_sb", [P, P])
        sim_sb, sim_n = sb("sim_sb", [P, E]), sb("sim_n", [P, E])
        gate_sb = sb("gate_sb", [P, E])
        rank_sb = sb("rank_sb", [P, E])
        half = sb("half", [P, NT])
        phalf = sb("phalf", [P, NT])
        xa = sb("xa", [P, NT, D])
        xb = sb("xb", [P, NT, D])
        xT = sb("xT", [P, NT * P])
        qk = sb("qk", [P, 2 * QN])
        qk_r = sb("qk_r", [P, 2 * QN])
        qk_p = sb("qk_p", [P, PARTS, 2 * QN], BF16)
        q_rep = sb("q_rep", [P, RING * HG * S], BF16)
        k_rep0 = sb("k_rep0", [P, RING * S], BF16)
        k_rep1 = sb("k_rep1", [P, RING * HG * S // 2], BF16)
        v_blk = sb("v_blk", [P, NT * 8 * 32])
        v_all = v_blk[:, 0:NS * KB * 32]
        v_cur = sb("v_cur", [P, KB * 32])
        probs = sb("probs", [P, 2, HG * S])
        o_seg = probs[:, 1, :]
        big = sb("big", [P, NS * S])
        we_qkv = big[:, 0:E * W3]
        we_o = big[:, E * W3:E * (W3 + D)]
        mx2 = sb("mx2", [P, 2 * STEPS])
        mx = sb("mx", [P, STEPS])
        mrow = sb("mrow", [STEPS, 2, P], BF16)
        att = sb("att", [P, QUAD * D])
        attT = sb("attT", [P, 2, QN])
        rec = sb("rec", [P, 2, H])
        st = sb("st", [P, QUAD, 6])
        mv = sb("mv", [P, QUAD, 2])
        ve = sb("ve", [P, QUAD])
        rstd = sb("rstd", [P, QUAD])
        res = sb("res", [P, QUAD, D])
        tick = sb("tick", [P, 8])

        psum = [ctx.enter_context(nc.psum_tensor(n, [P, w], F32))
                for n, w in (("ps_max", 2 * QN), ("ps_s", 4 * QN), ("ps_o", 2 * QN))]
        ps_max, ps_s, ps_o = psum

        def bank(n, count=1):
            t, at = ((ps_max, n), (ps_s, n - 2), (ps_o, n - 6))[0 if n < 2 else 1 if n < 6 else 2]
            return t[:, at * QN:(at + count) * QN]

        rt = [sb(f"rt{n}", [P, NT, E]) for n in range(6)]
        r1 = [sb(f"r1_{n}", [P, NT]) for n in range(4)]
        w_rt = sb("w_rt", [P, NT, E])

        f_q = q_rep[:].bitcast(F32)
        qkv = f_q[:, 0:NT * W3]
        x_cur = f_q[:, 6144:6144 + 2 * P].rearrange("p (b n) -> p b n", b=2)
        acc = f_q[:, 6400:6400 + 2 * 2 * W3].rearrange("p (b c n) -> p b c n", b=2, c=2)
        f_p = probs[:].rearrange("p a b -> p (a b)")
        qT_all = f_p[:, 0:2048]
        kT_all = f_p[:, 2048:4096]
        p_cur = f_p[:, 4096:5120]
        pT_cur = f_p[:, 5120:6144]
        tok_cur = f_p[:, 6144:6144 + 2 * W3].rearrange("p (b n) -> p b n", b=2)
        q_cur = f_p[:, 6912:7040]
        o_cur = f_p[:, 7040:7168]
        oT_cur = f_p[:, 7168:7296]
        y_acc = f_p[:, 7296:7552].rearrange("p (b n) -> p b n", b=2)
        w_cur = f_p[:, 7552:7568]
        x_tok = f_p[:, 7568:7696]
        y_out = f_p[:, 7696:7824]
        m_cur = f_p[:, 7824:7828]

        ld_x, ld_c, ld_w1, ld_bias, ld_we = (sem(n) for n in ("ld_x", "ld_c", "ld_w1", "ld_bias", "ld_we"))
        const_set = sem("const_set")
        rows_set = sem("rows_set")
        wq_scaled = sem("wq_scaled")
        dft_a, dft_a_sb, dft_m, dft_m_sb = sem("dft_a"), sem("dft_a_sb"), sem("dft_m"), sem("dft_m_sb")
        dve_step = sem("dve_step")
        xT_ps = [sem(f"xT_ps{n}") for n in range(2)]
        xT_sb = [sem(f"xT_sb{n}") for n in range(2)]
        qk_ps = [sem(f"qk_ps{n}") for n in range(2)]
        qk_sb = [sem(f"qk_sb{n}") for n in range(2)]
        qk_split = [sem(f"qk_split{n}") for n in range(2)]
        q_out = [sem(f"q_out{n}") for n in range(2)]
        k_out = [sem(f"k_out{n}") for n in range(2)]
        v_ps = [sem(f"v_ps{n}") for n in range(2)]
        v_sb = [sem(f"v_sb{n}") for n in range(2)]
        rep_loaded = [sem(f"rep_loaded{n}") for n in range(2)]
        max_ps = [sem(f"max_ps{n}") for n in range(2)]
        max_done = [sem(f"max_done{n}") for n in range(2)]
        max_all = [sem(f"max_all{n}") for n in range(2)]
        mrow_set = [sem(f"mrow_set{n}") for n in range(2)]
        mrow_in = [sem(f"mrow_in{n}") for n in range(2)]
        s_ps = [sem(f"s_ps{n}") for n in range(2)]
        s_free = [sem(f"s_free{n}") for n in range(2)]
        p_free = [sem(f"p_free{n}") for n in range(2)]
        v_cur_set = sem("v_cur_set")
        o_free = [sem(f"o_free{n}") for n in range(2)]
        ot_ps = [sem(f"ot_ps{n}") for n in range(2)]
        ot_read = [sem(f"ot_read{n}") for n in range(2)]
        at_ps = [sem(f"at_ps{n}") for n in range(2)]
        at_sb = [sem(f"at_sb{n}") for n in range(2)]
        wo_ps = [sem(f"wo_ps{n}") for n in range(2)]
        ln_res = [sem(f"ln_res{n}") for n in range(4)]
        ln_var = [sem(f"ln_var{n}") for n in range(4)]
        ln_std = [sem(f"ln_std{n}") for n in range(4)]
        ln_out = [sem(f"ln_out{n}") for n in range(4)]
        ft_ps, ft_sb, fm_ps = sem("ft_ps"), sem("ft_sb"), sem("fm_ps")
        xsel_set, ksel_sb = sem("xsel_set"), sem("ksel_sb")
        x3T_ps, x3T_sb = sem("x3T_ps"), sem("x3T_sb")
        sim_sq, sim_ss, sim_root, sim_root_done, sim_ready = (
            sem(n) for n in ("sim_sq", "sim_ss", "sim_root", "sim_root_done", "sim_ready"))
        lg_ps, gate_exp, nrm_ss, nrm_root = sem("lg_ps"), sem("gate_exp"), sem("nrm_ss"), sem("nrm_root")
        ex_in, ex_out, w_ready = sem("ex_in"), sem("ex_out"), sem("w_ready")
        xc_set, y_ps, y_free, tok_set, kq_ps, kq_sb = (
            sem(n) for n in ("xc_set", "y_ps", "y_free", "tok_set", "kq_ps", "kq_sb"))
        tok_free = sem("tok_free")
        q_set, sc_ps, nmax_set, p_set, pt_ps, pt_sb, o_ps, o_sb, ott_ps, ott_sb = (
            sem(n) for n in ("q_set", "sc_ps", "nmax_set", "p_set", "pt_ps", "pt_sb", "o_ps", "o_sb", "ott_ps",
                             "ott_sb"))
        z_ps, z_free, w_set, fin_var, fin_std, fin_set, stored = (
            sem(n) for n in ("z_ps", "z_free", "w_set", "fin_var", "fin_std", "fin_set", "stored"))
        layer0_over = sem("layer0_over")

        out_t = out.rearrange("b (t p) d -> p (b t) d", p=P)

        block = ctx.enter_context(nc.Block())

        @block.sync
        def _(sp):
            xv = x.rearrange("b (t p) d -> p (b t) d", p=P)
            for q in range(NQ):
                sp.dma_start(xa[:, q * QUAD:(q + 1) * QUAD, :], xv[:, q * QUAD:(q + 1) * QUAD, :]).then_inc(ld_x, 16)
                if q == 0:
                    sp.dma_start(ident_sb[:], ident).then_inc(ld_c, 16)
                    sp.dma_start(w_qkv0[:, 0, :], wq).then_inc(ld_c, 16)
                    sp.dma_start(w_qkv0[:, 1, :].rearrange("p (r n) -> p r n", r=HG),
                                 wk.unsqueeze(1).broadcast_to([P, HG, G * DH])).then_inc(ld_c, 16)
                    sp.dma_start(w_qkv0[:, 2, 0:G * DH], wv).then_inc(ld_c, 16)
            for dst, src in ((cos_sb, c_cos), (sin_sb, c_sin), (nsin_sb, c_nsin), (wre_sb, w_re), (wim_sb, w_im),
                             (wo_sb, wo), (w_qkv1, w_qkv), (wout_sb, w_out), (sim_sb, sim), (rank_sb, rank)):
                sp.dma_start(dst[:], src).then_inc(ld_w1, 16)
            sp.dma_start(bias_sb[:], bias.unsqueeze(0).broadcast_to([P, D])).then_inc(ld_bias, 16)
            sp.dma_start(gate_sb[:], gates.unsqueeze(0).broadcast_to([P, E])).then_inc(ld_bias, 16)

            def loaded(layer, s):
                return (s * 6 + RING) * 16 if layer == 0 else s * 5 * 16

            def store_q(layer, q):
                sp.wait_ge(qk_split[layer], q + 1)
                b, c0 = q // 2, (q % 2) * QN
                for i in range(PARTS):
                    sp.dma_start(dq[layer][b * H:(b + 1) * H, i * DH:(i + 1) * DH, c0:c0 + QN],
                                 qk_p[:, i, 0:QN]).then_inc(q_out[layer], 16)

            def load_rep(layer, s):
                slot = s % RING
                for h in range(HG):
                    sp.dma_start(q_rep[0:ROWS, bass.ds(slot * HG * S + h * S, S)],
                                 dq[layer][bass.ds(s * HG + h, 1)].squeeze(0).unsqueeze(0).broadcast_to(
                                     [PARTS, PARTS * DH, S])).then_inc(rep_loaded[layer], 16)
                if layer == 0:
                    sp.dma_start(k_rep0[0:ROWS, bass.ds(slot * S, S)],
                                 dk0[bass.ds(s, 1)].squeeze(0)).then_inc(rep_loaded[0], 16)
                    sp.dma_start(q_rep[BIAS_ROW:BIAS_ROW + N_BIAS, bass.ds(slot * HG * S, HG * S)],
                                 slopes[bass.ds(s % G, 1)].squeeze(0)).then_inc(rep_loaded[0], 16)
                else:
                    sp.dma_start(k_rep1[0:ROWS, bass.ds(slot * HG * S // 2, HG * S // 2)].rearrange(
                                     "p (h n) -> p h n", h=HG),
                                 dk1[bass.ds(s * HG, HG)].rearrange("h r n -> r h n")).then_inc(rep_loaded[1], 16)

            def load_mrow(layer, s):
                at = (s % RING) * (HG * S)
                at = at if isinstance(s, int) else sp.snap(at)
                sp.wait_ge(mrow_set[layer], s + 1)
                for part in range(2):
                    dst = q_rep[MAX_ROW + part:MAX_ROW + part + 1, bass.ds(at, HG * S)]
                    sp.dma_start(dst.rearrange("o (r n) -> o r n", n=P), mrow[:, part, :]).then_inc(mrow_in[layer], 16)

            for layer in range(2):
                for q in range(NQ):
                    store_q(layer, q)
                    if q % 2 == 1:
                        sp.wait_ge(q_out[layer], (q + 1) * PARTS * 16)
                        sp.wait_ge(k_out[layer], (q + 1) * ROWS // DH * 16)
                        if layer == 0 and q == 1:
                            sp.wait_ge(rows_set, 3)
                            for slot in range(RING):
                                sp.dma_start(k_rep0[BIAS_ROW:BIAS_ROW + N_BIAS, slot * S:(slot + 1) * S],
                                             kpos).then_inc(rep_loaded[0], 16)
                        if q == 1:
                            if layer == 1:
                                sp.wait_ge(rows_set, 5)
                                sp.wait_ge(s_ps[0], NS * STEPS)
                            for s in range(RING):
                                if s:
                                    sp.wait_ge(rep_loaded[layer], loaded(layer, s))
                                load_rep(layer, s)
                load_mrow(layer, 0)
                done_of = (STEPS if layer == 0 else 2)
                with sp.Fori(0, NS - RING) as s:
                    load_mrow(layer, s + 1)
                    sp.wait_ge(s_ps[layer], done_of * (s + 1))
                    sp.wait_ge(rep_loaded[layer], loaded(layer, s + RING))
                    sp.wait_ge(rows_set, 5)
                    load_rep(layer, s + RING)
                with sp.Fori(NS - RING, NS - 1) as s:
                    load_mrow(layer, s + 1)
                if layer == 0:
                    sp.wait_ge(ot_ps[0], NT)
                    for n, p in enumerate((p_q, p_k, p_v)):
                        sp.dma_start(we_qkv.rearrange("p (e n) -> p e n", e=E)[:, :, n * D:(n + 1) * D],
                                     p.rearrange("e c h -> c e h")).then_inc(ld_we, 16)
                    sp.dma_start(we_o.rearrange("p (e n) -> p e n", e=E),
                                 p_o.rearrange("e c h -> c e h")).then_inc(ld_we, 16)
            with sp.Fori(0, NT) as t:
                sp.wait_ge(fin_set, t + 1)
                sp.wait_ge(fin_set, 1)
                sp.dma_start(out_t[:, bass.ds(t, 1), :].squeeze(1), y_out).then_inc(stored, 16)
            sp.wait_ge(stored, 16 * (NT + 1))

        @block.gpsimd
        def _(pool):
            steps = [0]

            def fill(ap, value):
                pool.memset(ap, value).then_inc(const_set, 1)
                steps[0] += 1
                pool.wait_ge(const_set, steps[0])

            fill(ones[:], 1.0)
            fill(v_all, 0.0)
            fill(v_all.rearrange("p (n c) -> p n c", c=32)[:, :, DH:DH + 1], 1.0)
            fill(half[:], -0.5)
            fill(phalf[:], 0.5)

            def store_k(layer, q):
                pool.wait_ge(qk_split[layer], q + 1)
                b, n = q // 2, QN // (1 + layer)
                c0 = (q % 2) * n
                for j in range(PARTS):
                    for i in range(PARTS):
                        r = (j * PARTS + i) * DH
                        if layer == 0:
                            dst, src = dk0[b * G:(b + 1) * G], qk_p[0:G * DH, j, QN:QN + n]
                        else:
                            dst, src = dk1[b * H:(b + 1) * H], qk_p[:, j, QN:QN + n]
                        pool.dma_start(dst[:, r:r + DH, c0:c0 + n], src).then_inc(k_out[layer], 16)

            def root(n, q):
                pool.wait_ge(ln_var[n], q + 1)
                pool.tensor_tensor(rstd[:], ve[:], half[:, 0:QUAD], ALU.pow).then_inc(ln_std[n], 1)

            for q in range(NQ):
                store_k(0, q)
            with pool.Fori(0, NS) as s:
                pool.wait_ge(p_free[0], KB * s + 2)
                pool.tensor_copy(v_cur[:], v_all[:, bass.ds(s * KB * 32, KB * 32)]).then_inc(v_cur_set, 1)
            pool.wait_ge(p_free[0], KB * NS + 2)
            pool.wait_ge(v_cur_set, NS)
            vb = v_blk.rearrange("p (n c) -> p n c", c=32)
            fill(v_blk[:], 0.0)
            fill(vb[0:KSEG, :, DH:DH + 1], 1.0)
            fill(vb[KSEG:P, :, 16 + DH:16 + DH + 1], 1.0)
            for n in range(2):
                for q in range(NQ):
                    root(n, q)
            for q in range(NQ):
                store_k(1, q)
            for q in range(NQ):
                root(2, q)
            pool.wait_ge(sim_root, 1)
            pool.tensor_tensor(sim_n[:], sim_n[:], phalf[:, 0:E], ALU.pow).then_inc(sim_root_done, 1)
            pool.wait_ge(nrm_ss, 1)
            pool.tensor_tensor(r1[0][:], r1[0][:], phalf[:], ALU.pow).then_inc(nrm_root, 1)
            pool.wait_ge(kq_sb, NT)
            pool.tensor_copy(q_cur, qT_all[:, 0:P]).then_inc(q_set, 1)
            with pool.Fori(0, NT) as t:
                pool.wait_ge(sc_ps, t + 2)
                pool.tensor_copy(q_cur, qT_all[:, bass.ds((t + 1) % NT * P, P)]).then_inc(q_set, 1)
                pool.wait_ge(fin_var, t + 1)
                pool.tensor_tensor(rstd[:, 0:1], ve[:, 0:1], half[:, 0:1], ALU.pow).then_inc(fin_std, 1)

        @block.tensor
        def _(pe):
            def quad_transposes(src, q, dst):
                for t in range(QUAD):
                    mm = pe.transpose(dst[:, t * P:(t + 1) * P], src[:, q * QUAD + t, :], ident_sb[:])
                return mm

            pe.wait_ge(ld_c, 4 * 16)
            for q in range(NQ):
                pe.wait_ge(ld_x, NQ * 16)
                if q >= 2:
                    pe.wait_ge(xT_sb[0], q - 1)
                quad_transposes(xa, q, bank(q % 2)).then_inc(xT_ps[0], 1)
                if q == 0:
                    pe.wait_ge(wq_scaled, 1)
                pe.wait_ge(xT_sb[0], q + 1)
                if q >= 2:
                    pe.wait_ge(qk_sb[0], q - 1)
                xq = xT[:, q * QN:(q + 1) * QN]
                pair = bank(2 + 2 * (q % 2), 2)
                pe.matmul(pair[:, 0:QN], w_qkv0[:, 0, :], xq, start=True, stop=True)
                pe.matmul(pair[:, QN:2 * QN], w_qkv0[:, 1, :], xq, start=True, stop=True).then_inc(qk_ps[0], 1)
                if q >= 2:
                    pe.wait_ge(v_sb[0], q - 1)
                for t in range(QUAD):
                    mm = pe.matmul(bank(6 + q % 2)[:, t * 32:(t + 1) * 32], xq[:, t * P:(t + 1) * P],
                                   w_qkv0[:, 2, 0:G * DH], start=True, stop=True)
                mm.then_inc(v_ps[0], 1)
            pe.wait_ge(ld_w1, 10 * 16)
            pe.wait_ge(xT_sb[0], NQ)
            pe.matmul(bank(0)[:, 0:P], wre_sb[:], cos_sb[:], start=True, stop=False)
            pe.matmul(bank(0)[:, 0:P], wim_sb[:], sin_sb[:], start=False, stop=True)
            pe.matmul(bank(1)[:, 0:P], wim_sb[:], cos_sb[:], start=True, stop=False)
            pe.matmul(bank(1)[:, 0:P], wre_sb[:], nsin_sb[:], start=False, stop=True).then_inc(dft_a, 1)
            pe.wait_ge(dft_a_sb, 2)
            pe.matmul(bank(0)[:, 0:P], a_re[:], cos_sb[:], start=True, stop=False)
            pe.matmul(bank(0)[:, 0:P], a_im[:], nsin_sb[:], start=False, stop=True).then_inc(dft_m, 1)

            def max_pair(s, k):
                h, qb = k // KB, k % KB
                slot = s % RING
                for i in range(2):
                    n = s * (2 * STEPS + 2) + 2 * k + i
                    if not isinstance(n, int) or n >= 2:
                        pe.wait_ge(max_done[0], n - (2 * k + i > 0))
                    pe.matmul(bank(i), q_rep[0:K_MAX, bass.ds(slot * HG * S + h * S + qb * P, P)],
                              k_rep0[0:K_MAX, bass.ds(slot * S + i * QN, QN)],
                              start=True, stop=True).then_inc(max_ps[0], 1)

            def max_rows(s):
                pe.wait_ge(max_all[0], s + 1)
                pe.transpose(bank(0)[0:STEPS, 0:P], mx[:], ident_sb[:]).then_inc(max_ps[0], 2)

            def load_wait(s):
                pe.wait_ge(rep_loaded[0], (RING + 6 * (s + 1)) * 16)

            def stage(s, last):
                slot = s % RING
                pe.wait_ge(mrow_in[0], 32 * (s + 1))
                for kb in range(KB):
                    for h in range(HG):
                        k = kb * HG + h
                        pe.wait_ge(s_free[0], s * STEPS + k + 1)
                        for i in range(2):
                            mm = pe.matmul(bank(2 + 2 * (k % 2) + i),
                                           k_rep0[0:K_EXP, bass.ds(slot * S + kb * P, P)],
                                           q_rep[0:K_EXP, bass.ds(slot * HG * S + h * S + i * QN, QN)],
                                           start=True, stop=True)
                        mm.then_inc(s_ps[0], 1)
                        if last < 2:
                            if k < STEPS - LEAD:
                                max_pair(s + 1, k + LEAD)
                            else:
                                if k == STEPS - LEAD:
                                    max_rows(s + 1)
                                    if last == 0:
                                        load_wait(s + 2)
                                if last == 0:
                                    max_pair(s + 2, k - STEPS + LEAD)
                        if h % 2 == 1 and kb > 0:
                            out_half(s, kb - 1, h // 2)
                for i in range(2):
                    out_half(s, KB - 1, i)

            def out_half(s, kb, i):
                pe.wait_ge(s_free[0], s * STEPS + (kb + 1) * HG + 2)
                if kb == 0 and i == 0:
                    pe.wait_ge(v_cur_set, s + 1)
                    pe.wait_ge(o_free[0], s + 1)
                for h in range(HG):
                    mm = pe.matmul(bank(6 + i)[32 * h:32 * h + 32, :], v_cur[:, kb * 32:(kb + 1) * 32],
                                   probs[:, kb % 2, h * S + i * QN:h * S + (i + 1) * QN],
                                   start=(kb == 0), stop=(kb == KB - 1), tile_position=(0, 32 * h))
                if i == 1:
                    mm.then_inc(p_free[0], 1)

            pe.wait_ge(dft_m_sb, 1)
            pe.wait_ge(qk_sb[0], NQ)
            pe.wait_ge(v_sb[0], NQ)
            load_wait(0)
            for k in range(STEPS):
                max_pair(0, k)
            max_rows(0)
            load_wait(1)
            for k in range(LEAD):
                max_pair(1, k)
            with pe.Fori(0, NS - 2) as s:
                stage(s, 0)
            stage(NS - 2, 1)
            stage(NS - 1, 2)

            def heads_to_rows(layer, source):
                for t in range(NT):
                    if t >= 8:
                        pe.wait_ge(ot_read[layer], t - 7)
                    for g in range(G):
                        mm = pe.transpose(bank(t % 8)[:, g * P:(g + 1) * P], source(t, g), ident_sb[:])
                    mm.then_inc(ot_ps[layer], 1)

            def project(layer, w):
                for q in range(NQ):
                    pe.wait_ge(ot_read[layer], min(NT, max(4 * q + 4, 9 + q)))
                    for t in range(QUAD):
                        mm = pe.transpose(bank(q)[:, t * P:(t + 1) * P], xT[:, (q * QUAD + t) * D:(q * QUAD + t + 1) * D],
                                          ident_sb[:])
                    mm.then_inc(at_ps[layer], 1)
                for q in range(NQ):
                    pe.wait_ge(at_sb[layer], q + 1)
                    for t in range(QUAD):
                        mm = pe.matmul(bank(4 + q)[:, t * P:(t + 1) * P], attT[:, q % 2, t * P:(t + 1) * P], w[:],
                                       start=True, stop=True)
                    mm.then_inc(wo_ps[layer], 1)

            pe.wait_ge(o_free[0], NS + 1)
            heads_to_rows(0, lambda t, g: big[:, (t // KB * G + g) * S + (t % KB) * P:
                                              (t // KB * G + g) * S + (t % KB + 1) * P])
            project(0, wo_sb)
            for q in range(NQ):
                pe.wait_ge(ln_out[0], q + 1)
                quad_transposes(xb, q, bank(q)).then_inc(ft_ps, 1)
            for q in range(NQ):
                pe.wait_ge(ft_sb, q + 1)
                for t in range(QUAD):
                    mm = pe.matmul(bank(4 + q)[:, t * P:(t + 1) * P], attT[:, q % 2, t * P:(t + 1) * P], m_sb[:],
                                   start=True, stop=True)
                mm.then_inc(fm_ps, 1)
            for q in range(NQ):
                pe.wait_ge(ln_out[1], q + 1)
                if q >= 2:
                    pe.wait_ge(v_sb[1], q - 1)
                quad_transposes(xa, q, bank(q % 2)).then_inc(xT_ps[1], 1)
                pe.wait_ge(xT_sb[1], q + 1)
                if q >= 2:
                    pe.wait_ge(ksel_sb, q - 1)
                xq = xT[:, q * QN:(q + 1) * QN]
                pair = bank(2 + 2 * (q % 2), 2)
                pe.matmul(pair[:, 0:QN], w_qkv1[:, 0:D], xq, start=True, stop=True)
                pe.matmul(pair[:, QN:2 * QN], w_qkv1[:, D:2 * D], xq, start=True, stop=True).then_inc(qk_ps[1], 1)
                pe.wait_ge(xsel_set, q + 1)
                for t in range(QUAD):
                    mm = pe.matmul(bank(q % 2)[:, t * P:(t + 1) * P], attT[:, q % 2, t * P:(t + 1) * P],
                                   w_qkv1[:, 2 * D:W3], start=True, stop=True)
                mm.then_inc(v_ps[1], 1)

            def seg_max(s):
                slot = s % RING
                for h in range(HG):
                    n = s * (HG + 2) + h
                    if n >= 2:
                        pe.wait_ge(max_done[1], n - (h > 0))
                    for g in range(KB):
                        mm = pe.matmul(bank(h % 2)[:, g * KSEG:(g + 1) * KSEG],
                                       q_rep[0:K_MAX, slot * HG * S + h * S + g * SEG:slot * HG * S + h * S + (g + 1) * SEG],
                                       k_rep1[0:K_MAX, (slot * HG + h) * S // 2 + g * KSEG:
                                              (slot * HG + h) * S // 2 + (g + 1) * KSEG], start=True, stop=True)
                    mm.then_inc(max_ps[1], 1)
                pe.wait_ge(max_all[1], s + 1)
                pe.transpose(bank(0)[0:STEPS, 0:P], mx[:], ident_sb[:]).then_inc(max_ps[1], 2)

            def seg_scores(s):
                slot = s % RING
                pe.wait_ge(mrow_in[1], 32 * (s + 1))
                for f in range(2):
                    if s:
                        pe.wait_ge(s_free[1], 2 * s - 1 + f)
                    for g in range(4 * f, 4 * f + 4):
                        for h in range(HG):
                            c = (g % 4) * 2 * SEG + (h // 2) * SEG
                            mm = pe.matmul(bank(2 + 2 * f, 2)[KSEG * (h % 2):KSEG * (h % 2 + 1), c:c + SEG],
                                           k_rep1[0:K_EXP, (slot * HG + h) * S // 2 + g * KSEG:
                                                  (slot * HG + h) * S // 2 + (g + 1) * KSEG],
                                           q_rep[0:K_EXP, slot * HG * S + h * S + g * SEG:
                                                 slot * HG * S + h * S + (g + 1) * SEG],
                                           start=True, stop=True, tile_position=(0, KSEG * (h % 2)))
                    mm.then_inc(s_ps[1], 1)

            def seg_out(s):
                b, g4 = s // G, s % G
                pe.wait_ge(s_free[1], 2 * s + 2)
                if s >= 2:
                    pe.wait_ge(o_free[1], s - 1)
                for g in range(KB):
                    for pr in range(2):
                        j = (g % 2) * 2 + pr
                        mm = pe.matmul(bank(6 + s % 2)[32 * j:32 * j + 32, (g // 2) * SEG:(g // 2 + 1) * SEG],
                                       vblk(b * KB + g, g4 * 2 + pr),
                                       probs[:, 0, (s % 2) * 2 * S + g * 2 * SEG + pr * SEG:
                                             (s % 2) * 2 * S + g * 2 * SEG + (pr + 1) * SEG],
                                       start=True, stop=True, tile_position=(0, 32 * j))
                mm.then_inc(p_free[1], 1)

            def vblk(g, pair):
                return v_blk[:, (g * 8 + pair) * 32:(g * 8 + pair + 1) * 32]

            def rep1_wait(s):
                pe.wait_ge(rep_loaded[1], 5 * 16 * (s + 1))

            pe.wait_ge(v_sb[1], NQ)
            pe.wait_ge(ksel_sb, NQ)
            rep1_wait(0)
            seg_max(0)
            for s in range(NS):
                if s + 1 < NS:
                    rep1_wait(s + 1)
                    seg_max(s + 1)
                seg_scores(s)
                if s:
                    seg_out(s - 1)
            seg_out(NS - 1)

            def seg_heads(t, g):
                s = t // KB * G + g
                return o_seg[:, s * 512 + (t % KB // 2) * P:s * 512 + (t % KB // 2 + 1) * P]

            pe.wait_ge(o_free[1], NS)
            heads_to_rows(1, seg_heads)
            project(1, wout_sb)
            pe.wait_ge(sim_sq, 1)
            for q in range(NQ):
                pe.wait_ge(ln_out[2], q + 1)
                quad_transposes(xb, q, bank(q)).then_inc(x3T_ps, 1)
            pe.matmul(bank(6)[:, 0:E], ones[:], rt[0][:, 0, :], start=True, stop=True).then_inc(sim_ss, 1)
            pe.wait_ge(sim_ready, 1)
            pe.wait_ge(x3T_sb, NQ)
            for t in range(NT):
                mm = pe.matmul(bank(7)[:, t * E:(t + 1) * E], xT[:, t * P:(t + 1) * P], sim_n[:], start=True, stop=True)
            mm.then_inc(lg_ps, 1)

            pe.wait_ge(w_ready, 1)
            pe.wait_ge(ld_we, 4 * 16)
            def to_channels(t, u):
                pe.wait_ge(tok_set, t + 1)
                for n in range(2):
                    mm = pe.transpose(bank(4 + u)[:, n * P:(n + 1) * P], tok_cur[:, u, n * P:(n + 1) * P], ident_sb[:])
                mm.then_inc(kq_ps, 1)

            with pe.Fori(0, NT // 2) as t2:
                for u in range(2):
                    t = 2 * t2 + u
                    pe.wait_ge(xc_set, t + 1)
                    for e in range(E):
                        pe.wait_ge(y_free, t * E + e + 1)
                        pe.matmul(bank(e % YR)[:, 0:W3], x_cur[:, u, :], we_qkv[:, e * W3:(e + 1) * W3],
                                  start=True, stop=True).then_inc(y_ps, 1)
                        if u == 1 and e == 5:
                            to_channels(t - 1, 0)
                    if u == 1:
                        to_channels(t, 1)

            def scores(t):
                pe.wait_ge(q_set, t + 1)
                pe.wait_ge(p_set, t + 1)
                for i in range(2):
                    mm = pe.matmul(bank(i), q_cur, kT_all[:, bass.ds(t // KB * S + i * QN, QN)], start=True, stop=True)
                mm.then_inc(sc_ps, 1)

            def probs_T(t):
                pe.wait_ge(p_set, t + 2)
                pe.wait_ge(pt_sb, 2 * t + 2)
                for kb in range(KB):
                    mm = pe.transpose(bank(2 + kb // 4)[:, (kb % 4) * P:(kb % 4 + 1) * P], p_cur[:, kb * P:(kb + 1) * P],
                                      ident_sb[:])
                mm.then_inc(pt_ps, 1)

            def outputs(t):
                pe.wait_ge(pt_sb, 2 * t + 4)
                pe.wait_ge(o_sb, t + 1)
                for kb in range(KB):
                    mm = pe.matmul(bank(4)[:, 0:P], pT_cur[:, kb * P:(kb + 1) * P],
                                   qkv[:, bass.ds((t // KB * KB + kb) * W3 + 2 * D, D)], start=(kb == 0),
                                   stop=(kb == KB - 1))
                mm.then_inc(o_ps, 1)

            def outputs_T(t):
                pe.wait_ge(o_sb, t + 2)
                pe.wait_ge(ott_sb, t + 1)
                pe.transpose(bank(5)[:, 0:P], o_cur, ident_sb[:]).then_inc(ott_ps, 1)

            def out_experts(t):
                pe.wait_ge(ott_sb, t + 2)
                for n in range(E // 4):
                    pe.wait_ge(z_free, t * (E // 4) + n + 1)
                    pe.matmul(bank(6 + n % 2), oT_cur, we_o[:, n * 4 * D:(n + 1) * 4 * D], start=True,
                              stop=True).then_inc(z_ps, 1)

            def tile(t, more):
                outputs(t)
                if more:
                    scores(t + 1)
                outputs_T(t)
                out_experts(t)
                if more:
                    probs_T(t + 1)

            scores(0)
            probs_T(0)
            with pe.Fori(0, NT - 1) as t:
                tile(t, True)
            tile(NT - 1, False)

        @block.scalar
        def _(act):
            def copy(dst, src):
                return act.activation(dst, src, ACT.Copy)

            act.wait_ge(const_set, 1)
            act.activation(tick[:, 1:2], ones[:, 0:1], ACT.Exp).then_inc(s_free[0], 2)
            for q in range(NQ):
                act.wait_ge(xT_ps[0], q + 1)
                copy(xT[:, q * QN:(q + 1) * QN], bank(q % 2)).then_inc(xT_sb[0], 1)
                act.wait_ge(qk_ps[0], q + 1)
                if q >= 1:
                    act.wait_ge(qk_split[0], q)
                copy(qk[:], bank(2 + 2 * (q % 2), 2)).then_inc(qk_sb[0], 1)
                act.wait_ge(v_ps[0], q + 1)
                act.wait_ge(const_set, 3)
                va = v_all.rearrange("p (s k c) -> p s k c", s=NS, k=KB)
                b, k0 = q // 2, (q % 2) * QUAD
                copy(va[:, b * G:(b + 1) * G, k0:k0 + QUAD, 0:DH],
                     bank(6 + q % 2)[:, 0:QUAD * 32].rearrange("p (t g d) -> p g t d", t=QUAD, g=G)).then_inc(v_sb[0], 1)

            def exps(s):
                for k in range(STEPS):
                    kb, h = k // HG, k % HG
                    act.wait_ge(s_ps[0], s * STEPS + k + 1)
                    if h == 0:
                        act.wait_ge(p_free[0], s * KB + kb + 1)
                    act.activation(probs[:, kb % 2, h * S:(h + 1) * S], bank(2 + 2 * (k % 2), 2),
                                   ACT.Exp).then_inc(s_free[0], 1)
                act.wait_ge(p_free[0], (s + 1) * KB + 2)
                copy(big[:, bass.ds(s * S, S)], bank(6, 2)).then_inc(o_free[0], 1)

            with act.Fori(0, NS) as s:
                exps(s)

            def attT_copies(ps_sem, sb_sem, done_sem):
                for q in range(NQ):
                    act.wait_ge(ps_sem, q + 1)
                    if q >= 2:
                        act.wait_ge(done_sem, q - 1)
                    copy(attT[:, q % 2, :], bank(q)).then_inc(sb_sem, 1)

            attT_copies(at_ps[0], at_sb[0], wo_ps[0])
            attT_copies(ft_ps, ft_sb, fm_ps)

            def dilated(ap, par):
                v = ap.rearrange("p (r two i c) -> p r two i c", two=2, i=16, c=2)
                return v[:, :, par, :, par]

            for q in range(NQ):
                act.wait_ge(xT_ps[1], q + 1)
                copy(xT[:, q * QN:(q + 1) * QN], bank(q % 2)).then_inc(xT_sb[1], 1)
                act.wait_ge(qk_ps[1], q + 1)
                if q >= 1:
                    act.wait_ge(qk_split[1], q)
                pair = bank(2 + 2 * (q % 2), 2)
                act.activation(qk[:, 0:QN], pair[:, 0:QN], ACT.Copy, scale=scale)
                ks = qk[:, QN:QN + QN // 2].rearrange("p (r two i) -> p r two i", two=2, i=16)
                for par in range(2):
                    mm = copy(ks[:, :, par, :], dilated(pair[:, QN:2 * QN], par))
                mm.then_inc(ksel_sb, 1)
                act.wait_ge(v_ps[1], q + 1)
                act.wait_ge(const_set, 8)
                vb = v_blk.rearrange("p (g r c) -> p g r c", g=NT, r=8)[:, q * QUAD:(q + 1) * QUAD]
                vp = bank(q % 2).rearrange("p (g r two d) -> p g r two d", g=QUAD, r=8, two=2)
                copy(vb[0:KSEG, :, :, 0:DH], vp[0:KSEG, :, :, 0, :])
                copy(vb[KSEG:P, :, :, 16:16 + DH], vp[KSEG:P, :, :, 1, :]).then_inc(v_sb[1], 1)

            for s in range(NS):
                for f in range(2):
                    act.wait_ge(s_ps[1], 2 * s + f + 1)
                    if s >= 2 and f == 0:
                        act.wait_ge(p_free[1], s - 1)
                    act.activation(probs[:, 0, (s % 2) * 2 * S + f * S:(s % 2) * 2 * S + (f + 1) * S],
                                   bank(2 + 2 * f, 2), ACT.Exp).then_inc(s_free[1], 1)
            attT_copies(at_ps[1], at_sb[1], wo_ps[1])
            for q in range(NQ):
                act.wait_ge(x3T_ps, q + 1)
                copy(xT[:, q * QN:(q + 1) * QN], bank(q)).then_inc(x3T_sb, 1)
            act.wait_ge(ld_bias, 32)
            act.activation(gate_sb[:], gate_sb[:], ACT.Exp, scale=-1.0).then_inc(gate_exp, 1)
            act.wait_ge(ex_in, 1)
            act.activation(rt[1][:], rt[1][:], ACT.Exp).then_inc(ex_out, 1)
            act.wait_ge(x3T_sb, NQ)
            copy(x_cur[:, 0, :], xT[:, 0:P]).then_inc(xc_set, 1)
            with act.Fori(0, NT // 2) as t2:
                for u in range(2):
                    t = 2 * t2 + u
                    copy(x_cur[:, 1 - u, :], xT[:, bass.ds((t + 1) % NT * P, P)]).then_inc(xc_set, 1)
                    act.wait_ge(kq_ps, t + 1)
                    copy(qT_all[:, bass.ds(t * P, P)], bank(4 + u)[:, 0:P])
                    copy(kT_all[:, bass.ds(t * P, P)], bank(4 + u)[:, P:2 * P]).then_inc(kq_sb, 1)

            act.wait_ge(kq_sb, NT)
            act.sem_inc(sc_ps, 1)
            act.sem_inc(o_sb, 1)
            act.sem_inc(ott_sb, 1)
            act.sem_inc(p_set, 1)
            act.sem_inc(pt_sb, 2)
            act.sem_inc(pt_ps, 1)

            def p_exp(t):
                act.wait_ge(nmax_set, t + 1)
                act.wait_ge(pt_ps, t + 1)
                act.activation(p_cur, bank(0, 2), ACT.Exp, bias=m_cur[:, 1:2], scale=scale_moe,
                               accum_out=m_cur[:, 2:3]).then_inc(p_set, 1)

            def pT_copy(t):
                act.wait_ge(pt_ps, t + 2)
                act.wait_ge(o_ps, t + 1)
                copy(pT_cur[:, 0:QN], bank(2)).then_inc(pt_sb, 1)

            def tile(t, more):
                act.wait_ge(o_ps, t + 2)
                act.wait_ge(ott_ps, t + 1)
                copy(o_cur, bank(4)[:, 0:P]).then_inc(o_sb, 1)
                act.wait_ge(ott_ps, t + 2)
                act.wait_ge(z_ps, (t + 1) * (E // 4))
                copy(oT_cur, bank(5)[:, 0:P]).then_inc(ott_sb, 1)
                if more:
                    p_exp(t + 1)
                    pT_copy(t + 1)

            act.sem_inc(o_ps, 1)
            act.sem_inc(ott_ps, 1)
            act.sem_inc(z_ps, E // 4)
            p_exp(0)
            pT_copy(0)
            with act.Fori(0, NT - 1) as t:
                tile(t, True)
            tile(NT - 1, False)

        @block.vector
        def _(dve):
            steps = [0]

            def link(ins):
                steps[0] += 1
                ins.then_inc(dve_step, 1)
                dve.wait_ge(dve_step, steps[0])

            words = mybir.dt.uint32
            two_ones = 0x3F803F80
            dve.memset(k_rep0[64:MAX_ROW, :].bitcast(words), 0).then_inc(rows_set, 1)
            dve.memset(k_rep0[MAX_ROW:P, :].bitcast(words), two_ones).then_inc(rows_set, 1)
            dve.memset(q_rep[64:P, :].bitcast(words), 0).then_inc(rows_set, 1)
            dve.wait_ge(ld_c, 4 * 16)
            dve.tensor_scalar(w_qkv0[:, 0, :], w_qkv0[:, 0, :], scale, None, ALU.mult).then_inc(wq_scaled, 1)

            def split(layer, q, ready, n):
                dve.wait_ge(ready, q + 1)
                if q >= 1:
                    dve.wait_ge(q_out[layer], q * PARTS * 16)
                    dve.wait_ge(k_out[layer], q * ROWS // DH * 16)
                link(dve.tensor_copy(qk_p[:, 0, 0:n], qk[:, 0:n]))
                link(dve.tensor_tensor(qk_r[:, 0:n], qk[:, 0:n], qk_p[:, 0, 0:n], ALU.subtract))
                link(dve.tensor_copy(qk_p[:, 1, 0:n], qk_r[:, 0:n]))
                dve.tensor_tensor(qk_p[:, 2, 0:n], qk_r[:, 0:n], qk_p[:, 1, 0:n], ALU.subtract).then_inc(
                    qk_split[layer], 1)

            for q in range(NQ):
                split(0, q, qk_sb[0], 2 * QN)
            dve.memset(k_rep1[64:MAX_ROW, :].bitcast(words), 0).then_inc(rows_set, 1)
            dve.memset(k_rep1[MAX_ROW:P, :].bitcast(words), two_ones).then_inc(rows_set, 1)
            dve.wait_ge(dft_a, 1)
            dve.tensor_scalar(a_re[:], bank(0)[:, 0:P], 1.0 / D, None, ALU.mult).then_inc(dft_a_sb, 1)
            dve.tensor_scalar(a_im[:], bank(1)[:, 0:P], 1.0 / D, None, ALU.mult).then_inc(dft_a_sb, 1)
            dve.wait_ge(dft_m, 1)
            dve.tensor_copy(m_sb[:], bank(0)[:, 0:P]).then_inc(dft_m_sb, 1)
            dve.sem_inc(p_free[0], 2)
            dve.memset(rstd[:, 0:1], 0.0).then_inc(o_free[0], 1)

            def max_pair(s, k):
                for i in range(2):
                    n = s * (2 * STEPS + 2) + 2 * k + i
                    dve.wait_ge(max_ps[0], n + 1)
                    dve.reduce_max(mx2[:, 2 * k + i:2 * k + i + 1], bank(i), AX_X).then_inc(max_done[0], 1)

            def max_rows(s):
                n = s * (2 * STEPS + 2) + 2 * STEPS
                dve.wait_ge(max_done[0], n)
                if not isinstance(s, int):
                    dve.wait_ge(mrow_in[0], 32 * s)
                dve.reduce_max(mx[:], mx2[:].rearrange("p (k i) -> p k i", i=2), AX_X).then_inc(max_all[0], 1)
                dve.wait_ge(max_ps[0], n + 2)
                dve.tensor_scalar(mrow[:, 0, :], bank(0)[0:STEPS, 0:P], -1.0, None, ALU.mult).then_inc(max_done[0], 1)
                dve.wait_ge(max_done[0], n + 1)
                dve.scalar_tensor_tensor(out=mrow[:, 1, :], in0=bank(0)[0:STEPS, 0:P], scalar=-1.0, in1=mrow[:, 0, :],
                                         op0=ALU.mult, op1=ALU.subtract).then_inc(max_done[0], 1)
                dve.wait_ge(max_done[0], n + 2)
                dve.sem_inc(mrow_set[0], 1)

            for k in range(STEPS):
                max_pair(0, k)
            max_rows(0)
            for k in range(LEAD):
                max_pair(1, k)
            with dve.Fori(0, NS - 2) as s:
                for k in range(LEAD, STEPS):
                    max_pair(s + 1, k)
                max_rows(s + 1)
                for k in range(LEAD):
                    max_pair(s + 2, k)
            for k in range(LEAD, STEPS):
                max_pair(NS - 1, k)
            dve.wait_ge(mrow_in[0], 32 * (NS - 1))
            max_rows(NS - 1)

            def norm(n, q, src, dst, done):
                for t in range(QUAD):
                    ins = dve.bn_stats(st[:, t, :], src[:, t, :])
                link(ins)
                for t in range(QUAD):
                    ins = dve.bn_aggr(mv[:, t, :], st[:, t, :])
                link(ins)
                dve.tensor_scalar(ve[:], mv[:, :, 1], EPS, None, ALU.add).then_inc(ln_var[n], 1)
                dve.wait_ge(ln_std[n], q + 1)
                for t in range(QUAD):
                    ins = dve.tensor_scalar(dst[:, q * QUAD + t, :], src[:, t, :], mv[:, t, 0:1], rstd[:, t:t + 1],
                                            ALU.subtract, ALU.mult)
                link(ins)
                dve.sem_inc(done, 1)

            def heads(layer, view):
                for t in range(NT):
                    dve.wait_ge(ot_ps[layer], t + 1)
                    o, total, r = view(t)
                    link(dve.reciprocal(r, total))
                    a = xT[:, t * D:(t + 1) * D]
                    dve.tensor_tensor(a.rearrange("p (h d) -> p h d", d=DH), o,
                                      r.unsqueeze(2).broadcast_to([P, H, DH]), ALU.mult).then_inc(ot_read[layer], 1)

            def view0(t):
                b = bank(t % 8).rearrange("p (h c) -> p h c", c=32)
                return b[:, :, 0:DH], b[:, :, DH], rec[:, t % 2, :]

            heads(0, view0)

            def add_norm(n, ready, src, dst, bias=None):
                for q in range(NQ):
                    dve.wait_ge(ready, q + 1)
                    link(dve.tensor_tensor(res[:], bank(4 + q).rearrange("p (t d) -> p t d", t=QUAD),
                                           src[:, q * QUAD:(q + 1) * QUAD, :], ALU.add))
                    if bias is not None:
                        link(dve.tensor_tensor(res[:], res[:], bias[:].unsqueeze(1).broadcast_to([P, QUAD, D]), ALU.add))
                    norm(n, q, res, dst, ln_out[n])

            add_norm(0, wo_ps[0], xa, xb)
            dve.wait_ge(ld_bias, 32)
            add_norm(1, fm_ps, xb, xa, bias_sb)
            for q in range(NQ):
                dve.wait_ge(xT_sb[1], q + 1)
                if q >= 2:
                    dve.wait_ge(v_ps[1], q - 1)
                xs = attT[:, q % 2, :].rearrange("p (g dup r two i) -> p g dup r two i", g=QUAD, dup=2, r=2, two=2)
                xq = xT[:, q * QN:(q + 1) * QN].rearrange("p (g r two i c) -> p g r two i c", g=QUAD, r=2, two=2, c=2)
                for dup in range(2):
                    for par in range(2):
                        for g in range(QUAD):
                            ins = dve.tensor_copy(xs[:, g, dup, :, par, :], xq[:, g, :, par, :, par])
                ins.then_inc(xsel_set, 1)
                split(1, q, ksel_sb, QN + QN // 2)

            def seg_max(s):
                for h in range(HG):
                    n = s * (HG + 2) + h
                    dve.wait_ge(max_ps[1], n + 1)
                    dve.reduce_max(mx[:, h * KB:(h + 1) * KB], bank(h % 2).rearrange("p (g k) -> p g k", g=KB),
                                   AX_X).then_inc(max_done[1], 1)
                dve.wait_ge(max_done[1], s * (HG + 2) + HG)
                dve.sem_inc(max_all[1], 1)
                n = s * (HG + 2) + HG
                dve.wait_ge(max_ps[1], n + 2)
                if s:
                    dve.wait_ge(mrow_in[1], 32 * s)
                dve.tensor_scalar(mrow[:, 0, :], bank(0)[0:STEPS, 0:P], -1.0, None, ALU.mult).then_inc(max_done[1], 1)
                dve.wait_ge(max_done[1], n + 1)
                dve.scalar_tensor_tensor(out=mrow[:, 1, :], in0=bank(0)[0:STEPS, 0:P], scalar=-1.0, in1=mrow[:, 0, :],
                                         op0=ALU.mult, op1=ALU.subtract).then_inc(max_done[1], 1)
                dve.wait_ge(max_done[1], n + 2)
                dve.sem_inc(mrow_set[1], 1)

            def seg_o(s):
                dve.wait_ge(p_free[1], s + 1)
                dve.tensor_copy(o_seg[:, s * 512:(s + 1) * 512], bank(6 + s % 2)).then_inc(o_free[1], 1)

            seg_max(0)
            for s in range(NS):
                if s + 1 < NS:
                    seg_max(s + 1)
                if s:
                    seg_o(s - 1)
            seg_o(NS - 1)

            def view1(t):
                sp = t % 2
                b = bank(t % 8).rearrange("p (g s h c) -> p g s h c", g=G, s=2, h=4)[:, :, sp]
                return b[:, :, :, 0:DH], b[:, :, :, DH], rec[:, t % 2, :].rearrange("p (g h) -> p g h", g=G)

            for t in range(NT):
                dve.wait_ge(ot_ps[1], t + 1)
                o, total, r = view1(t)
                link(dve.reciprocal(r, total))
                a = xT[:, t * D:(t + 1) * D]
                dve.tensor_tensor(a.rearrange("p (g h d) -> p g h d", g=G, h=4), o,
                                  r.unsqueeze(3).broadcast_to([P, G, 4, DH]), ALU.mult).then_inc(ot_read[1], 1)
            link(dve.tensor_tensor(rt[0][:, 0, :], sim_sb[:], sim_sb[:], ALU.mult))
            dve.sem_inc(sim_sq, 1)
            add_norm(2, wo_ps[1], xa, xb)

            dve.wait_ge(sim_ss, 1)
            link(dve.tensor_copy(sim_n[:], bank(6)[:, 0:E]))
            dve.sem_inc(sim_root, 1)
            dve.wait_ge(sim_root_done, 1)
            link(dve.tensor_scalar(sim_n[:], sim_n[:], 1e-12, None, ALU.max))
            link(dve.reciprocal(sim_n[:], sim_n[:]))
            link(dve.tensor_tensor(sim_n[:], sim_sb[:], sim_n[:], ALU.mult))
            dve.sem_inc(sim_ready, 1)
            for q in range(NQ):
                xq = xb[:, q * QUAD:(q + 1) * QUAD, :]
                link(dve.tensor_tensor(res[:], xq, xq, ALU.mult))
                link(dve.reduce_sum(r1[0][:, q * QUAD:(q + 1) * QUAD], res[:], AX_X))
            dve.sem_inc(nrm_ss, 1)
            dve.wait_ge(nrm_root, 1)
            link(dve.tensor_scalar(r1[0][:], r1[0][:], 1e-12, None, ALU.max))
            link(dve.reciprocal(r1[0][:], r1[0][:]))
            dve.wait_ge(gate_exp, 1)
            link(dve.tensor_scalar(gate_sb[:], gate_sb[:], 1.0, None, ALU.add))
            link(dve.reciprocal(gate_sb[:], gate_sb[:]))

            def over_e(v):
                return v.unsqueeze(2).broadcast_to([P, NT, E])

            def over_t(v):
                return v.unsqueeze(1).broadcast_to([P, NT, E])

            lg, t1, t2_, t3, t4, t5 = (r[:] for r in rt)
            top, r_a, r_b = r1[1][:], r1[2][:], r1[3][:]
            dve.wait_ge(lg_ps, 1)
            link(dve.tensor_tensor(lg, bank(7)[:, 0:NT * E].rearrange("p (t e) -> p t e", e=E), over_e(r1[0][:]), ALU.mult))
            link(dve.tensor_tensor(lg, lg, over_t(gate_sb[:]), ALU.subtract))
            link(dve.reduce_max(top, lg, AX_X))

            def first_of(values, best, one_hot, work):
                link(dve.tensor_tensor(work, values, over_e(best), ALU.is_equal))
                link(dve.tensor_tensor(work, work, over_t(rank_sb[:]), ALU.mult))
                link(dve.reduce_max(r_a, work, AX_X))
                link(dve.tensor_tensor(one_hot, work, over_e(r_a), ALU.is_equal))

            first_of(lg, top, t2_, t1)
            link(dve.scalar_tensor_tensor(out=t3, in0=t2_, scalar=-1e30, in1=lg, op0=ALU.mult, op1=ALU.add))
            link(dve.reduce_max(r_b, t3, AX_X))
            first_of(t3, r_b, t4, t1)
            link(dve.tensor_tensor(t2_, t2_, t4, ALU.add))
            link(dve.tensor_scalar(r_a, top, 0.0, None, ALU.is_le))
            link(dve.tensor_tensor(t2_, t2_, over_e(r_a), ALU.mult))
            link(dve.tensor_scalar(t3, lg, 0.0, None, ALU.is_gt))
            link(dve.tensor_tensor(t2_, t2_, t3, ALU.add))
            link(dve.tensor_scalar(t3, lg, 0.0, None, ALU.max))
            link(dve.tensor_scalar(r_b, top, 0.0, None, ALU.max))
            link(dve.tensor_tensor(t1, t3, over_e(r_b), ALU.subtract))
            dve.sem_inc(ex_in, 1)
            dve.wait_ge(ex_out, 1)
            link(dve.tensor_tensor(t1, t1, t2_, ALU.mult))
            link(dve.reduce_sum(r_a, t1, AX_X))
            link(dve.reciprocal(r_a, r_a))
            link(dve.tensor_tensor(w_rt[:], t1, over_e(r_a), ALU.mult))
            dve.sem_inc(w_ready, 1)
            dve.sem_inc(y_free, YR)
            dve.sem_inc(w_set, 1)

            with dve.Fori(0, NT // 2) as t2:
                for u in range(2):
                    t = 2 * t2 + u
                    dve.tensor_copy(w_cur, w_rt[:].rearrange("p t e -> p (t e)")[:, bass.ds(t * E, E)]).then_inc(w_set, 1)
                    dve.wait_ge(w_set, t + 2)
                    for e in range(E):
                        a, y = acc[:, u, e % 2, :], bank(e % YR)[:, 0:W3]
                        dve.wait_ge(y_ps, t * E + e + 1)
                        if e < 2:
                            ins = dve.tensor_scalar(a, y, w_cur[:, e:e + 1], None, ALU.mult)
                        else:
                            dve.wait_ge(y_free, t * E + e - 1 + YR)
                            ins = dve.scalar_tensor_tensor(out=a, in0=y, scalar=w_cur[:, e:e + 1], in1=a,
                                                           op0=ALU.mult, op1=ALU.add)
                        ins.then_inc(y_free, 1)
                    dve.wait_ge(y_free, (t + 1) * E + YR)
                    dve.tensor_tensor(tok_cur[:, u, :], acc[:, u, 0, :], acc[:, u, 1, :], ALU.add).then_inc(tok_set, 1)
                    dve.tensor_tensor(qkv[:, bass.ds(t * W3, W3)], acc[:, u, 0, :], acc[:, u, 1, :], ALU.add)\
                       .then_inc(tok_free, 1)

            dve.wait_ge(tok_free, NT)
            dve.sem_inc(z_free, 2)
            dve.sem_inc(stored, 16)

            def row_max(t):
                dve.wait_ge(sc_ps, t + 2)
                dve.wait_ge(p_set, t + 1)
                dve.reduce_max(m_cur[:, 0:1], bank(0, 2), AX_X).then_inc(w_set, 1)

            def tile(t, base, more):
                dve.wait_ge(p_set, t + 2)
                dve.wait_ge(w_set, base)
                dve.reciprocal(m_cur[:, 3:4], m_cur[:, 2:3]).then_inc(w_set, 1)
                dve.wait_ge(w_set, base + 1)
                dve.tensor_scalar(w_cur, w_rt[:].rearrange("p t e -> p (t e)")[:, bass.ds(t * E, E)], m_cur[:, 3:4],
                                  None, ALU.mult).then_inc(w_set, 1)
                dve.tensor_copy(x_tok, xb[:].rearrange("p t d -> p (t d)")[:, bass.ds(t * D, D)]).then_inc(w_set, 1)
                dve.wait_ge(pt_ps, t + 2)
                dve.wait_ge(o_ps, t + 1)
                dve.tensor_copy(pT_cur[:, QN:2 * QN], bank(3)).then_inc(pt_sb, 1)
                dve.wait_ge(w_set, base + 3)
                n = base + 3
                if more:
                    dve.wait_ge(sc_ps, t + 3)
                    dve.reduce_max(m_cur[:, 0:1], bank(0, 2), AX_X).then_inc(w_set, 1)
                    dve.wait_ge(w_set, n + 1)
                    dve.tensor_scalar(m_cur[:, 1:2], m_cur[:, 0:1], -scale_moe, None, ALU.mult).then_inc(nmax_set, 1)
                    n += 1
                for e in range(E):
                    if e % 4 == 0:
                        dve.wait_ge(z_ps, (t + 1) * (E // 4) + e // 4 + 1)
                    z = bank(6 + e // 4 % 2)[:, (e % 4) * D:(e % 4 + 1) * D]
                    a = y_acc[:, e % 2, :]
                    if e == 0:
                        ins = dve.scalar_tensor_tensor(out=a, in0=z, scalar=w_cur[:, 0:1], in1=x_tok, op0=ALU.mult,
                                                       op1=ALU.add)
                    elif e == 1:
                        ins = dve.tensor_scalar(a, z, w_cur[:, 1:2], None, ALU.mult)
                    else:
                        dve.wait_ge(w_set, n + e - 1)
                        ins = dve.scalar_tensor_tensor(out=a, in0=z, scalar=w_cur[:, e:e + 1], in1=a, op0=ALU.mult,
                                                       op1=ALU.add)
                    ins.then_inc(w_set, 1)
                    if e % 4 == 3:
                        dve.wait_ge(w_set, n + e + 1)
                        dve.sem_inc(z_free, 1)
                n += E
                dve.tensor_tensor(res[:, 0, :], y_acc[:, 0, :], y_acc[:, 1, :], ALU.add).then_inc(w_set, 1)
                dve.wait_ge(w_set, n + 1)
                dve.bn_stats(st[:, 0, :], res[:, 0, :]).then_inc(w_set, 1)
                dve.wait_ge(w_set, n + 2)
                dve.memset(tick[:, 1:2], 0.0)
                dve.bn_aggr(mv[:, 0, :], st[:, 0, :]).then_inc(w_set, 1)
                dve.wait_ge(w_set, n + 3)
                dve.tensor_scalar(ve[:, 0:1], mv[:, 0, 1:2], EPS, None, ALU.add).then_inc(fin_var, 1)
                dve.wait_ge(fin_std, t + 1)
                dve.wait_ge(stored, 16 * (t + 1))
                dve.tensor_scalar(y_out, res[:, 0, :], mv[:, 0, 0:1], rstd[:, 0:1], ALU.subtract,
                                  ALU.mult).then_inc(fin_set, 1)

            base = 1 + NT
            dve.wait_ge(sc_ps, 2)
            dve.reduce_max(m_cur[:, 0:1], bank(0, 2), AX_X).then_inc(w_set, 1)
            base += 1
            dve.wait_ge(w_set, base)
            dve.tensor_scalar(m_cur[:, 1:2], m_cur[:, 0:1], -scale_moe, None, ALU.mult).then_inc(nmax_set, 1)
            per = 3 + 1 + E + 3
            with dve.Fori(0, NT - 1) as t:
                tile(t, base + t * per, True)
            tile(NT - 1, base + (NT - 1) * per, False)


def constants():
    def bf16(a):
        a = np.asarray(a, np.float32).view(np.uint32).astype(np.uint64)
        return ((a + 0x7FFF + ((a >> 16) & 1)) >> 16).astype(np.uint16)

    def widen(a):
        return (a.astype(np.uint32) << 16).view(np.float32)

    n = np.arange(D)
    angle = 2.0 * np.pi * ((n[:, None] * n[None, :]) % D) / D
    start = 2.0 ** -0.5
    slope = np.array([start * start ** i for i in range(H)], np.float32)
    s1 = bf16(slope)
    s2 = bf16(slope - widen(s1))
    s3 = bf16(slope - widen(s1) - widen(s2))
    rows = np.stack([s1, s1, s2, s2, s3, s3])
    slopes = np.ascontiguousarray(np.broadcast_to(rows.reshape(N_BIAS, G, HG, 1).transpose(1, 0, 2, 3),
                                                  (G, N_BIAS, HG, S)).reshape(G, N_BIAS, HG * S))
    pos = np.arange(S) - (S - 1)
    hi = pos // 8 * 8
    kpos = np.stack([bf16(hi), bf16(pos - hi)] * PARTS)
    return {"ident": np.eye(P, dtype=np.float32), "c_cos": np.cos(angle).astype(np.float32),
            "c_sin": np.sin(angle).astype(np.float32), "c_nsin": (-np.sin(angle)).astype(np.float32),
            "slopes": slopes, "kpos": np.ascontiguousarray(kpos),
            "rank": np.ascontiguousarray(np.broadcast_to(np.arange(E, 0, -1, dtype=np.float32), (P, E)))}


_INS = ["L0_attn_x", "L0_attn_Wq", "L0_attn_Wk", "L0_attn_Wv", "L0_attn_Wo", "L0_ffn_w_freq_real",
        "L0_ffn_w_freq_imag", "L0_ffn_bias", "L1_attn_W_qkv", "L1_attn_W_out", "L1_ffn_sim_matrix", "L1_ffn_gates",
        "L1_ffn_q_proj", "L1_ffn_k_proj", "L1_ffn_v_proj", "L1_ffn_o_proj"]


def kernel(**inputs):
    import concourse.bacc as bacc
    from concourse.bass_utils import run_bass_kernel_spmd

    nc = bacc.Bacc("TRN2", target_bir_lowering=False, num_devices=1)
    arrays, args = {}, []
    for name in _INS:
        a = np.ascontiguousarray(inputs[name])
        arrays["in_" + name] = a
        args.append(nc.dram_tensor("in_" + name, a.shape, mybir.dt.from_np(a.dtype), kind="ExternalInput").ap())
    for name, a in constants().items():
        arrays["const_" + name] = a
        ap = nc.dram_tensor("const_" + name, a.shape, mybir.dt.from_np(a.dtype), kind="ExternalInput").ap()
        args.append(ap.bitcast(BF16) if a.dtype == np.uint16 else ap)
    args.append(nc.dram_tensor("out_x", (NB, S, D), F32, kind="ExternalOutput").ap())
    build(nc, *args)
    r = run_bass_kernel_spmd(nc, [arrays], core_ids=[0])
    return r.results[0]["out_x"]
```

```python
from contextlib import ExitStack

import numpy as np

import concourse.bass as bass
from concourse import mybir

F32 = mybir.dt.float32
BF16 = mybir.dt.bfloat16
F32R = mybir.dt.float32r
ALU = mybir.AluOpType
ACT = mybir.ActivationFunctionType
AX_X = mybir.AxisListType.X

P = 128
D = 128
NB, S = 2, 1024
NT = NB * S // P
QUAD = 4
NQ = NT // QUAD
QN = QUAD * P
H, DH = 16, 8
G, HG = 4, 4
NS = NB * G
KB = S // P
SEG, KSEG = 128, 64
PARTS = 3
ROWS = PARTS * PARTS * DH
BIAS_ROW = ROWS
N_BIAS = 6
MAX_ROW = 96
K_MAX = 96
K_EXP = 98
RING = 4
LEAD = 4
STEPS = KB * HG
E = 16
EPS = 1e-5
W3 = 3 * D
WC, NWC = 1024, 8
YR = 4


def build(nc, x, wq, wk, wv, wo, w_re, w_im, bias, w_qkv, w_out, sim, gates, p_q, p_k, p_v, p_o,
          ident, c_cos, c_sin, c_nsin, slopes, kpos, rank, out):
    scale = float(DH) ** -0.5
    scale_moe = float(D) ** -0.5
    dq = [nc.dram_tensor(f"q_parts_{n}", [PARTS * DH, NB * H, S], BF16).ap() for n in range(2)]
    dk = [nc.dram_tensor("k_parts_0", [PARTS * DH, NS, S], BF16).ap(),
          nc.dram_tensor("k_parts_1", [PARTS * DH, NB * H, S // 2], BF16).ap()]

    with ExitStack() as ctx:
        def sb(name, shape, dt=F32, over=ctx):
            return over.enter_context(nc.sbuf_tensor(name, shape, dt))

        def sem(name):
            return ctx.enter_context(nc.semaphore(name))

        ident_sb = sb("ident_sb", [P, P])
        ones = sb("ones", [P, P])
        cos_sb, sin_sb, nsin_sb = sb("cos_sb", [P, P]), sb("sin_sb", [P, P]), sb("nsin_sb", [P, P])
        w_qkv0 = sb("w_qkv0", [P, 3, P])
        wo_sb = sb("wo_sb", [P, P])
        wre_sb, wim_sb = sb("wre_sb", [P, P]), sb("wim_sb", [P, P])
        a_re, a_im, m_sb = sb("a_re", [P, P]), sb("a_im", [P, P]), sb("m_sb", [P, P])
        bias_sb = sb("bias_sb", [P, P])
        w_qkv1 = sb("w_qkv1", [P, W3])
        wout_sb = sb("wout_sb", [P, P])
        sim_sb, sim_n = sb("sim_sb", [P, E]), sb("sim_n", [P, E])
        gate_sb = sb("gate_sb", [P, E])
        rank_sb = sb("rank_sb", [P, E])
        half = sb("half", [P, NT])
        phalf = sb("phalf", [P, NT])
        xa = sb("xa", [P, NT, D])
        xb = sb("xb", [P, NT, D])
        xT = sb("xT", [P, NT * P])
        v_cur = sb("v_cur", [P, KB * 32])
        probs = sb("probs", [P, 2, HG * S])
        o_seg = probs[:, 1, :]
        big = sb("big", [P, NS * S])
        mx2 = sb("mx2", [P, 2 * STEPS])
        mx = sb("mx", [P, STEPS])
        mrow = sb("mrow", [STEPS, 2, P], BF16)
        attT = sb("attT", [P, 2, QN])
        rec = sb("rec", [P, 2, H])
        st = sb("st", [P, QUAD, 6])
        mv = sb("mv", [P, QUAD, 2])
        ve = sb("ve", [P, QUAD])
        rstd = sb("rstd", [P, QUAD])
        res = sb("res", [P, QUAD, D])
        tick = sb("tick", [P, 8])

        psum = [ctx.enter_context(nc.psum_tensor(n, [P, w], F32))
                for n, w in (("ps_max", 2 * QN), ("ps_s", 4 * QN), ("ps_o", 2 * QN))]
        ps_max, ps_s, ps_o = psum

        def bank(n, count=1):
            t, at = ((ps_max, n), (ps_s, n - 2), (ps_o, n - 6))[0 if n < 2 else 1 if n < 6 else 2]
            return t[:, at * QN:(at + count) * QN]

        rt = [sb(f"rt{n}", [P, NT, E]) for n in range(6)]
        r1 = [sb(f"r1_{n}", [P, NT]) for n in range(4)]
        w_rt = sb("w_rt", [P, NT, E])

        attentions = ExitStack()
        q_rep = sb("q_rep", [P, RING * HG * S], BF16, attentions)
        k_rep0 = sb("k_rep0", [P, RING * S], BF16, attentions)
        k_rep1 = sb("k_rep1", [P, RING * HG * S // 2], BF16, attentions)
        v_blk = sb("v_blk", [P, NT * 8 * 32], F32, attentions)
        v_all = v_blk[:, 0:NS * KB * 32]
        qk = sb("qk", [P, QN + QN // 2], F32, attentions)
        qk_r = sb("qk_r", [P, 2 * QN], F32, attentions)
        qk_p = sb("qk_p", [P, 2, PARTS, 2 * QN], BF16, attentions)
        attentions.close()
        w_hi = sb("w_hi", [P, E * (W3 + D)], F32R)
        w_lo = sb("w_lo", [P, E * (W3 + D)], F32R)
        op_hi = sb("op_hi", [P, 2, 2, P], F32R)
        op_lo = sb("op_lo", [P, 2, 2, P], F32R)
        v_tok = sb("v_tok", [P, NT * D])
        tok_cur = sb("tok_cur", [P, 2, 2, W3])
        q_cur = sb("q_cur", [P, 2, P])
        w_cur = sb("w_cur", [P, QUAD, E])
        m_cur = sb("m_cur", [P, 2, 3])
        y_out = sb("y_out", [P, 2, QUAD, D])
        y_acc = sb("y_acc", [P, QUAD, D])
        r_sum = sb("r_sum", [P, NT])
        f_p = probs[:].rearrange("p a b -> p (a b)")
        qT_all = f_p[:, 0:2048]
        kT_all = f_p[:, 2048:4096]
        p_cur = f_p[:, 4096:6144].rearrange("p (u n) -> p u n", u=2)
        pT_cur = f_p[:, 6144:8192].rearrange("p (u n) -> p u n", u=2)
        oT_all = xT

        ld_dft = sem("ld_dft")
        ld_x, ld_c, ld_w1, ld_bias, ld_we = (sem(n) for n in ("ld_x", "ld_c", "ld_w1", "ld_bias", "ld_we"))
        const_set = sem("const_set")
        rows_set = sem("rows_set")
        wq_scaled = sem("wq_scaled")
        dft_a, dft_a_sb, dft_m, dft_m_sb = sem("dft_a"), sem("dft_a_sb"), sem("dft_m"), sem("dft_m_sb")
        dve_step = sem("dve_step")
        xT_ps = [sem(f"xT_ps{n}") for n in range(2)]
        xT_sb = [sem(f"xT_sb{n}") for n in range(2)]
        qk_ps = [sem(f"qk_ps{n}") for n in range(2)]
        qk_hi, qk_rest, qk_mid = sem("qk_hi"), sem("qk_rest"), sem("qk_mid")
        qk_split = [sem(f"qk_split{n}") for n in range(2)]
        q_out = [[sem(f"q_out{n}_{odd}") for odd in range(2)] for n in range(2)]
        k_out = [[sem(f"k_out{n}_{odd}") for odd in range(2)] for n in range(2)]
        v_ps = [sem(f"v_ps{n}") for n in range(2)]
        v_sb = [sem(f"v_sb{n}") for n in range(2)]
        rep_loaded = [sem(f"rep_loaded{n}") for n in range(2)]
        max_ps = [sem(f"max_ps{n}") for n in range(2)]
        max_done = [sem(f"max_done{n}") for n in range(2)]
        max_all = [sem(f"max_all{n}") for n in range(2)]
        mrow_set = [sem(f"mrow_set{n}") for n in range(2)]
        mrow_in = [sem(f"mrow_in{n}") for n in range(2)]
        s_ps = [sem(f"s_ps{n}") for n in range(2)]
        s_free = [sem(f"s_free{n}") for n in range(2)]
        p_free = [sem(f"p_free{n}") for n in range(2)]
        v_cur_set = sem("v_cur_set")
        o_free = [sem(f"o_free{n}") for n in range(2)]
        ot_ps = [sem(f"ot_ps{n}") for n in range(2)]
        ot_read = [sem(f"ot_read{n}") for n in range(2)]
        at_ps = [sem(f"at_ps{n}") for n in range(2)]
        at_sb = [sem(f"at_sb{n}") for n in range(2)]
        wo_ps = [sem(f"wo_ps{n}") for n in range(2)]
        ln_res = [sem(f"ln_res{n}") for n in range(4)]
        ln_var = [sem(f"ln_var{n}") for n in range(4)]
        ln_std = [sem(f"ln_std{n}") for n in range(4)]
        ln_out = [sem(f"ln_out{n}") for n in range(4)]
        ft_ps, ft_sb, fm_ps = sem("ft_ps"), sem("ft_sb"), sem("fm_ps")
        xsel_set, ksel_sb = sem("xsel_set"), sem("ksel_sb")
        x3T_ps, x3T_sb = sem("x3T_ps"), sem("x3T_sb")
        sim_sq, sim_ss, sim_root, sim_root_done, sim_ready = (
            sem(n) for n in ("sim_sq", "sim_ss", "sim_root", "sim_root_done", "sim_ready"))
        lg_ps, gate_exp, nrm_ss, nrm_root = sem("lg_ps"), sem("gate_exp"), sem("nrm_ss"), sem("nrm_root")
        ex_in, ex_out, w_ready = sem("ex_in"), sem("ex_out"), sem("w_ready")
        w_hi_set, w_lo_set, op_hi_set = sem("w_hi_set"), sem("w_lo_set"), sem("op_hi_set")
        xc_set, y_ps, y_free, tok_set, kq_ps, kq_sb = (
            sem(n) for n in ("xc_set", "y_ps", "y_free", "tok_set", "kq_ps", "kq_sb"))
        v_set, acc_step, fin_step = sem("v_set"), sem("acc_step"), sem("fin_step")
        q_set, sc_ps, nmax_set, p_set, pt_ps, pt_sb, o_ps, o_sb = (
            sem(n) for n in ("q_set", "sc_ps", "nmax_set", "p_set", "pt_ps", "pt_sb", "o_ps", "o_sb"))
        z_ps, w_set, fin_var, fin_std, fin_set = (
            sem(n) for n in ("z_ps", "w_set", "fin_var", "fin_std", "fin_set"))
        stored = [sem(f"stored{n}") for n in range(2)]

        out_t = out.rearrange("b (t p) d -> p (b t) d", p=P)

        words = mybir.dt.uint32
        two_ones = 0x3F803F80

        def parts_stored(engine, layer, q):
            engine.wait_ge(q_out[layer][q % 2], q // 2 * PARTS * 16)
            engine.wait_ge(k_out[layer][q % 2], q // 2 * PARTS * 16)

        block = ctx.enter_context(nc.Block())

        @block.sync
        def _(sp):
            xv = x.rearrange("b (t p) d -> p (b t) d", p=P)
            for q in range(NQ):
                sp.dma_start(xa[:, q * QUAD:(q + 1) * QUAD, :], xv[:, q * QUAD:(q + 1) * QUAD, :]).then_inc(ld_x, 16)
                if q == 0:
                    sp.dma_start(ident_sb[:], ident).then_inc(ld_c, 16)
                    sp.dma_start(w_qkv0[:, 0, :], wq).then_inc(ld_c, 16)
                    sp.dma_start(w_qkv0[:, 1, :].rearrange("p (r n) -> p r n", r=HG),
                                 wk.unsqueeze(1).broadcast_to([P, HG, G * DH])).then_inc(ld_c, 16)
                    sp.dma_start(w_qkv0[:, 2, 0:G * DH], wv).then_inc(ld_c, 16)
            for dst, src in ((cos_sb, c_cos), (sin_sb, c_sin), (nsin_sb, c_nsin), (wre_sb, w_re), (wim_sb, w_im)):
                sp.dma_start(dst[:], src).then_inc(ld_dft, 16)
            sp.wait_ge(rows_set, 1)
            sp.wait_ge(const_set, 5)
            sp.dma_start(q_rep[BIAS_ROW:BIAS_ROW + N_BIAS, :], slopes).then_inc(rep_loaded[0], 16)
            sp.dma_start(k_rep0[BIAS_ROW:BIAS_ROW + N_BIAS, :].rearrange("p (r n) -> p r n", r=RING),
                         kpos.unsqueeze(1).broadcast_to([N_BIAS, RING, S])).then_inc(rep_loaded[0], 16)

            def loaded(layer, s):
                return (s * (1 + PARTS) + 2 * (1 - layer)) * 16

            def store_q(layer, q):
                sp.wait_ge(qk_split[layer], q + 1)
                b, c0 = q // 2, (q % 2) * QN
                for i in range(PARTS):
                    sp.dma_start(dq[layer][i * DH:(i + 1) * DH, b * H:(b + 1) * H, c0:c0 + QN]
                                 .rearrange("d h n -> h d n"),
                                 qk_p[:, q % 2, i, 0:QN]).then_inc(q_out[layer][q % 2], 16)

            def stored_parts(layer, b):
                for odd in range(2):
                    sp.wait_ge(q_out[layer][odd], (b + 1) * PARTS * 16)
                    sp.wait_ge(k_out[layer][odd], (b + 1) * PARTS * 16)

            def load_rep(layer, s):
                slot, n = s % RING, S * (1 if layer == 0 else HG // 2)
                k_rep, kh = (k_rep0, 1) if layer == 0 else (k_rep1, HG)
                sp.dma_start(q_rep[0:ROWS, bass.ds(slot * HG * S, HG * S)],
                             dq[layer][:, bass.ds(s * HG, HG)].rearrange("r h n -> r (h n)").unsqueeze(0).broadcast_to(
                                 [PARTS, PARTS * DH, HG * S])).then_inc(rep_loaded[layer], 16)
                for j in range(PARTS):
                    r0 = j * PARTS * DH
                    sp.dma_start(k_rep[r0:r0 + PARTS * DH, bass.ds(slot * n, n)],
                                 dk[layer][j * DH:(j + 1) * DH, bass.ds(s * kh, kh)].rearrange("d h n -> d (h n)")
                                 .unsqueeze(0).broadcast_to([PARTS, DH, n])).then_inc(rep_loaded[layer], 16)

            def load_mrow(layer, s):
                at = (s % RING) * (HG * S)
                at = at if isinstance(s, int) else sp.snap(at)
                sp.wait_ge(mrow_set[layer], s + 1)
                for part in range(2):
                    dst = q_rep[MAX_ROW + part:MAX_ROW + part + 1, bass.ds(at, HG * S)]
                    sp.dma_start(dst.rearrange("o (r n) -> o r n", n=P), mrow[:, part, :]).then_inc(mrow_in[layer], 16)

            for layer in range(2):
                for q in range(2):
                    store_q(layer, q)
                stored_parts(layer, 0)
                if layer == 1:
                    sp.wait_ge(const_set, 9)
                    sp.wait_ge(s_ps[0], NS * STEPS)
                load_rep(layer, 0)
                for q in range(2, NQ):
                    store_q(layer, q)
                for s in range(1, RING):
                    sp.wait_ge(rep_loaded[layer], loaded(layer, s))
                    load_rep(layer, s)
                if layer == 0:
                    for dst, src in ((wo_sb, wo), (w_qkv1, w_qkv), (wout_sb, w_out), (sim_sb, sim), (rank_sb, rank)):
                        sp.dma_start(dst[:], src).then_inc(ld_w1, 16)
                    sp.dma_start(bias_sb[:], bias.unsqueeze(0).broadcast_to([P, D])).then_inc(ld_bias, 16)
                    sp.dma_start(gate_sb[:], gates.unsqueeze(0).broadcast_to([P, E])).then_inc(ld_bias, 16)
                stored_parts(layer, 1)
                load_mrow(layer, 0)
                done_of = (STEPS if layer == 0 else 2)
                with sp.Fori(0, NS - RING) as s:
                    load_mrow(layer, s + 1)
                    sp.wait_ge(s_ps[layer], done_of * (s + 1))
                    sp.wait_ge(rep_loaded[layer], loaded(layer, s + RING))
                    load_rep(layer, s + RING)
                with sp.Fori(NS - RING, NS - 1) as s:
                    load_mrow(layer, s + 1)
                if layer == 0:
                    sp.wait_ge(ot_ps[0], NT)
                    for n, p in enumerate((p_q, p_k, p_v)):
                        sp.dma_start(big[:, 0:E * W3].rearrange("p (e n) -> p e n", e=E)[:, :, n * D:(n + 1) * D],
                                     p.rearrange("e c h -> c e h")).then_inc(ld_we, 16)
                    sp.dma_start(big[:, E * W3:].rearrange("p (e n) -> p e n", e=E),
                                 p_o.rearrange("e c h -> c e h")).then_inc(ld_we, 16)
            with sp.Fori(0, NQ // 2) as i:
                for u in range(2):
                    q = 2 * i + u
                    at = sp.snap(q * QUAD)
                    sp.wait_ge(fin_set, q + 1)
                    sp.dma_start(out_t[:, bass.ds(at, QUAD), :], y_out[:, u]).then_inc(stored[u], 16)
            for u in range(2):
                sp.wait_ge(stored[u], 16 * (NQ // 2 + 1))

        @block.gpsimd
        def _(pool):
            steps = [0]

            def fill(ap, value):
                pool.memset(ap, value).then_inc(const_set, 1)
                steps[0] += 1
                pool.wait_ge(const_set, steps[0])

            fill(ones[:], 1.0)
            fill(v_all, 0.0)
            fill(v_all.rearrange("p (n c) -> p n c", c=32)[:, :, DH:DH + 1], 1.0)
            fill(k_rep0[64:MAX_ROW, :].bitcast(words), 0)
            fill(k_rep0[MAX_ROW:P, :].bitcast(words), two_ones)
            fill(half[:], -0.5)
            fill(phalf[:], 0.5)

            def store_k(layer, q):
                pool.wait_ge(qk_split[layer], q + 1)
                b, n = q // 2, QN // (1 + layer)
                c0 = (q % 2) * n
                heads, last = (G, G * DH) if layer == 0 else (H, P)
                for j in range(PARTS):
                    pool.dma_start(dk[layer][j * DH:(j + 1) * DH, b * heads:(b + 1) * heads, c0:c0 + n]
                                   .rearrange("d h n -> h d n"),
                                   qk_p[0:last, q % 2, j, QN:QN + n]).then_inc(k_out[layer][q % 2], 16)

            def root(n, q):
                pool.wait_ge(ln_var[n], q + 1)
                pool.tensor_tensor(rstd[:], ve[:], half[:, 0:QUAD], ALU.pow).then_inc(ln_std[n], 1)

            for q in range(NQ):
                store_k(0, q)
            fill(k_rep1[64:MAX_ROW, :].bitcast(words), 0)
            fill(k_rep1[MAX_ROW:P, :].bitcast(words), two_ones)
            with pool.Fori(0, NS) as s:
                pool.wait_ge(p_free[0], KB * s + 2)
                pool.tensor_copy(v_cur[:], v_all[:, bass.ds(s * KB * 32, KB * 32)]).then_inc(v_cur_set, 1)
            pool.wait_ge(p_free[0], KB * NS + 2)
            pool.wait_ge(v_cur_set, NS)
            vb = v_blk.rearrange("p (n c) -> p n c", c=32)
            fill(v_blk[:], 0.0)
            fill(vb[0:KSEG, :, DH:DH + 1], 1.0)
            fill(vb[KSEG:P, :, 16 + DH:16 + DH + 1], 1.0)
            for n in range(2):
                for q in range(NQ):
                    root(n, q)
            for q in range(NQ):
                store_k(1, q)
            def second_parts(first, last):
                for n in range(first, last):
                    at = slice(n * WC, (n + 1) * WC)
                    pool.wait_ge(w_hi_set, n + 1)
                    pool.tensor_tensor(w_lo[:, at], big[:, at], w_hi[:, at].bitcast(F32), ALU.subtract).then_inc(
                        w_lo_set, 1)

            second_parts(0, NWC // 2)
            for q in range(NQ):
                root(2, q)
            pool.wait_ge(sim_root, 1)
            pool.tensor_tensor(sim_n[:], sim_n[:], phalf[:, 0:E], ALU.pow).then_inc(sim_root_done, 1)
            pool.wait_ge(nrm_ss, 1)
            pool.tensor_tensor(r1[0][:], r1[0][:], phalf[:], ALU.pow).then_inc(nrm_root, 1)
            second_parts(NWC // 2, NWC)

            def op_second(t, a, u):
                pool.tensor_tensor(op_lo[:, a, u, :], xT[:, bass.ds(t * P, P)], op_hi[:, a, u, :].bitcast(F32),
                                   ALU.subtract).then_inc(xc_set, 1)

            def keep_v(t, a, u):
                pool.wait_ge(tok_set, t + 1)
                pool.tensor_copy(v_tok[:, bass.ds(t * D, D)], tok_cur[:, a, u, 2 * D:W3]).then_inc(v_set, 1)

            for t in range(QUAD):
                pool.wait_ge(op_hi_set, t + 1)
                op_second(t, t // 2, t % 2)
            with pool.Fori(0, NQ) as i:
                for a in range(2):
                    for u in range(2):
                        t = QUAD * i + 2 * a + u
                        pool.wait_ge(op_hi_set, t + QUAD + 1)
                        op_second((t + QUAD) % NT, a, u)
                    for u in range(2):
                        keep_v(QUAD * i + 2 * a + u, a, u)
            pool.wait_ge(kq_sb, NT + 4)
            for u in range(2):
                pool.tensor_copy(q_cur[:, u, :], qT_all[:, u * P:(u + 1) * P]).then_inc(q_set, 1)
            with pool.Fori(0, NT // 2 - 1) as i:
                for u in range(2):
                    pool.wait_ge(sc_ps, 2 * i + u + 1)
                    pool.tensor_copy(q_cur[:, u, :], qT_all[:, bass.ds((2 * i + u + 2) * P, P)]).then_inc(q_set, 1)
            done = NT + QUAD
            for t in range(QUAD):
                pool.wait_ge(op_hi_set, done + t + 1)
                op_second(t, t // 2, t % 2)
            with pool.Fori(0, NQ) as q:
                for j in range(QUAD):
                    pool.wait_ge(op_hi_set, done + QUAD * q + j + QUAD + 1)
                    op_second((QUAD * q + j + QUAD) % NT, j // 2, j % 2)
                pool.wait_ge(fin_var, q + 1)
                pool.tensor_tensor(rstd[:], ve[:], half[:, 0:QUAD], ALU.pow).then_inc(fin_std, 1)

        @block.tensor
        def _(pe):
            def quad_transposes(src, q, dst):
                for t in range(QUAD):
                    mm = pe.transpose(dst[:, t * P:(t + 1) * P], src[:, q * QUAD + t, :], ident_sb[:])
                return mm

            pe.wait_ge(ld_c, 4 * 16)
            for q in range(NQ):
                pe.wait_ge(ld_x, NQ * 16)
                if q >= 2:
                    pe.wait_ge(xT_sb[0], q - 1)
                quad_transposes(xa, q, bank(q % 2)).then_inc(xT_ps[0], 1)
                if q == 0:
                    pe.wait_ge(wq_scaled, 1)
                pe.wait_ge(xT_sb[0], q + 1)
                if q >= 2:
                    pe.wait_ge(qk_rest, q - 1)
                xq = xT[:, q * QN:(q + 1) * QN]
                pair = bank(2 + 2 * (q % 2), 2)
                pe.matmul(pair[:, 0:QN], w_qkv0[:, 0, :], xq, start=True, stop=True)
                pe.matmul(pair[:, QN:2 * QN], w_qkv0[:, 1, :], xq, start=True, stop=True).then_inc(qk_ps[0], 1)
                if q >= 2:
                    pe.wait_ge(v_sb[0], q - 1)
                for t in range(QUAD):
                    mm = pe.matmul(bank(6 + q % 2)[:, t * 32:(t + 1) * 32], xq[:, t * P:(t + 1) * P],
                                   w_qkv0[:, 2, 0:G * DH], start=True, stop=True)
                mm.then_inc(v_ps[0], 1)
            pe.wait_ge(ld_dft, 5 * 16)
            pe.wait_ge(xT_sb[0], NQ)
            pe.matmul(bank(0)[:, 0:P], wre_sb[:], cos_sb[:], start=True, stop=False)
            pe.matmul(bank(0)[:, 0:P], wim_sb[:], sin_sb[:], start=False, stop=True)
            pe.matmul(bank(1)[:, 0:P], wim_sb[:], cos_sb[:], start=True, stop=False)
            pe.matmul(bank(1)[:, 0:P], wre_sb[:], nsin_sb[:], start=False, stop=True).then_inc(dft_a, 1)
            pe.wait_ge(dft_a_sb, 2)
            pe.matmul(bank(0)[:, 0:P], a_re[:], cos_sb[:], start=True, stop=False)
            pe.matmul(bank(0)[:, 0:P], a_im[:], nsin_sb[:], start=False, stop=True).then_inc(dft_m, 1)

            def max_pair(s, k, only=None):
                h, qb = k // KB, k % KB
                slot = s % RING
                for i in (range(2) if only is None else [only]):
                    n = s * (2 * STEPS + 2) + 2 * k + i
                    if not isinstance(n, int) or n >= 2:
                        pe.wait_ge(max_done[0], n - (2 * k + i > 0))
                    pe.matmul(bank(i), q_rep[0:K_MAX, bass.ds(slot * HG * S + h * S + qb * P, P)],
                              k_rep0[0:K_MAX, bass.ds(slot * S + i * QN, QN)],
                              start=True, stop=True).then_inc(max_ps[0], 1)

            def max_rows(s):
                pe.wait_ge(max_all[0], s + 1)
                pe.transpose(bank(0)[0:STEPS, 0:P], mx[:], ident_sb[:]).then_inc(max_ps[0], 2)

            def load_wait(s):
                pe.wait_ge(rep_loaded[0], (2 + (1 + PARTS) * (s + 1)) * 16)

            def stage(s, last):
                slot = s % RING
                pe.wait_ge(mrow_in[0], 32 * (s + 1))
                for kb in range(KB):
                    for h in range(HG):
                        k = kb * HG + h
                        ahead = None
                        if last < 2 and k < STEPS - LEAD:
                            ahead = (s + 1, k + LEAD)
                        elif last == 0:
                            ahead = (s + 2, k - STEPS + LEAD)
                        turn = last < 2 and k == STEPS - LEAD
                        for i in range(2):
                            if i == 0:
                                pe.wait_ge(s_free[0], s * STEPS + k + 1)
                            mm = pe.matmul(bank(2 + 2 * (k % 2) + i),
                                           k_rep0[0:K_EXP, bass.ds(slot * S + kb * P, P)],
                                           q_rep[0:K_EXP, bass.ds(slot * HG * S + h * S + i * QN, QN)],
                                           start=True, stop=True)
                            if i == 1:
                                mm.then_inc(s_ps[0], 1)
                                if kb > 0:
                                    out_quarter(s, kb - 1, h)
                            if ahead and not turn:
                                max_pair(*ahead, only=i)
                        if turn:
                            max_rows(s + 1)
                            if last == 0:
                                load_wait(s + 2)
                                max_pair(*ahead)
                for i in range(4):
                    out_quarter(s, KB - 1, i)

            def out_quarter(s, kb, i):
                n = S // 4
                pe.wait_ge(s_free[0], s * STEPS + (kb + 1) * HG + 2)
                if kb == 0 and i == 0:
                    pe.wait_ge(v_cur_set, s + 1)
                    pe.wait_ge(o_free[0], s + 1)
                for h in range(HG):
                    mm = pe.matmul(bank(6, 2)[32 * h:32 * h + 32, i * n:(i + 1) * n], v_cur[:, kb * 32:(kb + 1) * 32],
                                   probs[:, kb % 2, h * S + i * n:h * S + (i + 1) * n],
                                   start=(kb == 0 and i % 2 == 0), stop=(kb == KB - 1 and i % 2 == 1),
                                   tile_position=(0, 32 * h))
                if i == 3:
                    mm.then_inc(p_free[0], 1)

            pe.wait_ge(dft_m_sb, 1)
            pe.wait_ge(qk_rest, NQ)
            pe.wait_ge(v_sb[0], NQ)
            load_wait(0)
            for k in range(STEPS):
                max_pair(0, k)
            max_rows(0)
            load_wait(1)
            for k in range(LEAD):
                max_pair(1, k)
            with pe.Fori(0, NS - 2) as s:
                stage(s, 0)
            stage(NS - 2, 1)
            stage(NS - 1, 2)

            def heads_to_rows(layer, source):
                for t in range(NT):
                    if t >= 8:
                        pe.wait_ge(ot_read[layer], t - 7)
                    for g in range(G):
                        mm = pe.transpose(bank(t % 8)[:, g * P:(g + 1) * P], source(t, g), ident_sb[:])
                    mm.then_inc(ot_ps[layer], 1)

            def project(layer, w):
                for q in range(NQ):
                    pe.wait_ge(ot_read[layer], min(NT, max(4 * q + 4, 9 + q)))
                    for t in range(QUAD):
                        mm = pe.transpose(bank(q)[:, t * P:(t + 1) * P], xT[:, (q * QUAD + t) * D:(q * QUAD + t + 1) * D],
                                          ident_sb[:])
                    mm.then_inc(at_ps[layer], 1)
                for q in range(NQ):
                    pe.wait_ge(at_sb[layer], q + 1)
                    for t in range(QUAD):
                        mm = pe.matmul(bank(4 + q)[:, t * P:(t + 1) * P], attT[:, q % 2, t * P:(t + 1) * P], w[:],
                                       start=True, stop=True)
                    mm.then_inc(wo_ps[layer], 1)

            pe.wait_ge(o_free[0], NS + 1)
            pe.wait_ge(ld_w1, 5 * 16)
            heads_to_rows(0, lambda t, g: big[:, (t // KB * G + g) * S + (t % KB) * P:
                                              (t // KB * G + g) * S + (t % KB + 1) * P])
            project(0, wo_sb)
            for q in range(NQ):
                pe.wait_ge(ln_out[0], q + 1)
                quad_transposes(xb, q, bank(q)).then_inc(ft_ps, 1)
            for q in range(NQ):
                pe.wait_ge(ft_sb, q + 1)
                for t in range(QUAD):
                    mm = pe.matmul(bank(4 + q)[:, t * P:(t + 1) * P], attT[:, q % 2, t * P:(t + 1) * P], m_sb[:],
                                   start=True, stop=True)
                mm.then_inc(fm_ps, 1)
            for q in range(NQ):
                pe.wait_ge(ln_out[1], q + 1)
                if q >= 2:
                    pe.wait_ge(v_sb[1], q - 1)
                quad_transposes(xa, q, bank(q % 2)).then_inc(xT_ps[1], 1)
                pe.wait_ge(xT_sb[1], q + 1)
                if q >= 2:
                    pe.wait_ge(ksel_sb, q - 1)
                xq = xT[:, q * QN:(q + 1) * QN]
                pair = bank(2 + 2 * (q % 2), 2)
                pe.matmul(pair[:, 0:QN], w_qkv1[:, 0:D], xq, start=True, stop=True)
                pe.matmul(pair[:, QN:2 * QN], w_qkv1[:, D:2 * D], xq, start=True, stop=True).then_inc(qk_ps[1], 1)
                pe.wait_ge(xsel_set, q + 1)
                for t in range(QUAD):
                    mm = pe.matmul(bank(q % 2)[:, t * P:(t + 1) * P], attT[:, q % 2, t * P:(t + 1) * P],
                                   w_qkv1[:, 2 * D:W3], start=True, stop=True)
                mm.then_inc(v_ps[1], 1)

            def seg_max(s):
                slot = s % RING
                for h in range(HG):
                    n = s * (HG + 2) + h
                    if n >= 2:
                        pe.wait_ge(max_done[1], n - (h > 0))
                    for g in range(KB):
                        mm = pe.matmul(bank(h % 2)[:, g * KSEG:(g + 1) * KSEG],
                                       q_rep[0:K_MAX, slot * HG * S + h * S + g * SEG:slot * HG * S + h * S + (g + 1) * SEG],
                                       k_rep1[0:K_MAX, (slot * HG + h) * S // 2 + g * KSEG:
                                              (slot * HG + h) * S // 2 + (g + 1) * KSEG], start=True, stop=True)
                    mm.then_inc(max_ps[1], 1)
                pe.wait_ge(max_all[1], s + 1)
                pe.transpose(bank(0)[0:STEPS, 0:P], mx[:], ident_sb[:]).then_inc(max_ps[1], 2)

            def seg_scores(s):
                slot = s % RING
                pe.wait_ge(mrow_in[1], 32 * (s + 1))
                for f in range(2):
                    if s:
                        pe.wait_ge(s_free[1], 2 * s - 1 + f)
                    for g in range(4 * f, 4 * f + 4):
                        for h in range(HG):
                            c = (g % 4) * 2 * SEG + (h // 2) * SEG
                            mm = pe.matmul(bank(2 + 2 * f, 2)[KSEG * (h % 2):KSEG * (h % 2 + 1), c:c + SEG],
                                           k_rep1[0:K_EXP, (slot * HG + h) * S // 2 + g * KSEG:
                                                  (slot * HG + h) * S // 2 + (g + 1) * KSEG],
                                           q_rep[0:K_EXP, slot * HG * S + h * S + g * SEG:
                                                 slot * HG * S + h * S + (g + 1) * SEG],
                                           start=True, stop=True, tile_position=(0, KSEG * (h % 2)))
                    mm.then_inc(s_ps[1], 1)

            def seg_out(s):
                b, g4 = s // G, s % G
                pe.wait_ge(s_free[1], 2 * s + 2)
                if s >= 2:
                    pe.wait_ge(o_free[1], s - 1)
                for g in range(KB):
                    for pr in range(2):
                        j = (g % 2) * 2 + pr
                        mm = pe.matmul(bank(6 + s % 2)[32 * j:32 * j + 32, (g // 2) * SEG:(g // 2 + 1) * SEG],
                                       vblk(b * KB + g, g4 * 2 + pr),
                                       probs[:, 0, (s % 2) * 2 * S + g * 2 * SEG + pr * SEG:
                                             (s % 2) * 2 * S + g * 2 * SEG + (pr + 1) * SEG],
                                       start=True, stop=True, tile_position=(0, 32 * j))
                mm.then_inc(p_free[1], 1)

            def vblk(g, pair):
                return v_blk[:, (g * 8 + pair) * 32:(g * 8 + pair + 1) * 32]

            def rep1_wait(s):
                pe.wait_ge(rep_loaded[1], (1 + PARTS) * 16 * (s + 1))

            pe.wait_ge(v_sb[1], NQ)
            pe.wait_ge(ksel_sb, NQ)
            rep1_wait(0)
            seg_max(0)
            for s in range(NS):
                if s + 1 < NS:
                    rep1_wait(s + 1)
                    seg_max(s + 1)
                seg_scores(s)
                if s:
                    seg_out(s - 1)
            seg_out(NS - 1)

            def seg_heads(t, g):
                s = t // KB * G + g
                return o_seg[:, s * 512 + (t % KB // 2) * P:s * 512 + (t % KB // 2 + 1) * P]

            pe.wait_ge(o_free[1], NS)
            heads_to_rows(1, seg_heads)
            project(1, wout_sb)
            pe.wait_ge(sim_sq, 1)
            for q in range(NQ):
                pe.wait_ge(ln_out[2], q + 1)
                quad_transposes(xb, q, bank(q)).then_inc(x3T_ps, 1)
            pe.matmul(bank(6)[:, 0:E], ones[:], rt[0][:, 0, :], start=True, stop=True).then_inc(sim_ss, 1)
            pe.wait_ge(sim_ready, 1)
            pe.wait_ge(x3T_sb, NQ)
            for t in range(NT):
                mm = pe.matmul(bank(7)[:, t * E:(t + 1) * E], xT[:, t * P:(t + 1) * P], sim_n[:], start=True, stop=True)
            mm.then_inc(lg_ps, 1)

            pe.wait_ge(w_ready, 1)
            pe.wait_ge(w_lo_set, NWC)

            def product(dst, a, u, at, n):
                hi, lo = op_hi[:, a, u, :], op_lo[:, a, u, :]
                pe.matmul(dst, hi, w_hi[:, at:at + n], start=True, stop=False)
                pe.matmul(dst, hi, w_lo[:, at:at + n], start=False, stop=False)
                return pe.matmul(dst, lo, w_hi[:, at:at + n], start=False, stop=True)

            def to_channels(pair, a):
                pe.wait_ge(tok_set, 2 * pair + 2)
                pe.wait_ge(kq_sb, 2 * pair + 2)
                for u in range(2):
                    for n in range(2):
                        mm = pe.transpose(bank(4 + a)[:, (2 * u + n) * P:(2 * u + n + 1) * P],
                                          tok_cur[:, a, u, n * P:(n + 1) * P], ident_sb[:])
                mm.then_inc(kq_ps, 2)

            with pe.Fori(0, NQ) as i:
                for a in range(2):
                    pair = 2 * i + a
                    pe.wait_ge(xc_set, 2 * pair + 2)
                    for e in range(E):
                        for u in range(2):
                            pe.wait_ge(y_free, pair * 2 * E + 2 * e + u + 1)
                            product(bank((2 * e + u) % YR)[:, 0:W3], a, u, e * W3, W3).then_inc(y_ps, 1)
                        if a == 1 and e == 2:
                            to_channels(pair - 1, 0)
                to_channels(2 * i + 1, 1)

            def scores(t, u):
                pe.wait_ge(q_set, t + 1)
                pe.wait_ge(p_set, t + 1)
                for i in range(2):
                    mm = pe.matmul(bank(2 * u + i), q_cur[:, u, :], kT_all[:, bass.ds(t // KB * S + i * QN, QN)],
                                   start=True, stop=True)
                mm.then_inc(sc_ps, 1)

            def probs_T(t, u):
                pe.wait_ge(p_set, t + 3)
                pe.wait_ge(pt_sb, 2 * t + 2)
                for kb in range(KB):
                    mm = pe.transpose(bank(4 + kb // 4)[:, (kb % 4) * P:(kb % 4 + 1) * P],
                                      p_cur[:, u, kb * P:(kb + 1) * P], ident_sb[:])
                mm.then_inc(pt_ps, 1)

            def outputs(t, u, b):
                pe.wait_ge(pt_sb, 2 * t + 4)
                pe.wait_ge(o_sb, t + 1)
                for kb in range(KB):
                    mm = pe.matmul(bank(6 + u)[:, 0:P], v_tok[:, (b * KB + kb) * D:(b * KB + kb + 1) * D],
                                   pT_cur[:, u, kb * P:(kb + 1) * P], start=(kb == 0), stop=(kb == KB - 1))
                mm.then_inc(o_ps, 1)

            pe.wait_ge(v_set, NT + 4)
            scores(0, 0)
            scores(1, 1)
            probs_T(0, 0)
            for b in range(NB):
                with pe.Fori(b * KB // 2, (b + 1) * KB // 2 - b) as i:
                    for u in range(2):
                        t = 2 * i + u
                        scores(t + 2, u)
                        outputs(t, u, b)
                        probs_T(t + 1, 1 - u)
            outputs(NT - 2, 0, NB - 1)
            probs_T(NT - 1, 1)
            outputs(NT - 1, 1, NB - 1)

            with pe.Fori(0, NQ) as i:
                for a in range(2):
                    pair = 2 * i + a
                    pe.wait_ge(o_sb, NT + 2)
                    pe.wait_ge(xc_set, NT + QUAD + 2 * pair + 2)
                    for n in range(E // 4):
                        for u in range(2):
                            pe.wait_ge(acc_step, NT + 8 * (pair * (E // 4) + n))
                            product(bank((2 * n + u) % 4), a, u, E * W3 + n * 4 * D, 4 * D).then_inc(z_ps, 1)

        @block.scalar
        def _(act):
            def copy(dst, src):
                return act.activation(dst, src, ACT.Copy)

            act.wait_ge(const_set, 1)
            act.activation(tick[:, 1:2], ones[:, 0:1], ACT.Exp).then_inc(s_free[0], 2)
            for q in range(NQ):
                act.wait_ge(xT_ps[0], q + 1)
                copy(xT[:, q * QN:(q + 1) * QN], bank(q % 2)).then_inc(xT_sb[0], 1)
                act.wait_ge(qk_ps[0], q + 1)
                if q >= 2:
                    parts_stored(act, 0, q)
                copy(qk_p[:, q % 2, 0, :], bank(2 + 2 * (q % 2), 2)).then_inc(qk_hi, 1)
                act.wait_ge(v_ps[0], q + 1)
                act.wait_ge(const_set, 3)
                va = v_all.rearrange("p (s k c) -> p s k c", s=NS, k=KB)
                b, k0 = q // 2, (q % 2) * QUAD
                copy(va[:, b * G:(b + 1) * G, k0:k0 + QUAD, 0:DH],
                     bank(6 + q % 2)[:, 0:QUAD * 32].rearrange("p (t g d) -> p g t d", t=QUAD, g=G)).then_inc(v_sb[0], 1)
                act.wait_ge(qk_rest, q + 1)
                copy(qk_p[:, q % 2, 1, :], qk_r[:]).then_inc(qk_mid, 1)

            def exps(s):
                for k in range(STEPS):
                    kb, h = k // HG, k % HG
                    act.wait_ge(s_ps[0], s * STEPS + k + 1)
                    if h == 0:
                        act.wait_ge(p_free[0], s * KB + kb + 1)
                    act.activation(probs[:, kb % 2, h * S:(h + 1) * S], bank(2 + 2 * (k % 2), 2),
                                   ACT.Exp).then_inc(s_free[0], 1)
                act.wait_ge(p_free[0], (s + 1) * KB + 2)
                copy(big[:, bass.ds(s * S, S)], bank(6, 2)).then_inc(o_free[0], 1)

            with act.Fori(0, NS) as s:
                exps(s)

            def attT_copies(ps_sem, sb_sem, done_sem):
                for q in range(NQ):
                    act.wait_ge(ps_sem, q + 1)
                    if q >= 2:
                        act.wait_ge(done_sem, q - 1)
                    copy(attT[:, q % 2, :], bank(q)).then_inc(sb_sem, 1)

            attT_copies(at_ps[0], at_sb[0], wo_ps[0])
            attT_copies(ft_ps, ft_sb, fm_ps)

            def dilated(ap, par):
                v = ap.rearrange("p (r two i c) -> p r two i c", two=2, i=16, c=2)
                return v[:, :, par, :, par]

            for q in range(NQ):
                act.wait_ge(xT_ps[1], q + 1)
                copy(xT[:, q * QN:(q + 1) * QN], bank(q % 2)).then_inc(xT_sb[1], 1)
                act.wait_ge(qk_ps[1], q + 1)
                if q >= 1:
                    act.wait_ge(qk_split[1], q)
                pair = bank(2 + 2 * (q % 2), 2)
                act.activation(qk[:, 0:QN], pair[:, 0:QN], ACT.Copy, scale=scale)
                ks = qk[:, QN:QN + QN // 2].rearrange("p (r two i) -> p r two i", two=2, i=16)
                for par in range(2):
                    mm = copy(ks[:, :, par, :], dilated(pair[:, QN:2 * QN], par))
                mm.then_inc(ksel_sb, 1)
                act.wait_ge(v_ps[1], q + 1)
                act.wait_ge(const_set, 12)
                vb = v_blk.rearrange("p (g r c) -> p g r c", g=NT, r=8)[:, q * QUAD:(q + 1) * QUAD]
                vp = bank(q % 2).rearrange("p (g r two d) -> p g r two d", g=QUAD, r=8, two=2)
                copy(vb[0:KSEG, :, :, 0:DH], vp[0:KSEG, :, :, 0, :])
                copy(vb[KSEG:P, :, :, 16:16 + DH], vp[KSEG:P, :, :, 1, :]).then_inc(v_sb[1], 1)

            for s in range(NS):
                for f in range(2):
                    act.wait_ge(s_ps[1], 2 * s + f + 1)
                    if s >= 2 and f == 0:
                        act.wait_ge(p_free[1], s - 1)
                    act.activation(probs[:, 0, (s % 2) * 2 * S + f * S:(s % 2) * 2 * S + (f + 1) * S],
                                   bank(2 + 2 * f, 2), ACT.Exp).then_inc(s_free[1], 1)
            act.wait_ge(ld_we, 4 * 16)
            act.wait_ge(p_free[1], NS)
            for n in range(NWC):
                copy(w_hi[:, n * WC:(n + 1) * WC], big[:, n * WC:(n + 1) * WC]).then_inc(w_hi_set, 1)
            attT_copies(at_ps[1], at_sb[1], wo_ps[1])
            for q in range(NQ):
                act.wait_ge(x3T_ps, q + 1)
                copy(xT[:, q * QN:(q + 1) * QN], bank(q)).then_inc(x3T_sb, 1)
            act.wait_ge(ld_bias, 32)
            act.activation(gate_sb[:], gate_sb[:], ACT.Exp, scale=-1.0).then_inc(gate_exp, 1)
            act.wait_ge(ex_in, 1)
            act.activation(rt[1][:], rt[1][:], ACT.Exp).then_inc(ex_out, 1)
            act.wait_ge(x3T_sb, NQ)
            for a in range(2):
                for u in range(2):
                    copy(op_hi[:, a, u, :], xT[:, (2 * a + u) * P:(2 * a + u + 1) * P]).then_inc(op_hi_set, 1)
            with act.Fori(0, NQ) as i:
                for a in range(2):
                    pair = 2 * i + a
                    act.wait_ge(y_ps, 2 * E * (pair + 1))
                    for u in range(2):
                        copy(op_hi[:, a, u, :], xT[:, bass.ds((2 * pair + 4 + u) % NT * P, P)])\
                            .then_inc(op_hi_set, 1)
                    act.wait_ge(kq_ps, 2 * pair + 2 + 4)
                    for u in range(2):
                        at = 2 * pair + u
                        copy(qT_all[:, bass.ds(at * P, P)], bank(4 + a)[:, 2 * u * P:(2 * u + 1) * P])
                        copy(kT_all[:, bass.ds(at * P, P)], bank(4 + a)[:, (2 * u + 1) * P:(2 * u + 2) * P])\
                            .then_inc(kq_sb, 1)

            act.wait_ge(kq_sb, NT + 4)
            for s_, n in ((o_sb, 2), (p_set, 2), (pt_sb, 2), (pt_ps, 1), (o_ps, 2)):
                act.sem_inc(s_, n)

            def p_exp(t, u):
                act.wait_ge(nmax_set, t + 1)
                act.wait_ge(pt_ps, max(t, 1) if isinstance(t, int) else t)
                act.activation(p_cur[:, u, :], bank(2 * u, 2), ACT.Exp, bias=m_cur[:, u, 1:2], scale=scale_moe,
                               accum_out=m_cur[:, u, 2:3]).then_inc(p_set, 1)

            def pT_copy(t, u):
                act.wait_ge(pt_ps, t + 2)
                act.wait_ge(o_ps, t + 1)
                copy(pT_cur[:, u, 0:QN], bank(4)).then_inc(pt_sb, 1)

            def o_copy(t, u):
                act.wait_ge(o_ps, t + 3)
                copy(oT_all[:, bass.ds(t * P, P)], bank(6 + u)[:, 0:P]).then_inc(o_sb, 1)

            p_exp(0, 0)
            p_exp(1, 1)
            pT_copy(0, 0)
            with act.Fori(0, NT // 2 - 1) as i:
                for u in range(2):
                    t = 2 * i + u
                    o_copy(t, u)
                    pT_copy(t + 1, 1 - u)
                    p_exp(t + 2, u)
            o_copy(NT - 2, 0)
            pT_copy(NT - 1, 1)
            o_copy(NT - 1, 1)
            act.wait_ge(o_sb, NT + 2)

            for a in range(2):
                for u in range(2):
                    copy(op_hi[:, a, u, :], oT_all[:, (2 * a + u) * P:(2 * a + u + 1) * P]).then_inc(op_hi_set, 1)
            with act.Fori(0, NQ) as i:
                for a in range(2):
                    pair = 2 * i + a
                    act.wait_ge(z_ps, E // 2 * (pair + 1))
                    for u in range(2):
                        copy(op_hi[:, a, u, :], oT_all[:, bass.ds((2 * pair + 4 + u) % NT * P, P)])\
                            .then_inc(op_hi_set, 1)

        @block.vector
        def _(dve):
            steps = [0]

            def link(ins):
                steps[0] += 1
                ins.then_inc(dve_step, 1)
                dve.wait_ge(dve_step, steps[0])

            dve.memset(q_rep[64:P, :].bitcast(words), 0).then_inc(rows_set, 1)
            dve.wait_ge(ld_c, 4 * 16)
            dve.tensor_scalar(w_qkv0[:, 0, :], w_qkv0[:, 0, :], scale, None, ALU.mult).then_inc(wq_scaled, 1)

            for q in range(NQ):
                dve.wait_ge(qk_hi, q + 1)
                if q:
                    dve.wait_ge(qk_split[0], q)
                dve.tensor_tensor(qk_r[:], bank(2 + 2 * (q % 2), 2), qk_p[:, q % 2, 0, :], ALU.subtract).then_inc(
                    qk_rest, 1)
                dve.wait_ge(qk_mid, q + 1)
                if q >= 2:
                    parts_stored(dve, 0, q)
                dve.tensor_tensor(qk_p[:, q % 2, 2, :], qk_r[:], qk_p[:, q % 2, 1, :], ALU.subtract).then_inc(
                    qk_split[0], 1)

            def split(q, n):
                dve.wait_ge(ksel_sb, q + 1)
                if q >= 2:
                    parts_stored(dve, 1, q)
                parts = [qk_p[:, q % 2, i, 0:n] for i in range(PARTS)]
                link(dve.tensor_copy(parts[0], qk[:, 0:n]))
                link(dve.tensor_tensor(qk_r[:, 0:n], qk[:, 0:n], parts[0], ALU.subtract))
                link(dve.tensor_copy(parts[1], qk_r[:, 0:n]))
                dve.tensor_tensor(parts[2], qk_r[:, 0:n], parts[1], ALU.subtract).then_inc(qk_split[1], 1)

            dve.wait_ge(dft_a, 1)
            dve.tensor_scalar(a_re[:], bank(0)[:, 0:P], 1.0 / D, None, ALU.mult).then_inc(dft_a_sb, 1)
            dve.tensor_scalar(a_im[:], bank(1)[:, 0:P], 1.0 / D, None, ALU.mult).then_inc(dft_a_sb, 1)
            dve.wait_ge(dft_m, 1)
            dve.tensor_copy(m_sb[:], bank(0)[:, 0:P]).then_inc(dft_m_sb, 1)
            dve.sem_inc(p_free[0], 2)
            dve.memset(rstd[:, 0:1], 0.0).then_inc(o_free[0], 1)

            def max_pair(s, k):
                for i in range(2):
                    n = s * (2 * STEPS + 2) + 2 * k + i
                    dve.wait_ge(max_ps[0], n + 1)
                    dve.reduce_max(mx2[:, 2 * k + i:2 * k + i + 1], bank(i), AX_X).then_inc(max_done[0], 1)

            def max_rows(s):
                n = s * (2 * STEPS + 2) + 2 * STEPS
                dve.wait_ge(max_done[0], n)
                if not isinstance(s, int):
                    dve.wait_ge(mrow_in[0], 32 * s)
                dve.reduce_max(mx[:], mx2[:].rearrange("p (k i) -> p k i", i=2), AX_X).then_inc(max_all[0], 1)
                dve.wait_ge(max_ps[0], n + 2)
                dve.tensor_scalar(mrow[:, 0, :], bank(0)[0:STEPS, 0:P], -1.0, None, ALU.mult).then_inc(max_done[0], 1)
                dve.wait_ge(max_done[0], n + 1)
                dve.scalar_tensor_tensor(out=mrow[:, 1, :], in0=bank(0)[0:STEPS, 0:P], scalar=-1.0, in1=mrow[:, 0, :],
                                         op0=ALU.mult, op1=ALU.subtract).then_inc(max_done[0], 1)
                dve.wait_ge(max_done[0], n + 2)
                dve.sem_inc(mrow_set[0], 1)

            for k in range(STEPS):
                max_pair(0, k)
            max_rows(0)
            for k in range(LEAD):
                max_pair(1, k)
            with dve.Fori(0, NS - 2) as s:
                for k in range(LEAD, STEPS):
                    max_pair(s + 1, k)
                max_rows(s + 1)
                for k in range(LEAD):
                    max_pair(s + 2, k)
            for k in range(LEAD, STEPS):
                max_pair(NS - 1, k)
            dve.wait_ge(mrow_in[0], 32 * (NS - 1))
            max_rows(NS - 1)

            def norm(n, q, src, dst, done):
                for t in range(QUAD):
                    ins = dve.bn_stats(st[:, t, :], src[:, t, :])
                link(ins)
                for t in range(QUAD):
                    ins = dve.bn_aggr(mv[:, t, :], st[:, t, :])
                link(ins)
                dve.tensor_scalar(ve[:], mv[:, :, 1], EPS, None, ALU.add).then_inc(ln_var[n], 1)
                dve.wait_ge(ln_std[n], q + 1)
                for t in range(QUAD):
                    ins = dve.tensor_scalar(dst[:, q * QUAD + t, :], src[:, t, :], mv[:, t, 0:1], rstd[:, t:t + 1],
                                            ALU.subtract, ALU.mult)
                link(ins)
                dve.sem_inc(done, 1)

            def heads(layer, view):
                for t in range(NT):
                    dve.wait_ge(ot_ps[layer], t + 1)
                    o, total, r = view(t)
                    link(dve.reciprocal(r, total))
                    a = xT[:, t * D:(t + 1) * D]
                    dve.tensor_tensor(a.rearrange("p (h d) -> p h d", d=DH), o,
                                      r.unsqueeze(2).broadcast_to([P, H, DH]), ALU.mult).then_inc(ot_read[layer], 1)

            def view0(t):
                b = bank(t % 8).rearrange("p (h c) -> p h c", c=32)
                return b[:, :, 0:DH], b[:, :, DH], rec[:, t % 2, :]

            heads(0, view0)

            def add_norm(n, ready, src, dst, bias=None):
                for q in range(NQ):
                    dve.wait_ge(ready, q + 1)
                    link(dve.tensor_tensor(res[:], bank(4 + q).rearrange("p (t d) -> p t d", t=QUAD),
                                           src[:, q * QUAD:(q + 1) * QUAD, :], ALU.add))
                    if bias is not None:
                        link(dve.tensor_tensor(res[:], res[:], bias[:].unsqueeze(1).broadcast_to([P, QUAD, D]), ALU.add))
                    norm(n, q, res, dst, ln_out[n])

            add_norm(0, wo_ps[0], xa, xb)
            dve.wait_ge(ld_bias, 32)
            add_norm(1, fm_ps, xb, xa, bias_sb)
            for q in range(NQ):
                dve.wait_ge(xT_sb[1], q + 1)
                if q >= 2:
                    dve.wait_ge(v_ps[1], q - 1)
                xs = attT[:, q % 2, :].rearrange("p (g dup r two i) -> p g dup r two i", g=QUAD, dup=2, r=2, two=2)
                xq = xT[:, q * QN:(q + 1) * QN].rearrange("p (g r two i c) -> p g r two i c", g=QUAD, r=2, two=2, c=2)
                for dup in range(2):
                    for par in range(2):
                        for g in range(QUAD):
                            ins = dve.tensor_copy(xs[:, g, dup, :, par, :], xq[:, g, :, par, :, par])
                ins.then_inc(xsel_set, 1)
                split(q, QN + QN // 2)

            def seg_max(s):
                for h in range(HG):
                    n = s * (HG + 2) + h
                    dve.wait_ge(max_ps[1], n + 1)
                    dve.reduce_max(mx[:, h * KB:(h + 1) * KB], bank(h % 2).rearrange("p (g k) -> p g k", g=KB),
                                   AX_X).then_inc(max_done[1], 1)
                dve.wait_ge(max_done[1], s * (HG + 2) + HG)
                dve.sem_inc(max_all[1], 1)
                n = s * (HG + 2) + HG
                dve.wait_ge(max_ps[1], n + 2)
                if s:
                    dve.wait_ge(mrow_in[1], 32 * s)
                dve.tensor_scalar(mrow[:, 0, :], bank(0)[0:STEPS, 0:P], -1.0, None, ALU.mult).then_inc(max_done[1], 1)
                dve.wait_ge(max_done[1], n + 1)
                dve.scalar_tensor_tensor(out=mrow[:, 1, :], in0=bank(0)[0:STEPS, 0:P], scalar=-1.0, in1=mrow[:, 0, :],
                                         op0=ALU.mult, op1=ALU.subtract).then_inc(max_done[1], 1)
                dve.wait_ge(max_done[1], n + 2)
                dve.sem_inc(mrow_set[1], 1)

            def seg_o(s):
                dve.wait_ge(p_free[1], s + 1)
                dve.tensor_copy(o_seg[:, s * 512:(s + 1) * 512], bank(6 + s % 2)).then_inc(o_free[1], 1)

            seg_max(0)
            for s in range(NS):
                if s + 1 < NS:
                    seg_max(s + 1)
                if s:
                    seg_o(s - 1)
            seg_o(NS - 1)

            def view1(t):
                sp = t % 2
                b = bank(t % 8).rearrange("p (g s h c) -> p g s h c", g=G, s=2, h=4)[:, :, sp]
                return b[:, :, :, 0:DH], b[:, :, :, DH], rec[:, t % 2, :].rearrange("p (g h) -> p g h", g=G)

            for t in range(NT):
                dve.wait_ge(ot_ps[1], t + 1)
                o, total, r = view1(t)
                link(dve.reciprocal(r, total))
                a = xT[:, t * D:(t + 1) * D]
                dve.tensor_tensor(a.rearrange("p (g h d) -> p g h d", g=G, h=4), o,
                                  r.unsqueeze(3).broadcast_to([P, G, 4, DH]), ALU.mult).then_inc(ot_read[1], 1)
            link(dve.tensor_tensor(rt[0][:, 0, :], sim_sb[:], sim_sb[:], ALU.mult))
            dve.sem_inc(sim_sq, 1)
            add_norm(2, wo_ps[1], xa, xb)

            dve.wait_ge(sim_ss, 1)
            link(dve.tensor_copy(sim_n[:], bank(6)[:, 0:E]))
            dve.sem_inc(sim_root, 1)
            dve.wait_ge(sim_root_done, 1)
            link(dve.tensor_scalar(sim_n[:], sim_n[:], 1e-12, None, ALU.max))
            link(dve.reciprocal(sim_n[:], sim_n[:]))
            link(dve.tensor_tensor(sim_n[:], sim_sb[:], sim_n[:], ALU.mult))
            dve.sem_inc(sim_ready, 1)
            for q in range(NQ):
                xq = xb[:, q * QUAD:(q + 1) * QUAD, :]
                link(dve.tensor_tensor(res[:], xq, xq, ALU.mult))
                link(dve.reduce_sum(r1[0][:, q * QUAD:(q + 1) * QUAD], res[:], AX_X))
            dve.sem_inc(nrm_ss, 1)
            dve.wait_ge(nrm_root, 1)
            link(dve.tensor_scalar(r1[0][:], r1[0][:], 1e-12, None, ALU.max))
            link(dve.reciprocal(r1[0][:], r1[0][:]))
            dve.wait_ge(gate_exp, 1)
            link(dve.tensor_scalar(gate_sb[:], gate_sb[:], 1.0, None, ALU.add))
            link(dve.reciprocal(gate_sb[:], gate_sb[:]))

            def over_e(v):
                return v.unsqueeze(2).broadcast_to([P, NT, E])

            def over_t(v):
                return v.unsqueeze(1).broadcast_to([P, NT, E])

            lg, t1, t2_, t3, t4, t5 = (r[:] for r in rt)
            top, r_a, r_b = r1[1][:], r1[2][:], r1[3][:]
            dve.wait_ge(lg_ps, 1)
            link(dve.tensor_tensor(lg, bank(7)[:, 0:NT * E].rearrange("p (t e) -> p t e", e=E), over_e(r1[0][:]), ALU.mult))
            link(dve.tensor_tensor(lg, lg, over_t(gate_sb[:]), ALU.subtract))
            link(dve.reduce_max(top, lg, AX_X))

            def first_of(values, best, one_hot, work):
                link(dve.tensor_tensor(work, values, over_e(best), ALU.is_equal))
                link(dve.tensor_tensor(work, work, over_t(rank_sb[:]), ALU.mult))
                link(dve.reduce_max(r_a, work, AX_X))
                link(dve.tensor_tensor(one_hot, work, over_e(r_a), ALU.is_equal))

            first_of(lg, top, t2_, t1)
            link(dve.scalar_tensor_tensor(out=t3, in0=t2_, scalar=-1e30, in1=lg, op0=ALU.mult, op1=ALU.add))
            link(dve.reduce_max(r_b, t3, AX_X))
            first_of(t3, r_b, t4, t1)
            link(dve.tensor_tensor(t2_, t2_, t4, ALU.add))
            link(dve.tensor_scalar(r_a, top, 0.0, None, ALU.is_le))
            link(dve.tensor_tensor(t2_, t2_, over_e(r_a), ALU.mult))
            link(dve.tensor_scalar(t3, lg, 0.0, None, ALU.is_gt))
            link(dve.tensor_tensor(t2_, t2_, t3, ALU.add))
            link(dve.tensor_scalar(t3, lg, 0.0, None, ALU.max))
            link(dve.tensor_scalar(r_b, top, 0.0, None, ALU.max))
            link(dve.tensor_tensor(t1, t3, over_e(r_b), ALU.subtract))
            dve.sem_inc(ex_in, 1)
            dve.wait_ge(ex_out, 1)
            link(dve.tensor_tensor(t1, t1, t2_, ALU.mult))
            link(dve.reduce_sum(r_a, t1, AX_X))
            link(dve.reciprocal(r_a, r_a))
            link(dve.tensor_tensor(w_rt[:], t1, over_e(r_a), ALU.mult))
            dve.sem_inc(w_ready, 1)
            dve.sem_inc(y_free, YR)
            dve.sem_inc(v_set, 4)
            dve.sem_inc(kq_ps, 4)
            dve.sem_inc(kq_sb, 4)

            def weights(q, first):
                dve.tensor_copy(w_cur[:].rearrange("p t e -> p (t e)"),
                                w_rt[:].rearrange("p t e -> p (t e)")[:, bass.ds(q * QUAD * E, QUAD * E)])\
                   .then_inc(w_set, 1)
                dve.wait_ge(w_set, q + first + 1)

            with dve.Fori(0, NQ) as i:
                weights(i, 0)
                for a in range(2):
                    pair = 2 * i + a
                    for e in range(E):
                        for u in range(2):
                            n = pair * 2 * E + 2 * e + u
                            y, w = bank((2 * e + u) % YR)[:, 0:W3], w_cur[:, 2 * a + u, e:e + 1]
                            dve.wait_ge(y_ps, n + 1)
                            if e == 0:
                                dve.wait_ge(v_set, 2 * pair + u + 1)
                                dve.wait_ge(kq_ps, 2 * pair + 2)
                                ins = dve.tensor_scalar(tok_cur[:, a, u, :], y, w, None, ALU.mult)
                            else:
                                dve.wait_ge(y_free, n - 1 + YR)
                                ins = dve.scalar_tensor_tensor(out=tok_cur[:, a, u, :], in0=y, scalar=w,
                                                               in1=tok_cur[:, a, u, :], op0=ALU.mult, op1=ALU.add)
                            ins.then_inc(y_free, 1)
                    dve.wait_ge(y_free, (pair + 1) * 2 * E + YR)
                    dve.sem_inc(tok_set, 2)

            def row_max(t, u):
                dve.wait_ge(sc_ps, t + 1)
                dve.reduce_max(m_cur[:, u, 0:1], bank(2 * u, 2), AX_X).then_inc(acc_step, 1)
                dve.wait_ge(acc_step, t + 1)
                dve.tensor_scalar(m_cur[:, u, 1:2], m_cur[:, u, 0:1], -scale_moe, None, ALU.mult).then_inc(nmax_set, 1)

            def pT_copy(t, u):
                dve.wait_ge(p_set, t + 3)
                dve.reciprocal(r_sum[:, bass.ds(t, 1)], m_cur[:, u, 2:3]).then_inc(fin_step, 1)
                dve.wait_ge(pt_ps, t + 2)
                dve.wait_ge(o_ps, t + 1)
                dve.tensor_copy(pT_cur[:, u, QN:2 * QN], bank(5)).then_inc(pt_sb, 1)

            row_max(0, 0)
            row_max(1, 1)
            pT_copy(0, 0)
            with dve.Fori(0, NT // 2 - 1) as i:
                for u in range(2):
                    t = 2 * i + u
                    row_max(t + 2, u)
                    pT_copy(t + 1, 1 - u)
            pT_copy(NT - 1, 1)
            dve.wait_ge(fin_step, NT)
            link(dve.tensor_tensor(w_rt[:], w_rt[:], over_e(r_sum[:]), ALU.mult))
            dve.sem_inc(acc_step, 8)
            for u in range(2):
                dve.sem_inc(stored[u], 16)

            per = QUAD * E

            with dve.Fori(0, NQ // 2) as i:
                for v in range(2):
                    q = 2 * i + v
                    weights(q, NQ)
                    for a in range(2):
                        for n in range(E // 4):
                            for j in range(4):
                                for u in range(2):
                                    t, e = 2 * a + u, 4 * n + j
                                    k = q * per + a * 2 * E + 2 * e + u
                                    z = bank((2 * n + u) % 4)[:, j * D:(j + 1) * D]
                                    if j == 0:
                                        dve.wait_ge(z_ps, q * E + a * (E // 2) + 2 * n + u + 1)
                                    if e == 0:
                                        x_res = xb[:].rearrange("p t d -> p (t d)")[:, bass.ds((q * QUAD + t) * D, D)]
                                    else:
                                        x_res = y_acc[:, t, :]
                                        dve.wait_ge(acc_step, NT + 8 + k - 1)
                                    dve.scalar_tensor_tensor(out=y_acc[:, t, :], in0=z, scalar=w_cur[:, t, e:e + 1],
                                                             in1=x_res, op0=ALU.mult, op1=ALU.add)\
                                       .then_inc(acc_step, 1)
                    dve.wait_ge(acc_step, NT + 8 + (q + 1) * per)
                    for t in range(QUAD):
                        ins = dve.bn_stats(st[:, t, :], y_acc[:, t, :])
                    ins.then_inc(fin_step, 1)
                    dve.wait_ge(fin_step, NT + 4 * q + 1)
                    dve.memset(tick[:, 0:1], 0.0).then_inc(fin_step, 1)
                    for t in range(QUAD):
                        ins = dve.bn_aggr(mv[:, t, :], st[:, t, :])
                    ins.then_inc(fin_step, 1)
                    dve.wait_ge(fin_step, NT + 4 * q + 3)
                    dve.tensor_scalar(ve[:], mv[:, :, 1], EPS, None, ALU.add).then_inc(fin_var, 1)
                    dve.wait_ge(fin_std, q + 1)
                    dve.wait_ge(stored[v], 16 * (i + 1))
                    for t in range(QUAD):
                        ins = dve.tensor_scalar(y_out[:, v, t, :], y_acc[:, t, :], mv[:, t, 0:1], rstd[:, t:t + 1],
                                                ALU.subtract, ALU.mult)
                    ins.then_inc(fin_step, 1)
                    dve.wait_ge(fin_step, NT + 4 * q + 4)
                    dve.sem_inc(fin_set, 1)


def constants():
    def bf16(a):
        a = np.asarray(a, np.float32).view(np.uint32).astype(np.uint64)
        return ((a + 0x7FFF + ((a >> 16) & 1)) >> 16).astype(np.uint16)

    def widen(a):
        return (a.astype(np.uint32) << 16).view(np.float32)

    n = np.arange(D)
    angle = 2.0 * np.pi * ((n[:, None] * n[None, :]) % D) / D
    start = 2.0 ** -0.5
    slope = np.array([start * start ** i for i in range(H)], np.float32)
    s1 = bf16(slope)
    s2 = bf16(slope - widen(s1))
    s3 = bf16(slope - widen(s1) - widen(s2))
    rows = np.stack([s1, s1, s2, s2, s3, s3])
    slopes = np.ascontiguousarray(np.broadcast_to(rows.reshape(N_BIAS, G, HG, 1).transpose(1, 0, 2, 3),
                                                  (G, N_BIAS, HG, S)).transpose(1, 0, 2, 3).reshape(N_BIAS, H * S))
    pos = np.arange(S) - (S - 1)
    hi = pos // 8 * 8
    kpos = np.stack([bf16(hi), bf16(pos - hi)] * PARTS)
    return {"ident": np.eye(P, dtype=np.float32), "c_cos": np.cos(angle).astype(np.float32),
            "c_sin": np.sin(angle).astype(np.float32), "c_nsin": (-np.sin(angle)).astype(np.float32),
            "slopes": slopes, "kpos": np.ascontiguousarray(kpos),
            "rank": np.ascontiguousarray(np.broadcast_to(np.arange(E, 0, -1, dtype=np.float32), (P, E)))}


_INS = ["L0_attn_x", "L0_attn_Wq", "L0_attn_Wk", "L0_attn_Wv", "L0_attn_Wo", "L0_ffn_w_freq_real",
        "L0_ffn_w_freq_imag", "L0_ffn_bias", "L1_attn_W_qkv", "L1_attn_W_out", "L1_ffn_sim_matrix", "L1_ffn_gates",
        "L1_ffn_q_proj", "L1_ffn_k_proj", "L1_ffn_v_proj", "L1_ffn_o_proj"]


def kernel(**inputs):
    import concourse.bacc as bacc
    from concourse.bass_utils import run_bass_kernel_spmd

    nc = bacc.Bacc("TRN2", target_bir_lowering=False, num_devices=1)
    arrays, args = {}, []
    for name in _INS:
        a = np.ascontiguousarray(inputs[name])
        arrays["in_" + name] = a
        args.append(nc.dram_tensor("in_" + name, a.shape, mybir.dt.from_np(a.dtype), kind="ExternalInput").ap())
    for name, a in constants().items():
        arrays["const_" + name] = a
        ap = nc.dram_tensor("const_" + name, a.shape, mybir.dt.from_np(a.dtype), kind="ExternalInput").ap()
        args.append(ap.bitcast(BF16) if a.dtype == np.uint16 else ap)
    args.append(nc.dram_tensor("out_x", (NB, S, D), F32, kind="ExternalOutput").ap())
    build(nc, *args)
    r = run_bass_kernel_spmd(nc, [arrays], core_ids=[0])
    return r.results[0]["out_x"]
```

```python
from contextlib import ExitStack

import numpy as np

import concourse.bass as bass
from concourse import mybir

F32 = mybir.dt.float32
BF16 = mybir.dt.bfloat16
F32R = mybir.dt.float32r
ALU = mybir.AluOpType
ACT = mybir.ActivationFunctionType
AX_X = mybir.AxisListType.X

P = 128
D = 128
NB, S = 2, 1024
NT = NB * S // P
QUAD = 4
NQ = NT // QUAD
QN = QUAD * P
H, DH = 16, 8
G, HG = 4, 4
NS = NB * G
KB = S // P
SEG, KSEG = 128, 64
PARTS = 3
ROWS = PARTS * PARTS * DH
BIAS_ROW = ROWS
N_BIAS = 6
MAX_ROW = 96
K_MAX = 96
K_EXP = 98
RING = 4
LEAD = 4
STEPS = KB * HG
E = 16
EPS = 1e-5
W3 = 3 * D
K_STORES = (1, PARTS)
WC, NWC = 1024, 8
YR = 4


def build(nc, x, wq, wk, wv, wo, w_re, w_im, bias, w_qkv, w_out, sim, gates, p_q, p_k, p_v, p_o,
          ident, c_cos, c_sin, c_nsin, slopes, kpos, rank, out):
    scale = float(DH) ** -0.5
    scale_moe = float(D) ** -0.5
    dq = [nc.dram_tensor(f"q_parts_{n}", [PARTS * DH, NB * H, S], BF16).ap() for n in range(2)]
    dk = [nc.dram_tensor("k_parts_0", [PARTS, NS * DH, S], BF16).ap(),
          nc.dram_tensor("k_parts_1", [PARTS * DH, NB * H, S // 2], BF16).ap()]

    with ExitStack() as ctx:
        def sb(name, shape, dt=F32, over=ctx):
            return over.enter_context(nc.sbuf_tensor(name, shape, dt))

        def sem(name):
            return ctx.enter_context(nc.semaphore(name))

        ident_sb = sb("ident_sb", [P, P])
        ones = sb("ones", [P, P])
        cos_sb, sin_sb, nsin_sb = sb("cos_sb", [P, P]), sb("sin_sb", [P, P]), sb("nsin_sb", [P, P])
        w_qkv0 = sb("w_qkv0", [P, 3, P])
        wo_sb = sb("wo_sb", [P, P])
        wre_sb, wim_sb = sb("wre_sb", [P, P]), sb("wim_sb", [P, P])
        a_re, a_im, m_sb = sb("a_re", [P, P]), sb("a_im", [P, P]), sb("m_sb", [P, P])
        bias_sb = sb("bias_sb", [P, P])
        w_qkv1 = sb("w_qkv1", [P, W3])
        wout_sb = sb("wout_sb", [P, P])
        sim_sb, sim_n = sb("sim_sb", [P, E]), sb("sim_n", [P, E])
        gate_sb = sb("gate_sb", [P, E])
        rank_sb = sb("rank_sb", [P, E])
        half = sb("half", [P, NT])
        phalf = sb("phalf", [P, NT])
        xa = sb("xa", [P, NT, D])
        xb = sb("xb", [P, NT, D])
        xT = sb("xT", [P, NT * P])
        v_cur = sb("v_cur", [P, KB * 32])
        probs = sb("probs", [P, 2, HG * S])
        o_seg = probs[:, 1, :]
        mx2 = sb("mx2", [P, 2 * STEPS])
        mx = sb("mx", [P, STEPS])
        mrow = sb("mrow", [STEPS, 2, P], BF16)
        attT = sb("attT", [P, 2, QN])
        rec = sb("rec", [P, 2, H])
        st = sb("st", [P, NQ, QUAD, 6])
        mv = sb("mv", [P, NQ, QUAD, 2])
        ve, rstd, nb = sb("ve", [P, NQ, QUAD]), sb("rstd", [P, NQ, QUAD]), sb("nb", [P, NQ, QUAD])
        tick = sb("tick", [P, 8])

        psum = [ctx.enter_context(nc.psum_tensor(n, [P, w], F32))
                for n, w in (("ps_max", 2 * QN), ("ps_s", 4 * QN), ("ps_o", 2 * QN))]
        ps_max, ps_s, ps_o = psum

        def bank(n, count=1):
            t, at = ((ps_max, n), (ps_s, n - 2), (ps_o, n - 6))[0 if n < 2 else 1 if n < 6 else 2]
            return t[:, at * QN:(at + count) * QN]

        rt = [sb(f"rt{n}", [P, NT, E]) for n in range(6)]
        r1 = [sb(f"r1_{n}", [P, NT]) for n in range(4)]
        w_rt = sb("w_rt", [P, NT, E])

        attentions = ExitStack()
        q_rep = sb("q_rep", [P, RING * HG * S], BF16, attentions)
        k_rep0 = sb("k_rep0", [P, RING * S], BF16, attentions)
        k_rep1 = sb("k_rep1", [P, RING * HG * S // 2], BF16, attentions)
        v_blk = sb("v_blk", [P, NT * 8 * 32], F32, attentions)
        v_all = v_blk[:, 0:NS * KB * 32]
        qk = sb("qk", [P, QN + QN // 2], F32, attentions)
        qk_r = sb("qk_r", [P, 2 * QN], F32, attentions)
        qk_p = sb("qk_p", [P, 2, PARTS, 2 * QN], BF16, attentions)
        big = sb("big", [P, NS * S], F32, attentions)
        attentions.close()
        w_hi = sb("w_hi", [P, E * (W3 + D)], F32R)
        w_lo = sb("w_lo", [P, E * (W3 + D)], F32R)
        op_hi = sb("op_hi", [P, 2, 2, P], F32R)
        op_lo = sb("op_lo", [P, 2, 2, P], F32R)
        v_tok = sb("v_tok", [P, NT * D])
        tok_cur = sb("tok_cur", [P, 2, 2, W3])
        q_hi, q_lo = sb("q_hi", [P, 2, P], F32R), sb("q_lo", [P, 2, P], F32R)
        w_cur = sb("w_cur", [P, QUAD, E])
        m_cur = sb("m_cur", [P, 2, 3])
        y_out = sb("y_out", [P, 2, QUAD, D])
        w_act = sb("w_act", [P, 2, 2, E])
        r_sum = sb("r_sum", [P, NT])
        kT_hi, kT_lo = sb("kT_hi", [P, NT * P], F32R), sb("kT_lo", [P, NT * P], F32R)
        f_p = probs[:].rearrange("p a b -> p (a b)")
        qT_all = f_p[:, 0:2048]
        kT_all = f_p[:, 2048:4096]
        p_cur = f_p[:, 4096:6144].rearrange("p (u n) -> p u n", u=2)
        pT_cur = f_p[:, 6144:8192].rearrange("p (u n) -> p u n", u=2)
        oT_all = xT
        z_first = f_p[:, 0:2048].rearrange("p (a u n) -> p a u n", a=2, u=2)
        y_acc = f_p[:, 2048:3072].rearrange("p (v t n) -> p v t n", v=2, t=QUAD)

        ld_dft = sem("ld_dft")
        ld_x = [sem(f"ld_x{n}") for n in range(NQ)]
        ld_c, ld_w1, ld_bias, ld_we = (sem(n) for n in ("ld_c", "ld_w1", "ld_bias", "ld_we"))
        const_set = sem("const_set")
        rows_set = sem("rows_set")
        wq_scaled = sem("wq_scaled")
        dft_a, dft_a_sb, dft_m, dft_m_sb = sem("dft_a"), sem("dft_a_sb"), sem("dft_m"), sem("dft_m_sb")
        dve_step = sem("dve_step")
        xT_ps = [sem(f"xT_ps{n}") for n in range(2)]
        xT_sb = [sem(f"xT_sb{n}") for n in range(2)]
        qk_ps = [sem(f"qk_ps{n}") for n in range(2)]
        qk_hi, qk_rest, qk_mid = sem("qk_hi"), sem("qk_rest"), sem("qk_mid")
        qk_split = [sem(f"qk_split{n}") for n in range(2)]
        part_set = [[qk_hi, qk_mid, qk_split[0]], [sem("part1_hi"), sem("part1_mid"), qk_split[1]]]
        q_out = [[sem(f"q_out{n}_{odd}") for odd in range(2)] for n in range(2)]
        k_out = [[sem(f"k_out{n}_{odd}") for odd in range(2)] for n in range(2)]
        v_ps = [sem(f"v_ps{n}") for n in range(2)]
        v_sb = [sem(f"v_sb{n}") for n in range(2)]
        rep_loaded = sem("rep_loaded")
        max_ps = [sem(f"max_ps{n}") for n in range(2)]
        max_done = [sem(f"max_done{n}") for n in range(2)]
        max_all = [sem(f"max_all{n}") for n in range(2)]
        mrow_set = [sem(f"mrow_set{n}") for n in range(2)]
        mrow_in = [sem(f"mrow_in{n}") for n in range(2)]
        s_ps = [sem(f"s_ps{n}") for n in range(2)]
        s_free = [sem(f"s_free{n}") for n in range(2)]
        p_free = [sem(f"p_free{n}") for n in range(2)]
        v_cur_set = sem("v_cur_set")
        o_free = [sem(f"o_free{n}") for n in range(2)]
        ot_ps = [sem(f"ot_ps{n}") for n in range(2)]
        ot_read = [sem(f"ot_read{n}") for n in range(2)]
        at_ps = [sem(f"at_ps{n}") for n in range(2)]
        at_sb = [sem(f"at_sb{n}") for n in range(2)]
        wo_ps = [sem(f"wo_ps{n}") for n in range(2)]
        ln_var = [sem(f"ln_var{n}") for n in range(3)]
        ln_std = [sem(f"ln_std{n}") for n in range(3)]
        ln_nb = [sem(f"ln_nb{n}") for n in range(3)]
        ln_out = [sem(f"ln_out{n}") for n in range(3)]
        ft_ps, ft_sb, fm_ps = sem("ft_ps"), sem("ft_sb"), sem("fm_ps")
        xsel_set, ksel_sb, qk_read = sem("xsel_set"), sem("ksel_sb"), sem("qk_read")
        rep1_in = [sem(f"rep1_in{n}") for n in range(RING)]
        x3T_ps, x3T_sb = sem("x3T_ps"), sem("x3T_sb")
        sim_sq, sim_ss, sim_root, sim_root_done, sim_ready = (
            sem(n) for n in ("sim_sq", "sim_ss", "sim_root", "sim_root_done", "sim_ready"))
        lg_ps, gate_exp, nrm_root = sem("lg_ps"), sem("gate_exp"), sem("nrm_root")
        nrm_ss = [sem(f"nrm_ss{n}") for n in range(2)]
        ex_in, ex_out, w_ready = sem("ex_in"), sem("ex_out"), sem("w_ready")
        tok_first = sem("tok_first")
        w_div, z0_ps, z0_sb, y0_set, w_act_set, y0_step = (
            sem(n) for n in ("w_div", "z0_ps", "z0_sb", "y0_set", "w_act_set", "y0_step"))
        w_hi_set, w_lo_set, op_hi_set = sem("w_hi_set"), sem("w_lo_set"), sem("op_hi_set")
        xc_set, y_ps, y_free, tok_set, kq_ps, kq_sb = (
            sem(n) for n in ("xc_set", "y_ps", "y_free", "tok_set", "kq_ps", "kq_sb"))
        v_set, acc_step, fin_step = sem("v_set"), sem("acc_step"), sem("fin_step")
        pool_step = sem("pool_step")
        q_hi_set, k_lo_set = sem("q_hi_set"), sem("k_lo_set")
        q_set, sc_ps, nmax_set, p_set, pt_ps, pt_sb, o_ps, o_sb = (
            sem(n) for n in ("q_set", "sc_ps", "nmax_set", "p_set", "pt_ps", "pt_sb", "o_ps", "o_sb"))
        fin_root = sem("fin_root")
        z_ps, w_set, fin_var, fin_std, fin_set = (
            sem(n) for n in ("z_ps", "w_set", "fin_var", "fin_std", "fin_set"))
        stored = [sem(f"stored{n}") for n in range(2)]

        out_t = out.rearrange("b (t p) d -> p (b t) d", p=P)

        words = mybir.dt.uint32
        two_ones = 0x3F803F80

        def max_bank(s, k, i):
            return bank(2 * (k % 3) + i if isinstance(s, int) and s == 0 else i)

        def heads_bank(layer, t):
            return bank(t % 2 if layer == 0 and t < KB else t % 8)

        def heads_reader(layer, t):
            if layer == 0 and t < KB + 2:
                return max(t - 1, 0)
            return max(t - 7, 0)

        def res_bank(n, q):
            return bank(q if n == 1 else 4 + q)

        def qkv_banks(q):
            return bank(4, 2) if q % 2 == 0 else bank(0, 2)

        def kept(ap, units):
            return bass.AP(ap.tensor, ap.offset, [list(ap.ap[0]), [2 * 32, units], [32 + 1, 2], [2, 16]])

        def parts_stored(engine, layer, q):
            engine.wait_ge(q_out[layer][q % 2], q // 2 * PARTS * 16)
            engine.wait_ge(k_out[layer][q % 2], q // 2 * K_STORES[layer] * 16)

        block = ctx.enter_context(nc.Block())

        @block.sync
        def _(sp):
            xv = x.rearrange("b (t p) d -> p (b t) d", p=P)
            for q in range(NQ):
                sp.dma_start(xa[:, q * QUAD:(q + 1) * QUAD, :], xv[:, q * QUAD:(q + 1) * QUAD, :]).then_inc(ld_x[q], 16)
                if q == 0:
                    sp.dma_start(ident_sb[:], ident).then_inc(ld_c, 16)
                    sp.dma_start(w_qkv0[:, 0, :], wq).then_inc(ld_c, 16)
                    sp.dma_start(w_qkv0[:, 1, :].rearrange("p (r n) -> p r n", r=HG),
                                 wk.unsqueeze(1).broadcast_to([P, HG, G * DH])).then_inc(ld_c, 16)
                    sp.dma_start(w_qkv0[:, 2, 0:G * DH], wv).then_inc(ld_c, 16)
            for dst, src in ((cos_sb, c_cos), (sin_sb, c_sin), (nsin_sb, c_nsin), (wre_sb, w_re), (wim_sb, w_im)):
                sp.dma_start(dst[:], src).then_inc(ld_dft, 16)
            sp.wait_ge(rows_set, 1)
            sp.wait_ge(const_set, 5)
            sp.dma_start(q_rep[BIAS_ROW:BIAS_ROW + N_BIAS, :], slopes).then_inc(rep_loaded, 16)
            sp.dma_start(k_rep0[BIAS_ROW:BIAS_ROW + N_BIAS, :].rearrange("p (r n) -> p r n", r=RING),
                         kpos.unsqueeze(1).broadcast_to([N_BIAS, RING, S])).then_inc(rep_loaded, 16)

            def loaded(s):
                return (s * (1 + PARTS) + 2) * 16

            def store_q(layer, q):
                b, c0 = q // 2, (q % 2) * QN
                for i in range(PARTS):
                    sp.wait_ge(part_set[layer][i], q + 1)
                    sp.dma_start(dq[layer][i * DH:(i + 1) * DH, b * H:(b + 1) * H, c0:c0 + QN]
                                 .rearrange("d h n -> h d n"),
                                 qk_p[:, q % 2, i, 0:QN]).then_inc(q_out[layer][q % 2], 16)

            def stored_parts(layer, b):
                for odd in range(2):
                    sp.wait_ge(q_out[layer][odd], (b + 1) * PARTS * 16)
                    sp.wait_ge(k_out[layer][odd], (b + 1) * K_STORES[layer] * 16)

            def load_rep(layer, s):
                slot, n = s % RING, S * (1 if layer == 0 else HG // 2)
                k_rep = k_rep0 if layer == 0 else k_rep1
                into = rep_loaded if layer == 0 else rep1_in[slot]
                sp.dma_start(q_rep[0:ROWS, bass.ds(slot * HG * S, HG * S)],
                             dq[layer][:, bass.ds(s * HG, HG)].rearrange("r h n -> r (h n)").unsqueeze(0).broadcast_to(
                                 [PARTS, PARTS * DH, HG * S])).then_inc(into, 16)
                for j in range(PARTS):
                    r0 = j * PARTS * DH
                    if layer == 0:
                        part = dk[0][j, bass.ds(s * DH, DH)]
                    else:
                        part = dk[1][j * DH:(j + 1) * DH, s * HG:(s + 1) * HG].rearrange("d h n -> d (h n)")
                    sp.dma_start(k_rep[r0:r0 + PARTS * DH, bass.ds(slot * n, n)],
                                 part.unsqueeze(0).broadcast_to([PARTS, DH, n])).then_inc(into, 16)

            def load_mrow(layer, s):
                at = (s % RING) * (HG * S)
                at = at if isinstance(s, int) else sp.snap(at)
                sp.wait_ge(mrow_set[layer], s + 1)
                for part in range(2):
                    dst = q_rep[MAX_ROW + part:MAX_ROW + part + 1, bass.ds(at, HG * S)]
                    sp.dma_start(dst.rearrange("o (r n) -> o r n", n=P), mrow[:, part, :]).then_inc(mrow_in[layer], 16)

            for q in range(2):
                store_q(0, q)
            stored_parts(0, 0)
            load_rep(0, 0)
            for q in range(2, NQ):
                store_q(0, q)
            for s in range(1, RING):
                sp.wait_ge(rep_loaded, loaded(s))
                load_rep(0, s)
            for dst, src in ((wo_sb, wo), (w_qkv1, w_qkv), (wout_sb, w_out), (sim_sb, sim), (rank_sb, rank)):
                sp.dma_start(dst[:], src).then_inc(ld_w1, 16)
            sp.dma_start(bias_sb[:], bias.unsqueeze(0).broadcast_to([P, D])).then_inc(ld_bias, 16)
            sp.dma_start(gate_sb[:], gates.unsqueeze(0).broadcast_to([P, E])).then_inc(ld_bias, 16)
            stored_parts(0, 1)
            load_mrow(0, 0)
            with sp.Fori(0, NS - RING) as s:
                load_mrow(0, s + 1)
                sp.wait_ge(s_ps[0], STEPS * (s + 1))
                sp.wait_ge(rep_loaded, loaded(s + RING))
                load_rep(0, s + RING)
            with sp.Fori(NS - RING, NS - 1) as s:
                load_mrow(0, s + 1)
            sp.wait_ge(ot_ps[0], NT)
            for n, p in enumerate((p_q, p_k, p_v)):
                sp.dma_start(big[:, 0:E * W3].rearrange("p (e n) -> p e n", e=E)[:, :, n * D:(n + 1) * D],
                             p.rearrange("e c h -> c e h")).then_inc(ld_we, 16)
            sp.dma_start(big[:, E * W3:].rearrange("p (e n) -> p e n", e=E),
                         p_o.rearrange("e c h -> c e h")).then_inc(ld_we, 16)
            for q in range(2):
                store_q(1, q)
            stored_parts(1, 0)
            sp.wait_ge(const_set, 9)
            sp.wait_ge(s_ps[0], NS * STEPS)
            for s in range(2):
                load_rep(1, s)
            for q in range(2, NQ):
                store_q(1, q)
            load_mrow(1, 0)
            for s in range(2, RING):
                load_rep(1, s)
            load_mrow(1, 1)
            stored_parts(1, 1)
            for s in range(NS - RING):
                sp.wait_ge(s_ps[1], 2 * (s + 1))
                load_rep(1, s + RING)
                load_mrow(1, s + 2)
            for s in range(NS - RING + 2, NS):
                load_mrow(1, s)
            with sp.Fori(0, NQ // 2) as i:
                for u in range(2):
                    q = 2 * i + u
                    at = sp.snap(q * QUAD)
                    sp.wait_ge(fin_set, q + 3)
                    sp.dma_start(out_t[:, bass.ds(at, QUAD), :], y_out[:, u]).then_inc(stored[u], 16)
            for u in range(2):
                sp.wait_ge(stored[u], 16 * (NQ // 2 + 1))

        @block.gpsimd
        def _(pool):
            steps = [0]

            def fill(ap, value):
                pool.memset(ap, value).then_inc(const_set, 1)
                steps[0] += 1
                pool.wait_ge(const_set, steps[0])

            fill(ones[:], 1.0)
            fill(v_all, 0.0)
            fill(v_all.rearrange("p (n c) -> p n c", c=32)[:, :, DH:DH + 1], 1.0)
            fill(k_rep0[64:MAX_ROW, :].bitcast(words), 0)
            fill(k_rep0[MAX_ROW:P, :].bitcast(words), two_ones)
            fill(half[:], -0.5)
            fill(phalf[:], 0.5)

            def store_k(layer, q):
                b, n = q // 2, QN // (1 + layer)
                c0 = (q % 2) * n
                if layer == 0:
                    pool.wait_ge(qk_split[0], q + 1)
                    pool.dma_start(dk[0][:, b * G * DH:(b + 1) * G * DH, c0:c0 + n].rearrange("j r n -> r j n"),
                                   qk_p[0:G * DH, q % 2, :, QN:QN + n]).then_inc(k_out[0][q % 2], 16)
                    return
                for j in range(PARTS):
                    pool.wait_ge(part_set[1][j], q + 1)
                    pool.dma_start(dk[1][j * DH:(j + 1) * DH, b * H:(b + 1) * H, c0:c0 + n]
                                   .rearrange("d h n -> h d n"),
                                   qk_p[:, q % 2, j, QN:QN + n]).then_inc(k_out[1][q % 2], 16)

            def root(n, q):
                pool.wait_ge(ln_var[n], q + 1)
                pool.tensor_tensor(rstd[:, q, :], ve[:, q, :], half[:, 0:QUAD], ALU.pow).then_inc(ln_std[n], 1)

            for q in range(NQ):
                store_k(0, q)
            fill(k_rep1[64:MAX_ROW, :].bitcast(words), 0)
            fill(k_rep1[MAX_ROW:P, :].bitcast(words), two_ones)
            with pool.Fori(0, NS) as s:
                pool.wait_ge(p_free[0], KB * s + 2)
                pool.tensor_copy(v_cur[:], v_all[:, bass.ds(s * KB * 32, KB * 32)]).then_inc(v_cur_set, 1)
            pool.wait_ge(p_free[0], KB * NS + 2)
            pool.wait_ge(v_cur_set, NS)
            vb = v_blk.rearrange("p (n c) -> p n c", c=32)
            fill(v_blk[:], 0.0)
            fill(vb[0:KSEG, :, DH:DH + 1], 1.0)
            fill(vb[KSEG:P, :, 16 + DH:16 + DH + 1], 1.0)
            for n in range(2):
                for q in range(NQ):
                    root(n, q)
            for q in range(NQ):
                store_k(1, q)
            def second_parts(first, last):
                for n in range(first, last):
                    at = slice(n * WC, (n + 1) * WC)
                    pool.wait_ge(w_hi_set, n + 1)
                    pool.tensor_tensor(w_lo[:, at], big[:, at], w_hi[:, at].bitcast(F32), ALU.subtract).then_inc(
                        w_lo_set, 1)

            pool.wait_ge(sim_root, 1)
            pool.tensor_tensor(sim_n[:], sim_n[:], phalf[:, 0:E], ALU.pow).then_inc(sim_root_done, 1)
            second_parts(0, NWC // 2)
            for q in range(NQ):
                root(2, q)
            second_parts(NWC // 2, 3 * NWC // 4)
            for b in range(NB):
                tiles = slice(b * KB, (b + 1) * KB)
                pool.wait_ge(nrm_ss[b], NQ // NB)
                pool.tensor_tensor(r1[0][:, tiles], r1[0][:, tiles], phalf[:, tiles], ALU.pow).then_inc(nrm_root, 1)
            second_parts(3 * NWC // 4, NWC)

            def op_second(t, a, u):
                pool.tensor_tensor(op_lo[:, a, u, :], xT[:, bass.ds(t * P, P)], op_hi[:, a, u, :].bitcast(F32),
                                   ALU.subtract).then_inc(xc_set, 1)

            def keep_v(t, a, u):
                pool.wait_ge(tok_set, t + 1)
                pool.tensor_copy(v_tok[:, bass.ds(t * D, D)], tok_cur[:, a, u, 2 * D:W3]).then_inc(v_set, 1)

            for t in range(QUAD):
                pool.wait_ge(op_hi_set, t + 1)
                op_second(t, t // 2, t % 2)

            def k_second(t):
                pool.wait_ge(kq_sb, t + 4 + 1)
                pool.sem_inc(pool_step, 1)
                at = bass.ds(t * P, P)
                pool.tensor_tensor(kT_lo[:, at], kT_all[:, at], kT_hi[:, at].bitcast(F32), ALU.subtract).then_inc(
                    k_lo_set, 1)

            def q_second(t, u):
                pool.wait_ge(q_hi_set, t + 1)
                pool.sem_inc(pool_step, 1)
                pool.tensor_tensor(q_lo[:, u, :], qT_all[:, bass.ds(t * P, P)], q_hi[:, u, :].bitcast(F32),
                                   ALU.subtract).then_inc(q_set, 1)

            def expert_quad(i, first, end):
                for a in range(2):
                    pair = 2 * i + a
                    for u in range(2):
                        if not (first and a == 0):
                            k_second(2 * pair - 2 + u)
                    for u in range(2):
                        if end and a == 1:
                            q_second(u, u)
                    for u in range(2):
                        t = 2 * pair + u
                        pool.wait_ge(op_hi_set, t + QUAD + 1)
                        op_second((t + QUAD) % NT, a, u)
                    for u in range(2):
                        keep_v(2 * pair + u, a, u)

            expert_quad(0, True, False)
            with pool.Fori(1, NQ - 1) as i:
                expert_quad(i, False, False)
            expert_quad(NQ - 1, False, True)
            for u in range(2):
                k_second(NT - 2 + u)
            with pool.Fori(0, NT // 2 - 1) as i:
                for u in range(2):
                    t = 2 * i + u + 2
                    pool.wait_ge(sc_ps, t - 1)
                    pool.tensor_copy(q_hi[:, u, :], qT_all[:, bass.ds(t * P, P)]).then_inc(q_hi_set, 1)
                    q_second(t, u)
            done = NT + QUAD
            for t in range(QUAD):
                pool.wait_ge(op_hi_set, done + t + 1)
                op_second(t, t // 2, t % 2)

            def first_sum(pair, a, u, q, v):
                z, y = z_first[:, a, u], y_acc[:, v, 2 * a + u, :]
                n = 2 * pair + u
                pool.wait_ge(z0_sb, n + 5)
                pool.tensor_tensor(z[:, 0:2 * D], z[:, 0:2 * D], z[:, 2 * D:4 * D], ALU.add).then_inc(y0_step, 1)
                pool.wait_ge(y0_step, 2 * n + 1)
                pool.wait_ge(fin_set, q + 1)
                pool.tensor_tensor(y, z[:, 0:D], z[:, D:2 * D], ALU.add).then_inc(y0_step, 1)
                pool.wait_ge(y0_step, 2 * n + 2)
                pool.tensor_tensor(y, y, xb[:].rearrange("p t d -> p (t d)")[:, bass.ds(n * D, D)], ALU.add)\
                    .then_inc(y0_set, 1)

            def sums_quad(q, v, end):
                for a in range(2):
                    pair = 2 * q + a
                    if not (end and a == 1):
                        for u in range(2):
                            first_sum(pair + 1, 1 - a, u, q + a, (v + a) % 2)
                    for u in range(2):
                        t = 2 * pair + u
                        pool.wait_ge(op_hi_set, done + t + QUAD + 1)
                        op_second((t + QUAD) % NT, a, u)
                pool.wait_ge(fin_var, 2 * q + 2)
                pool.wait_ge(fin_set, q + 1)
                pool.tensor_tensor(rstd[:, v, :], ve[:, v, :], half[:, 0:QUAD], ALU.pow).then_inc(fin_root, 1)
                pool.wait_ge(fin_root, q + 1)
                pool.tensor_tensor(nb[:, v, :], nb[:, 2 + v, :], rstd[:, v, :], ALU.mult).then_inc(fin_std, 1)

            for u in range(2):
                first_sum(0, 0, u, 0, 0)
            with pool.Fori(0, NQ // 2 - 1) as i:
                for v in range(2):
                    sums_quad(2 * i + v, v, False)
            for v in range(2):
                sums_quad(NQ - 2 + v, v, v == 1)

        @block.tensor
        def _(pe):
            def quad_transposes(src, q, dst):
                for t in range(QUAD):
                    mm = pe.transpose(dst[:, t * P:(t + 1) * P], src[:, q * QUAD + t, :], ident_sb[:])
                return mm

            pe.wait_ge(ld_c, 4 * 16)
            def x_T(q):
                pe.wait_ge(ld_x[q], 16)
                if q >= 2:
                    pe.wait_ge(xT_sb[0], q - 1)
                quad_transposes(xa, q, bank(q % 2)).then_inc(xT_ps[0], 1)

            x_T(0)
            x_T(1)
            pe.wait_ge(wq_scaled, 1)
            for q in range(NQ):
                pe.wait_ge(xT_sb[0], q + 1)
                if q >= 2:
                    pe.wait_ge(qk_rest, q - 1)
                xq = xT[:, q * QN:(q + 1) * QN]
                pair = bank(2 + 2 * (q % 2), 2)
                pe.matmul(pair[:, 0:QN], w_qkv0[:, 0, :], xq, start=True, stop=True)
                pe.matmul(pair[:, QN:2 * QN], w_qkv0[:, 1, :], xq, start=True, stop=True).then_inc(qk_ps[0], 1)
                if q >= 2:
                    pe.wait_ge(v_sb[0], q - 1)
                for t in range(QUAD):
                    mm = pe.matmul(bank(6 + q % 2)[:, t * 32:(t + 1) * 32], xq[:, t * P:(t + 1) * P],
                                   w_qkv0[:, 2, 0:G * DH], start=True, stop=True)
                mm.then_inc(v_ps[0], 1)
                if q + 2 < NQ:
                    x_T(q + 2)
            pe.wait_ge(ld_dft, 5 * 16)
            pe.matmul(bank(0)[:, 0:P], wre_sb[:], cos_sb[:], start=True, stop=False)
            pe.matmul(bank(0)[:, 0:P], wim_sb[:], sin_sb[:], start=False, stop=True)
            pe.matmul(bank(1)[:, 0:P], wim_sb[:], cos_sb[:], start=True, stop=False)
            pe.matmul(bank(1)[:, 0:P], wre_sb[:], nsin_sb[:], start=False, stop=True).then_inc(dft_a, 1)
            pe.wait_ge(dft_a_sb, 2)
            pe.matmul(bank(0)[:, 0:P], a_re[:], cos_sb[:], start=True, stop=False)
            pe.matmul(bank(0)[:, 0:P], a_im[:], nsin_sb[:], start=False, stop=True).then_inc(dft_m, 1)

            def max_pair(s, k, only=None):
                h, qb = k // KB, k % KB
                slot = s % RING
                for i in (range(2) if only is None else [only]):
                    n = s * (2 * STEPS + 2) + 2 * k + i
                    if not isinstance(n, int) or n > 2 * STEPS:
                        pe.wait_ge(max_done[0], n - (2 * k + i > 0))
                    elif n >= 6 and i == 0:
                        pe.wait_ge(max_done[0], n - 4)
                    pe.matmul(max_bank(s, k, i), q_rep[0:K_MAX, bass.ds(slot * HG * S + h * S + qb * P, P)],
                              k_rep0[0:K_MAX, bass.ds(slot * S + i * QN, QN)],
                              start=True, stop=True).then_inc(max_ps[0], 1)

            def max_rows(s):
                pe.wait_ge(max_all[0], s + 1)
                pe.transpose(bank(0)[0:STEPS, 0:P], mx[:], ident_sb[:]).then_inc(max_ps[0], 2)

            def load_wait(s):
                pe.wait_ge(rep_loaded, (2 + (1 + PARTS) * (s + 1)) * 16)

            def stage(s, last, first=False):
                slot = s % RING
                pe.wait_ge(mrow_in[0], 32 * (s + 1))
                for kb in range(KB):
                    for h in range(HG):
                        k = kb * HG + h
                        ahead = None
                        if last < 2 and k < STEPS - LEAD:
                            ahead = (s + 1, k + LEAD)
                        elif last == 0:
                            ahead = (s + 2, k - STEPS + LEAD)
                        turn = last < 2 and k == STEPS - LEAD
                        for i in range(2):
                            if i == 0:
                                pe.wait_ge(s_free[0], s * STEPS + k + 1)
                            mm = pe.matmul(bank(2 + 2 * (k % 2) + i),
                                           k_rep0[0:K_EXP, bass.ds(slot * S + kb * P, P)],
                                           q_rep[0:K_EXP, bass.ds(slot * HG * S + h * S + i * QN, QN)],
                                           start=True, stop=True)
                            if i == 1:
                                mm.then_inc(s_ps[0], 1)
                                if kb > 0:
                                    out_quarter(s, kb - 1, h)
                                elif not first:
                                    out_quarter(s - 1, KB - 1, h)
                            if ahead and not turn:
                                max_pair(*ahead, only=i)
                        if turn:
                            max_rows(s + 1)
                            if last == 0:
                                load_wait(s + 2)
                                max_pair(*ahead)
                    if last == 2:
                        heads_tile(0, kb, heads_in_big)

            def out_quarter(s, kb, i):
                n = S // 4
                pe.wait_ge(s_free[0], s * STEPS + (kb + 1) * HG + 2)
                if kb == 0 and i == 0:
                    pe.wait_ge(v_cur_set, s + 1)
                    pe.wait_ge(o_free[0], s + 1)
                for h in range(HG):
                    mm = pe.matmul(bank(6, 2)[32 * h:32 * h + 32, i * n:(i + 1) * n], v_cur[:, kb * 32:(kb + 1) * 32],
                                   probs[:, kb % 2, h * S + i * n:h * S + (i + 1) * n],
                                   start=(kb == 0 and i % 2 == 0), stop=(kb == KB - 1 and i % 2 == 1),
                                   tile_position=(0, 32 * h))
                if i == 3:
                    mm.then_inc(p_free[0], 1)

            def heads_tile(layer, t, source):
                reader = heads_reader(layer, t)
                if reader:
                    pe.wait_ge(ot_read[layer], reader)
                for g in range(G):
                    mm = pe.transpose(heads_bank(layer, t)[:, g * P:(g + 1) * P], source(t, g), ident_sb[:])
                mm.then_inc(ot_ps[layer], 1)

            def heads_in_big(t, g):
                at = (t // KB * G + g) * S + (t % KB) * P
                return big[:, at:at + P]

            pe.wait_ge(dft_m_sb, 1)
            pe.wait_ge(qk_rest, NQ)
            pe.wait_ge(v_sb[0], NQ)
            load_wait(0)
            for k in range(STEPS):
                max_pair(0, k)
            max_rows(0)
            load_wait(1)
            for k in range(LEAD):
                max_pair(1, k)
            stage(0, 0, first=True)
            with pe.Fori(1, NS - 2) as s:
                stage(s, 0)
            stage(NS - 2, 1)
            stage(NS - 1, 2)
            for i in range(4):
                out_quarter(NS - 1, KB - 1, i)

            def add_rows(dst, rows, first=True):
                pe.matmul(dst, ident_sb[:], rows, start=first, stop=False)

            def quad_products(dst, a, w):
                for t in range(QUAD):
                    mm = pe.matmul(dst[:, t * P:(t + 1) * P], a[:, t * P:(t + 1) * P], w[:], start=False,
                                   stop=(t == QUAD - 1))
                return mm

            def project(layer, w):
                for q in range(NQ):
                    pe.wait_ge(ot_read[layer], min(NT, max(4 * q + 4, 9 + q)))
                    for t in range(QUAD):
                        mm = pe.transpose(bank(q)[:, t * P:(t + 1) * P], xT[:, (q * QUAD + t) * D:(q * QUAD + t + 1) * D],
                                          ident_sb[:])
                    mm.then_inc(at_ps[layer], 1)
                for q in range(NQ):
                    add_rows(bank(4 + q), xa[:, q * QUAD:(q + 1) * QUAD, :].rearrange("p t d -> p (t d)"))
                    pe.wait_ge(at_sb[layer], q + 1)
                    quad_products(bank(4 + q), attT[:, q % 2, :], w).then_inc(wo_ps[layer], 1)

            pe.wait_ge(o_free[0], NS + 1)
            pe.wait_ge(ld_w1, 5 * 16)
            pe.wait_ge(s_free[0], NS * STEPS + 2)
            for t in range(KB, NT):
                heads_tile(0, t, heads_in_big)
            project(0, wo_sb)
            def ffn_in(q):
                pe.wait_ge(ln_out[0], q + 1)
                quad_transposes(xb, q, bank(4 + q)).then_inc(ft_ps, 1)
                add_rows(bank(q), bias_rows)
                add_rows(bank(q), xb[:, q * QUAD:(q + 1) * QUAD, :].rearrange("p t d -> p (t d)"), first=False)

            def ffn_product(q):
                pe.wait_ge(ft_sb, q + 1)
                quad_products(bank(q), attT[:, q % 2, :], m_sb).then_inc(fm_ps, 1)

            pe.wait_ge(ld_bias, 32)
            bias_rows = bias_sb[:].unsqueeze(1).broadcast_to([P, QUAD, D])
            ffn_in(0)
            for q in range(1, NQ):
                ffn_in(q)
                ffn_product(q - 1)
            ffn_product(NQ - 1)
            def x2_T(q):
                pe.wait_ge(ln_out[1], q + 1)
                if q >= 2:
                    pe.wait_ge(v_sb[1], q - 1)
                quad_transposes(xa, q, bank(6 + q % 2)).then_inc(xT_ps[1], 1)

            def qk_products(q):
                pe.wait_ge(xT_sb[1], q + 1)
                if q >= 2:
                    pe.wait_ge(ksel_sb, q - 1)
                xq = xT[:, q * QN:(q + 1) * QN]
                pair = qkv_banks(q)
                pe.matmul(pair[:, 0:QN], w_qkv1[:, 0:D], xq, start=True, stop=True)
                pe.matmul(pair[:, QN:2 * QN], w_qkv1[:, D:2 * D], xq, start=True, stop=True).then_inc(qk_ps[1], 1)

            def v_products(q):
                pe.wait_ge(xsel_set, q + 1)
                for t in range(QUAD):
                    mm = pe.matmul(bank(6 + q % 2)[:, t * P:(t + 1) * P], attT[:, q % 2, t * P:(t + 1) * P],
                                   w_qkv1[:, 2 * D:W3], start=True, stop=True)
                mm.then_inc(v_ps[1], 1)

            x2_T(0)
            x2_T(1)
            for q in range(NQ):
                qk_products(q)
                if 1 <= q < NQ - 1:
                    x2_T(q + 1)
                v_products(q)

            def seg_max(s, h):
                slot = s % RING
                n = s * (HG + 2) + h
                if n >= 2:
                    pe.wait_ge(max_done[1], n - (h > 0))
                for g in range(KB):
                    mm = pe.matmul(bank(h % 2)[:, g * KSEG:(g + 1) * KSEG],
                                   q_rep[0:K_MAX, slot * HG * S + h * S + g * SEG:slot * HG * S + h * S + (g + 1) * SEG],
                                   k_rep1[0:K_MAX, (slot * HG + h) * S // 2 + g * KSEG:
                                          (slot * HG + h) * S // 2 + (g + 1) * KSEG], start=True, stop=True)
                mm.then_inc(max_ps[1], 1)

            def seg_rows(s):
                pe.wait_ge(max_all[1], s + 1)
                pe.transpose(bank(0)[0:STEPS, 0:P], mx[:], ident_sb[:]).then_inc(max_ps[1], 2)

            def seg_scores(s, f):
                slot = s % RING
                pe.wait_ge(mrow_in[1], 32 * (s + 1))
                if s:
                    pe.wait_ge(s_free[1], 2 * s - 1 + f)
                for g in range(4 * f, 4 * f + 4):
                    for h in range(HG):
                        c = (g % 4) * 2 * SEG + (h // 2) * SEG
                        mm = pe.matmul(bank(2 + 2 * f, 2)[KSEG * (h % 2):KSEG * (h % 2 + 1), c:c + SEG],
                                       k_rep1[0:K_EXP, (slot * HG + h) * S // 2 + g * KSEG:
                                              (slot * HG + h) * S // 2 + (g + 1) * KSEG],
                                       q_rep[0:K_EXP, slot * HG * S + h * S + g * SEG:
                                             slot * HG * S + h * S + (g + 1) * SEG],
                                       start=True, stop=True, tile_position=(0, KSEG * (h % 2)))
                mm.then_inc(s_ps[1], 1)

            def seg_out(s):
                b, g4 = s // G, s % G
                pe.wait_ge(s_free[1], 2 * s + 2)
                if s >= 2:
                    pe.wait_ge(o_free[1], s - 1)
                for g in range(KB):
                    for pr in range(2):
                        j = (g % 2) * 2 + pr
                        mm = pe.matmul(bank(6 + s % 2)[32 * j:32 * j + 32, (g // 2) * SEG:(g // 2 + 1) * SEG],
                                       vblk(b * KB + g, g4 * 2 + pr),
                                       probs[:, 0, (s % 2) * 2 * S + g * 2 * SEG + pr * SEG:
                                             (s % 2) * 2 * S + g * 2 * SEG + (pr + 1) * SEG],
                                       start=True, stop=True, tile_position=(0, 32 * j))
                mm.then_inc(p_free[1], 1)

            def vblk(g, pair):
                return v_blk[:, (g * 8 + pair) * 32:(g * 8 + pair + 1) * 32]

            def rep1_wait(s):
                pe.wait_ge(rep1_in[s % RING], (1 + PARTS) * 16 * (s // RING + 1))

            pe.wait_ge(v_sb[1], NQ)
            pe.wait_ge(ksel_sb, NQ)
            pe.wait_ge(sim_sq, 1)
            pe.matmul(bank(6)[:, 0:E], ones[:], rt[0][:, 0, :], start=True, stop=True).then_inc(sim_ss, 1)
            for s in range(2):
                rep1_wait(s)
                for h in range(HG):
                    seg_max(s, h)
                seg_rows(s)
            pe.wait_ge(sim_root, 1)
            for s in range(NS):
                more = s + 2 < NS
                seg_scores(s, 0)
                if more:
                    rep1_wait(s + 2)
                    seg_max(s + 2, 0)
                    seg_max(s + 2, 1)
                seg_scores(s, 1)
                if more:
                    seg_max(s + 2, 2)
                    seg_max(s + 2, 3)
                if s:
                    seg_out(s - 1)
                if more:
                    seg_rows(s + 2)
            seg_out(NS - 1)

            def seg_heads(t, g):
                s = t // KB * G + g
                return o_seg[:, s * 512 + (t % KB // 2) * P:s * 512 + (t % KB // 2 + 1) * P]

            pe.wait_ge(o_free[1], NS)
            for t in range(NT):
                heads_tile(1, t, seg_heads)
            project(1, wout_sb)
            for q in range(NQ):
                pe.wait_ge(ln_out[2], q + 1)
                quad_transposes(xb, q, bank(q)).then_inc(x3T_ps, 1)
            pe.wait_ge(sim_ready, 1)
            for t in range(NT):
                if t % QUAD == 0:
                    pe.wait_ge(x3T_sb, t // QUAD + 1)
                mm = pe.matmul(bank(7)[:, t * E:(t + 1) * E], xT[:, t * P:(t + 1) * P], sim_n[:], start=True, stop=True)
            mm.then_inc(lg_ps, 1)

            pe.wait_ge(w_lo_set, NWC)

            def product(dst, a, u, at, n):
                hi, lo = op_hi[:, a, u, :], op_lo[:, a, u, :]
                pe.matmul(dst, hi, w_hi[:, at:at + n], start=True, stop=False)
                pe.matmul(dst, hi, w_lo[:, at:at + n], start=False, stop=False)
                return pe.matmul(dst, lo, w_hi[:, at:at + n], start=False, stop=True)

            def to_channels(pair, a):
                pe.wait_ge(tok_set, 2 * pair + 2)
                pe.wait_ge(kq_sb, 2 * pair + 2)
                for u in range(2):
                    for n in range(2):
                        mm = pe.transpose(bank(4 + a)[:, (2 * u + n) * P:(2 * u + n + 1) * P],
                                          tok_cur[:, a, u, n * P:(n + 1) * P], ident_sb[:])
                mm.then_inc(kq_ps, 2)

            D_ADDS = 2 * (E - 1)

            def expert_quad(i, first):
                for a in range(2):
                    pair = 2 * i + a
                    pe.wait_ge(xc_set, 2 * pair + 2)
                    for e in range(E):
                        for u in range(2):
                            if e < 2:
                                pe.wait_ge(y_free, D_ADDS * pair + 2 * (e + E - 3) + u + 1)
                            elif e == 2:
                                pe.wait_ge(tok_first, 2 * pair + u + 5)
                            else:
                                pe.wait_ge(y_free, D_ADDS * (pair + 1) + 2 * (e - 3) + u + 1)
                            product(bank((2 * e + u) % YR)[:, 0:W3], a, u, e * W3, W3).then_inc(y_ps, 1)
                        if e == 2 and not (first and a == 0):
                            to_channels(pair - 1, 1 - a)

            expert_quad(0, True)
            with pe.Fori(1, NQ) as i:
                expert_quad(i, False)
            def scores(t, u):
                pe.wait_ge(q_set, t + 1)
                pe.wait_ge(p_set, t + 1)
                for i in range(2):
                    at = bass.ds(t // KB * S + i * QN, QN)
                    pe.matmul(bank(2 * u + i), q_hi[:, u, :], kT_hi[:, at], start=True, stop=False)
                    pe.matmul(bank(2 * u + i), q_hi[:, u, :], kT_lo[:, at], start=False, stop=False)
                    mm = pe.matmul(bank(2 * u + i), q_lo[:, u, :], kT_hi[:, at], start=False, stop=True)
                mm.then_inc(sc_ps, 1)

            def probs_T(t, u):
                pe.wait_ge(p_set, t + 3)
                pe.wait_ge(pt_sb, 2 * t + 2)
                for kb in range(KB):
                    mm = pe.transpose(bank(4 + kb // 4)[:, (kb % 4) * P:(kb % 4 + 1) * P],
                                      p_cur[:, u, kb * P:(kb + 1) * P], ident_sb[:])
                mm.then_inc(pt_ps, 1)

            def outputs(t, u, b):
                pe.wait_ge(pt_sb, 2 * t + 4)
                pe.wait_ge(o_sb, t + 1)
                for kb in range(KB):
                    mm = pe.matmul(bank(6 + u)[:, 0:P], v_tok[:, (b * KB + kb) * D:(b * KB + kb + 1) * D],
                                   pT_cur[:, u, kb * P:(kb + 1) * P], start=(kb == 0), stop=(kb == KB - 1))
                mm.then_inc(o_ps, 1)

            pe.wait_ge(k_lo_set, KB)
            for u in range(2):
                pe.wait_ge(y_free, D_ADDS * (NT // 2 + 1) - 2 + 2 * u)
                scores(u, u)
            to_channels(NT // 2 - 1, 1)
            pe.wait_ge(kq_sb, NT + 4)
            probs_T(0, 0)
            pe.wait_ge(v_set, NT + 4)
            pe.wait_ge(k_lo_set, NT)
            for b in range(NB):
                with pe.Fori(b * KB // 2, (b + 1) * KB // 2 - b) as i:
                    for u in range(2):
                        t = 2 * i + u
                        scores(t + 2, u)
                        outputs(t, u, b)
                        probs_T(t + 1, 1 - u)
            outputs(NT - 2, 0, NB - 1)

            def group(pair, a, n):
                for u in range(2):
                    pe.wait_ge(acc_step, NT + 8 * (pair * 3 + n - 1))
                    product(bank((2 * (3 * a + n - 1) + u) % 4), a, u, E * W3 + n * 4 * D, 4 * D).then_inc(z_ps, 1)

            def first_group(pair, a):
                pe.wait_ge(xc_set, NT + QUAD + 2 * pair + 2)
                for u in range(2):
                    pe.wait_ge(z0_sb, 2 * pair + u + 1)
                    product(bank(4 + 2 * a + u), a, u, E * W3, 4 * D).then_inc(z0_ps, 1)

            def out_quad(q, begin, end):
                for a in range(2):
                    pair = 2 * q + a
                    if not (begin and a == 0):
                        group(pair, a, 1)
                    if not (end and a == 1):
                        first_group(pair + 1, 1 - a)
                    group(pair, a, 2)
                    group(pair, a, 3)

            pe.wait_ge(xc_set, NT + QUAD + 2)
            group(0, 0, 1)
            probs_T(NT - 1, 1)
            pe.wait_ge(pt_sb, 2 * NT + 2)
            first_group(0, 0)
            outputs(NT - 1, 1, NB - 1)
            pe.wait_ge(o_sb, NT + 2)
            out_quad(0, True, False)
            with pe.Fori(1, NQ - 1) as q:
                out_quad(q, False, False)
            out_quad(NQ - 1, False, True)

        @block.scalar
        def _(act):
            def copy(dst, src):
                return act.activation(dst, src, ACT.Copy)

            act.wait_ge(const_set, 1)
            act.activation(tick[:, 1:2], ones[:, 0:1], ACT.Exp).then_inc(s_free[0], 2)

            def x_copy(q):
                act.wait_ge(xT_ps[0], q + 1)
                copy(xT[:, q * QN:(q + 1) * QN], bank(q % 2)).then_inc(xT_sb[0], 1)

            x_copy(0)
            x_copy(1)
            for q in range(NQ):
                act.wait_ge(qk_ps[0], q + 1)
                if q >= 2:
                    parts_stored(act, 0, q)
                copy(qk_p[:, q % 2, 0, :], bank(2 + 2 * (q % 2), 2)).then_inc(qk_hi, 1)
                act.wait_ge(v_ps[0], q + 1)
                act.wait_ge(const_set, 3)
                va = v_all.rearrange("p (s k c) -> p s k c", s=NS, k=KB)
                b, k0 = q // 2, (q % 2) * QUAD
                copy(va[:, b * G:(b + 1) * G, k0:k0 + QUAD, 0:DH],
                     bank(6 + q % 2)[:, 0:QUAD * 32].rearrange("p (t g d) -> p g t d", t=QUAD, g=G)).then_inc(v_sb[0], 1)
                if q + 2 < NQ:
                    x_copy(q + 2)
                act.wait_ge(qk_rest, q + 1)
                copy(qk_p[:, q % 2, 1, :], qk_r[:]).then_inc(qk_mid, 1)

            def heads_out(s):
                act.wait_ge(p_free[0], (s + 1) * KB + 2)
                copy(big[:, bass.ds(s * S, S)], bank(6, 2)).then_inc(o_free[0], 1)

            def exps(s, first=False):
                for k in range(STEPS):
                    kb, h = k // HG, k % HG
                    act.wait_ge(s_ps[0], s * STEPS + k + 1)
                    if h == 0:
                        act.wait_ge(p_free[0], s * KB + kb + 1)
                    act.activation(probs[:, kb % 2, h * S:(h + 1) * S], bank(2 + 2 * (k % 2), 2),
                                   ACT.Exp).then_inc(s_free[0], 1)
                    if k == HG - 1 and not first:
                        heads_out(s - 1)

            exps(0, first=True)
            with act.Fori(1, NS) as s:
                exps(s)
            heads_out(NS - 1)

            def attT_copy(q, src, ps_sem, sb_sem, done_sem):
                act.wait_ge(ps_sem, q + 1)
                if q >= 2:
                    act.wait_ge(done_sem, q - 1)
                copy(attT[:, q % 2, :], src).then_inc(sb_sem, 1)

            def normalise(n, q, dst):
                act.wait_ge(ln_nb[n], q + 1)
                for t in range(QUAD):
                    ins = act.activation(dst[:, q * QUAD + t, :], res_bank(n, q)[:, t * D:(t + 1) * D], ACT.Identity,
                                         bias=nb[:, q, t:t + 1], scale=rstd[:, q, t:t + 1])
                ins.then_inc(ln_out[n], 1)

            def ft_copy(q):
                attT_copy(q, bank(4 + q), ft_ps, ft_sb, fm_ps)

            def x2_copy(q):
                act.wait_ge(xT_ps[1], q + 1)
                copy(xT[:, q * QN:(q + 1) * QN], bank(6 + q % 2)).then_inc(xT_sb[1], 1)

            def qkv1(q):
                act.wait_ge(qk_ps[1], q + 1)
                if q >= 1:
                    act.wait_ge(qk_read, q)
                pair = qkv_banks(q)
                act.activation(qk[:, 0:QN], pair[:, 0:QN], ACT.Copy, scale=scale)
                copy(qk[:, QN:QN + QN // 2].rearrange("p (r two i) -> p r two i", two=2, i=16),
                     kept(pair[:, QN:2 * QN], QN // 64)).then_inc(ksel_sb, 1)
                act.wait_ge(v_ps[1], q + 1)
                act.wait_ge(const_set, 12)
                vb = v_blk[:].rearrange("p (g r c) -> p g r c", g=NT, r=8)[:, q * QUAD:(q + 1) * QUAD]
                vp = bank(6 + q % 2).rearrange("p (g r two d) -> p g r two d", g=QUAD, r=8, two=2)
                copy(vb[0:KSEG, :, :, 0:DH], vp[0:KSEG, :, :, 0, :])
                copy(vb[KSEG:P, :, :, 16:16 + DH], vp[KSEG:P, :, :, 1, :]).then_inc(v_sb[1], 1)

            for q in range(NQ):
                attT_copy(q, bank(q), at_ps[0], at_sb[0], wo_ps[0])
            normalise(0, 0, xb)
            normalise(0, 1, xb)
            ft_copy(0)
            normalise(0, 2, xb)
            ft_copy(1)
            normalise(0, 3, xb)
            ft_copy(2)
            normalise(1, 0, xa)
            ft_copy(3)
            normalise(1, 1, xa)
            x2_copy(0)
            normalise(1, 2, xa)
            x2_copy(1)
            qkv1(0)
            normalise(1, 3, xa)
            x2_copy(2)
            qkv1(1)
            x2_copy(3)
            qkv1(2)
            qkv1(3)

            act.wait_ge(ld_bias, 32)
            act.activation(gate_sb[:], gate_sb[:], ACT.Exp, scale=-1.0).then_inc(gate_exp, 1)
            for s in range(NS):
                for f in range(2):
                    act.wait_ge(s_ps[1], 2 * s + f + 1)
                    if s >= 2 and f == 0:
                        act.wait_ge(p_free[1], s - 1)
                    act.activation(probs[:, 0, (s % 2) * 2 * S + f * S:(s % 2) * 2 * S + (f + 1) * S],
                                   bank(2 + 2 * f, 2), ACT.Exp).then_inc(s_free[1], 1)
            act.wait_ge(ld_we, 4 * 16)
            act.wait_ge(p_free[1], NS)
            for n in range(NWC):
                copy(w_hi[:, n * WC:(n + 1) * WC], big[:, n * WC:(n + 1) * WC]).then_inc(w_hi_set, 1)
            for q in range(NQ):
                attT_copy(q, bank(q), at_ps[1], at_sb[1], wo_ps[1])
            def x3_copy(q):
                act.wait_ge(x3T_ps, q + 1)
                copy(xT[:, q * QN:(q + 1) * QN], bank(q)).then_inc(x3T_sb, 1)

            normalise(2, 0, xb)
            for q in range(1, NQ):
                normalise(2, q, xb)
                x3_copy(q - 1)
            x3_copy(NQ - 1)
            act.wait_ge(ln_out[2], NQ)
            for t in range(NT - QUAD, NT):
                ins = act.activation(xa[:, t, :], xb[:, t, :], ACT.Square, accum_out=r1[0][:, t:t + 1])
            ins.then_inc(nrm_ss[1], 1)
            act.wait_ge(ex_in, 1)
            act.activation(rt[1][:], rt[1][:], ACT.Exp).then_inc(ex_out, 1)
            act.wait_ge(x3T_sb, NQ)
            for a in range(2):
                for u in range(2):
                    copy(op_hi[:, a, u, :], xT[:, (2 * a + u) * P:(2 * a + u + 1) * P]).then_inc(op_hi_set, 1)
            def weights_of(pair, a, count):
                copy(w_act[:, a].rearrange("p u e -> p (u e)"),
                     w_rt[:].rearrange("p t e -> p (t e)")[:, bass.ds(pair * 2 * E, 2 * E)]).then_inc(w_act_set, 1)
                act.wait_ge(w_act_set, count)

            def first_expert(pair, a):
                act.wait_ge(tok_first, 2 * pair + 2)
                weights_of(pair, a, pair + 1)
                act.wait_ge(kq_ps, 2 * pair + 2)
                for u in range(2):
                    act.wait_ge(v_set, 2 * pair + u + 1)
                    act.wait_ge(y_ps, 2 * E * pair + u + 1)
                    act.activation(tok_cur[:, a, u, :], bank(u)[:, 0:W3], ACT.Copy, scale=w_act[:, a, u, 0:1])\
                       .then_inc(tok_first, 1)

            def expert_quad(i, end):
                for a in range(2):
                    pair = 2 * i + a
                    act.wait_ge(y_ps, 2 * E * (pair + 1))
                    for u in range(2):
                        copy(op_hi[:, a, u, :], xT[:, bass.ds((2 * pair + 4 + u) % NT * P, P)])\
                            .then_inc(op_hi_set, 1)
                    if not (end and a == 1):
                        first_expert(pair + 1, 1 - a)
                    if not (end and a == 1):
                        kq_copies(pair, a)

            def kq_copies(pair, a):
                act.wait_ge(kq_ps, 2 * pair + 2 + 4)
                for u in range(2):
                    at = 2 * pair + u
                    copy(qT_all[:, bass.ds(at * P, P)], bank(4 + a)[:, 2 * u * P:(2 * u + 1) * P])
                    copy(kT_hi[:, bass.ds(at * P, P)], bank(4 + a)[:, (2 * u + 1) * P:(2 * u + 2) * P])
                    copy(kT_all[:, bass.ds(at * P, P)], bank(4 + a)[:, (2 * u + 1) * P:(2 * u + 2) * P])\
                        .then_inc(kq_sb, 1)

            for free, n in ((o_sb, 2), (p_set, 2), (pt_sb, 2), (pt_ps, 1), (o_ps, 2), (z0_sb, 4)):
                act.sem_inc(free, n)
            act.wait_ge(w_ready, 1)
            first_expert(0, 0)
            with act.Fori(0, NQ - 1) as i:
                expert_quad(i, False)
            act.wait_ge(kq_sb, 2 + 4)
            for u in range(2):
                copy(q_hi[:, u, :], qT_all[:, u * P:(u + 1) * P]).then_inc(q_hi_set, 1)
            expert_quad(NQ - 1, True)
            act.wait_ge(tok_first, NT + 4)


            def p_exp(t, u):
                act.wait_ge(nmax_set, t + 1)
                act.wait_ge(pt_ps, max(t, 1) if isinstance(t, int) else t)
                act.activation(p_cur[:, u, :], bank(2 * u, 2), ACT.Exp, bias=m_cur[:, u, 1:2], scale=scale_moe,
                               accum_out=m_cur[:, u, 2:3]).then_inc(p_set, 1)

            def pT_copy(t, u):
                act.wait_ge(pt_ps, t + 2)
                act.wait_ge(o_ps, t + 1)
                copy(pT_cur[:, u, 0:QN], bank(4)).then_inc(pt_sb, 1)

            def o_copy(t, u):
                act.wait_ge(o_ps, t + 3)
                copy(oT_all[:, bass.ds(t * P, P)], bank(6 + u)[:, 0:P]).then_inc(o_sb, 1)

            p_exp(0, 0)
            kq_copies(NT // 2 - 1, 1)
            p_exp(1, 1)
            pT_copy(0, 0)

            def attend(first, last):
                with act.Fori(first, last) as i:
                    for u in range(2):
                        t = 2 * i + u
                        o_copy(t, u)
                        pT_copy(t + 1, 1 - u)
                        p_exp(t + 2, u)

            attend(0, NT // 4)
            for a in range(2):
                for u in range(2):
                    copy(op_hi[:, a, u, :], oT_all[:, (2 * a + u) * P:(2 * a + u + 1) * P]).then_inc(op_hi_set, 1)
            attend(NT // 4, NT // 2 - 1)
            o_copy(NT - 2, 0)
            pT_copy(NT - 1, 1)

            def first_weighted(pair, a):
                act.wait_ge(z0_sb, 2 * pair + 4)
                weights_of(pair, a, NT // 2 + pair + 1)
                for u in range(2):
                    act.wait_ge(z0_ps, 2 * pair + u + 1)
                    act.wait_ge(y0_set, 2 * pair + u + 1)
                    for e in range(4):
                        ins = act.activation(z_first[:, a, u, e * D:(e + 1) * D],
                                             bank(4 + 2 * a + u)[:, e * D:(e + 1) * D], ACT.Copy,
                                             scale=w_act[:, a, u, e:e + 1])
                    ins.then_inc(z0_sb, 1)

            def out_quad(q):
                for a in range(2):
                    pair = 2 * q + a
                    if pair + 1 == NT // 4:
                        act.wait_ge(w_div, 2)
                    if pair + 1 < NT // 2:
                        first_weighted(pair + 1, 1 - a)
                    if a == 0 and q:
                        last_norm(q - 1)
                    act.wait_ge(z_ps, 6 * (pair + 1))
                    for u in range(2):
                        copy(op_hi[:, a, u, :], oT_all[:, bass.ds((2 * pair + 4 + u) % NT * P, P)])\
                            .then_inc(op_hi_set, 1)

            def last_norm(q):
                act.wait_ge(fin_std, q + 3)
                act.wait_ge(stored[q % 2], 16 * (q // 2 + 1))
                for t in range(QUAD):
                    ins = act.activation(y_out[:, q % 2, t, :], y_acc[:, q % 2, t, :], ACT.Identity,
                                         bias=nb[:, q % 2, t:t + 1], scale=rstd[:, q % 2, t:t + 1])
                ins.then_inc(fin_set, 1)

            act.wait_ge(w_div, 1)
            first_weighted(0, 0)
            o_copy(NT - 1, 1)
            act.wait_ge(o_sb, NT + 2)
            for q in range(NQ):
                out_quad(q)
            last_norm(NQ - 1)

        @block.vector
        def _(dve):
            steps = [0]

            def link(ins):
                steps[0] += 1
                ins.then_inc(dve_step, 1)
                dve.wait_ge(dve_step, steps[0])

            dve.memset(q_rep[64:P, :].bitcast(words), 0).then_inc(rows_set, 1)
            dve.wait_ge(ld_c, 4 * 16)
            dve.tensor_scalar(w_qkv0[:, 0, :], w_qkv0[:, 0, :], scale, None, ALU.mult).then_inc(wq_scaled, 1)

            for q in range(NQ):
                dve.wait_ge(qk_hi, q + 1)
                if q:
                    dve.wait_ge(qk_split[0], q)
                dve.tensor_tensor(qk_r[:], bank(2 + 2 * (q % 2), 2), qk_p[:, q % 2, 0, :], ALU.subtract).then_inc(
                    qk_rest, 1)
                dve.wait_ge(qk_mid, q + 1)
                if q >= 2:
                    parts_stored(dve, 0, q)
                dve.tensor_tensor(qk_p[:, q % 2, 2, :], qk_r[:], qk_p[:, q % 2, 1, :], ALU.subtract).then_inc(
                    qk_split[0], 1)

            def split(q, n):
                dve.wait_ge(ksel_sb, q + 1)
                if q >= 2:
                    parts_stored(dve, 1, q)
                parts = [qk_p[:, q % 2, i, 0:n] for i in range(PARTS)]
                link(dve.tensor_copy(parts[0], qk[:, 0:n]))
                dve.sem_inc(part_set[1][0], 1)
                link(dve.tensor_tensor(qk_r[:, 0:n], qk[:, 0:n], parts[0], ALU.subtract))
                dve.sem_inc(qk_read, 1)
                link(dve.tensor_copy(parts[1], qk_r[:, 0:n]))
                dve.sem_inc(part_set[1][1], 1)
                dve.tensor_tensor(parts[2], qk_r[:, 0:n], parts[1], ALU.subtract).then_inc(qk_split[1], 1)

            dve.wait_ge(dft_a, 1)
            dve.tensor_scalar(a_re[:], bank(0)[:, 0:P], 1.0 / D, None, ALU.mult).then_inc(dft_a_sb, 1)
            dve.tensor_scalar(a_im[:], bank(1)[:, 0:P], 1.0 / D, None, ALU.mult).then_inc(dft_a_sb, 1)
            dve.wait_ge(dft_m, 1)
            dve.tensor_copy(m_sb[:], bank(0)[:, 0:P]).then_inc(dft_m_sb, 1)
            dve.sem_inc(p_free[0], 2)
            dve.memset(tick[:, 3:4], 0.0).then_inc(o_free[0], 1)

            def max_pair(s, k):
                for i in range(2):
                    n = s * (2 * STEPS + 2) + 2 * k + i
                    dve.wait_ge(max_ps[0], n + 1)
                    dve.reduce_max(mx2[:, 2 * k + i:2 * k + i + 1], bank(i), AX_X).then_inc(max_done[0], 1)

            def max_rows(s):
                n = s * (2 * STEPS + 2) + 2 * STEPS
                dve.wait_ge(max_done[0], n)
                if not isinstance(s, int):
                    dve.wait_ge(mrow_in[0], 32 * s)
                if isinstance(s, int) and s == 0:
                    dve.sem_inc(max_all[0], 1)
                else:
                    dve.reduce_max(mx[:], mx2[:].rearrange("p (k i) -> p k i", i=2), AX_X).then_inc(max_all[0], 1)
                dve.wait_ge(max_ps[0], n + 2)
                dve.tensor_scalar(mrow[:, 0, :], bank(0)[0:STEPS, 0:P], -1.0, None, ALU.mult).then_inc(max_done[0], 1)
                dve.wait_ge(max_done[0], n + 1)
                dve.scalar_tensor_tensor(out=mrow[:, 1, :], in0=bank(0)[0:STEPS, 0:P], scalar=-1.0, in1=mrow[:, 0, :],
                                         op0=ALU.mult, op1=ALU.subtract).then_inc(max_done[0], 1)
                dve.wait_ge(max_done[0], n + 2)
                dve.sem_inc(mrow_set[0], 1)

            for k in range(STEPS):
                dve.wait_ge(max_ps[0], 2 * k + 2)
                dve.reduce_max(mx[:, k:k + 1], bank(2 * (k % 3), 2), AX_X).then_inc(max_done[0], 2)
            max_rows(0)
            for k in range(LEAD):
                max_pair(1, k)
            with dve.Fori(0, NS - 2) as s:
                for k in range(LEAD, STEPS):
                    max_pair(s + 1, k)
                max_rows(s + 1)
                for k in range(LEAD):
                    max_pair(s + 2, k)
            for k in range(LEAD, STEPS):
                max_pair(NS - 1, k)
            dve.wait_ge(mrow_in[0], 32 * (NS - 1))
            max_rows(NS - 1)

            def stats(n, q, ready):
                dve.wait_ge(ready, q + 1)
                for t in range(QUAD):
                    ins = dve.bn_stats(st[:, q, t, :], res_bank(n, q)[:, t * D:(t + 1) * D])
                link(ins)
                for t in range(QUAD):
                    ins = dve.bn_aggr(mv[:, q, t, :], st[:, q, t, :])
                link(ins)
                dve.tensor_scalar(ve[:, q, :], mv[:, q, :, 1], EPS, None, ALU.add).then_inc(ln_var[n], 1)

            def shift(n, q):
                dve.wait_ge(ln_std[n], q + 1)
                dve.scalar_tensor_tensor(out=nb[:, q, :], in0=mv[:, q, :, 0], scalar=-1.0, in1=rstd[:, q, :],
                                         op0=ALU.mult, op1=ALU.mult).then_inc(ln_nb[n], 1)

            def norm(n, ready):
                stats(n, 0, ready)
                for q in range(1, NQ):
                    stats(n, q, ready)
                    shift(n, q - 1)
                shift(n, NQ - 1)

            def heads(layer, view):
                for t in range(NT):
                    dve.wait_ge(ot_ps[layer], t + 1)
                    o, total, r = view(t)
                    link(dve.reciprocal(r, total))
                    a = xT[:, t * D:(t + 1) * D]
                    dve.tensor_tensor(a.rearrange("p (h d) -> p h d", d=DH), o,
                                      r.unsqueeze(2).broadcast_to([P, H, DH]), ALU.mult).then_inc(ot_read[layer], 1)

            def view0(t):
                b = heads_bank(0, t).rearrange("p (h c) -> p h c", c=32)
                return b[:, :, 0:DH], b[:, :, DH], rec[:, t % 2, :]

            heads(0, view0)

            dve.wait_ge(ld_w1, 5 * 16)
            norm(0, wo_ps[0])
            norm(1, fm_ps)
            link(dve.tensor_tensor(rt[0][:, 0, :], sim_sb[:], sim_sb[:], ALU.mult))
            dve.sem_inc(sim_sq, 1)
            def select(q):
                dve.wait_ge(xT_sb[1], q + 1)
                if q >= 2:
                    dve.wait_ge(v_ps[1], q - 1)
                xs = attT[:, q % 2, :].rearrange("p (g dup k) -> p g dup k", g=QUAD, dup=2)
                for dup in range(2):
                    for g in range(QUAD):
                        at = q * QN + g * P
                        ins = dve.tensor_copy(xs[:, g, dup].rearrange("p (r two i) -> p r two i", two=2, i=16),
                                              kept(xT[:, at:at + P], 2))
                ins.then_inc(xsel_set, 1)

            select(0)
            select(1)
            for q in range(NQ):
                split(q, QN + QN // 2)
                if q + 2 < NQ:
                    select(q + 2)

            def seg_max(s):
                for h in range(HG):
                    n = s * (HG + 2) + h
                    dve.wait_ge(max_ps[1], n + 1)
                    dve.reduce_max(mx[:, h * KB:(h + 1) * KB], bank(h % 2).rearrange("p (g k) -> p g k", g=KB),
                                   AX_X).then_inc(max_done[1], 1)
                dve.wait_ge(max_done[1], s * (HG + 2) + HG)
                dve.sem_inc(max_all[1], 1)
                n = s * (HG + 2) + HG
                dve.wait_ge(max_ps[1], n + 2)
                if s:
                    dve.wait_ge(mrow_in[1], 32 * s)
                dve.tensor_scalar(mrow[:, 0, :], bank(0)[0:STEPS, 0:P], -1.0, None, ALU.mult).then_inc(max_done[1], 1)
                dve.wait_ge(max_done[1], n + 1)
                dve.scalar_tensor_tensor(out=mrow[:, 1, :], in0=bank(0)[0:STEPS, 0:P], scalar=-1.0, in1=mrow[:, 0, :],
                                         op0=ALU.mult, op1=ALU.subtract).then_inc(max_done[1], 1)
                dve.wait_ge(max_done[1], n + 2)
                dve.sem_inc(mrow_set[1], 1)

            def sim_norms():
                dve.wait_ge(sim_ss, 1)
                link(dve.tensor_copy(sim_n[:], bank(6)[:, 0:E]))
                dve.sem_inc(sim_root, 1)
                dve.wait_ge(gate_exp, 1)
                link(dve.tensor_scalar(gate_sb[:], gate_sb[:], 1.0, None, ALU.add))
                link(dve.reciprocal(gate_sb[:], gate_sb[:]))

            def sim_scale():
                dve.wait_ge(sim_root_done, 1)
                link(dve.tensor_scalar(sim_n[:], sim_n[:], 1e-12, None, ALU.max))
                link(dve.reciprocal(sim_n[:], sim_n[:]))
                link(dve.tensor_tensor(sim_n[:], sim_sb[:], sim_n[:], ALU.mult))
                dve.sem_inc(sim_ready, 1)

            def seg_o(s):
                dve.wait_ge(p_free[1], s + 1)
                dve.tensor_copy(o_seg[:, s * 512:(s + 1) * 512], bank(6 + s % 2)).then_inc(o_free[1], 1)

            seg_max(0)
            sim_norms()
            seg_max(1)
            for s in range(NS):
                if s + 2 < NS:
                    seg_max(s + 2)
                if s:
                    seg_o(s - 1)
                if s == 1:
                    sim_scale()
            seg_o(NS - 1)

            def view1(t):
                sp = t % 2
                b = bank(t % 8).rearrange("p (g s h c) -> p g s h c", g=G, s=2, h=4)[:, :, sp]
                return b[:, :, :, 0:DH], b[:, :, :, DH], rec[:, t % 2, :].rearrange("p (g h) -> p g h", g=G)

            for t in range(NT):
                dve.wait_ge(ot_ps[1], t + 1)
                o, total, r = view1(t)
                link(dve.reciprocal(r, total))
                a = xT[:, t * D:(t + 1) * D]
                dve.tensor_tensor(a.rearrange("p (g h d) -> p g h d", g=G, h=4), o,
                                  r.unsqueeze(3).broadcast_to([P, G, 4, DH]), ALU.mult).then_inc(ot_read[1], 1)
            norm(2, wo_ps[1])

            for q in range(NQ - 1):
                xq, sq = xb[:, q * QUAD:(q + 1) * QUAD, :], xa[:, q * QUAD:(q + 1) * QUAD, :]
                dve.wait_ge(ln_out[2], q + 1)
                link(dve.tensor_tensor(sq, xq, xq, ALU.mult))
                dve.reduce_sum(r1[0][:, q * QUAD:(q + 1) * QUAD], sq, AX_X).then_inc(nrm_ss[q // 2], 1)
            dve.wait_ge(nrm_root, 2)
            link(dve.tensor_scalar(r1[0][:], r1[0][:], 1e-12, None, ALU.max))
            link(dve.reciprocal(r1[0][:], r1[0][:]))
            def over_e(v):
                return v.unsqueeze(2).broadcast_to([P, NT, E])

            def over_t(v):
                return v.unsqueeze(1).broadcast_to([P, NT, E])

            lg, t1, fall, t3, t4, t5 = (r[:] for r in rt)
            r_top, top, r_a, r_b = (r[:] for r in r1)
            dve.wait_ge(lg_ps, 1)
            link(dve.tensor_tensor(lg, bank(7)[:, 0:NT * E].rearrange("p (t e) -> p t e", e=E), over_e(r1[0][:]),
                                   ALU.mult))
            link(dve.tensor_tensor(lg, lg, over_t(gate_sb[:]), ALU.subtract))
            link(dve.reduce_max(top, lg, AX_X))
            link(dve.tensor_scalar(r_top, top, 0.0, None, ALU.max))
            link(dve.scalar_tensor_tensor(out=t1, in0=lg, scalar=0.0, in1=over_e(r_top), op0=ALU.max,
                                          op1=ALU.subtract))
            dve.sem_inc(ex_in, 1)

            def first_of(values, best, one_hot, work):
                link(dve.tensor_tensor(work, values, over_e(best), ALU.is_equal))
                link(dve.tensor_tensor(work, work, over_t(rank_sb[:]), ALU.mult))
                link(dve.reduce_max(r_a, work, AX_X))
                link(dve.tensor_tensor(one_hot, work, over_e(r_a), ALU.is_equal))

            first_of(lg, top, fall, t5)
            link(dve.scalar_tensor_tensor(out=t3, in0=fall, scalar=-1e30, in1=lg, op0=ALU.mult, op1=ALU.add))
            link(dve.reduce_max(r_b, t3, AX_X))
            first_of(t3, r_b, t4, t5)
            link(dve.tensor_tensor(fall, fall, t4, ALU.add))
            dve.wait_ge(x3T_sb, NQ)
            dve.sem_inc(y_free, 2 * (E - 1))
            link(dve.tensor_scalar(r_a, top, 0.0, None, ALU.is_le))
            link(dve.tensor_tensor(fall, fall, over_e(r_a), ALU.mult))
            link(dve.scalar_tensor_tensor(out=fall, in0=lg, scalar=0.0, in1=fall, op0=ALU.is_gt, op1=ALU.add))
            dve.wait_ge(ex_out, 1)
            link(dve.tensor_tensor(t1, t1, fall, ALU.mult))
            link(dve.reduce_sum(r_a, t1, AX_X))
            link(dve.reciprocal(r_a, r_a))
            link(dve.tensor_tensor(w_rt[:], t1, over_e(r_a), ALU.mult))
            dve.sem_inc(tok_first, 4)
            dve.sem_inc(v_set, 4)
            dve.sem_inc(kq_ps, 4)
            dve.sem_inc(kq_sb, 4)
            dve.sem_inc(w_ready, 1)

            def weights(q, first):
                dve.tensor_copy(w_cur[:].rearrange("p t e -> p (t e)"),
                                w_rt[:].rearrange("p t e -> p (t e)")[:, bass.ds(q * QUAD * E, QUAD * E)])\
                   .then_inc(w_set, 1)
                dve.wait_ge(w_set, q + first + 1)

            adds = 2 * (E - 1)
            with dve.Fori(0, NQ) as i:
                weights(i, 0)
                for a in range(2):
                    pair = 2 * i + a
                    for e in range(1, E):
                        for u in range(2):
                            k = (pair + 1) * adds + 2 * (e - 1) + u
                            y, w = bank((2 * e + u) % YR)[:, 0:W3], w_cur[:, 2 * a + u, e:e + 1]
                            dve.wait_ge(y_ps, pair * 2 * E + 2 * e + u + 1)
                            if e == 1:
                                dve.wait_ge(tok_first, 2 * pair + u + 5)
                            else:
                                dve.wait_ge(y_free, k - 1)
                            dve.scalar_tensor_tensor(out=tok_cur[:, a, u, :], in0=y, scalar=w, in1=tok_cur[:, a, u, :],
                                                     op0=ALU.mult, op1=ALU.add).then_inc(y_free, 1)
                    dve.wait_ge(y_free, (pair + 2) * adds)
                    dve.sem_inc(tok_set, 2)

            def row_max(t, u):
                dve.wait_ge(sc_ps, t + 1)
                dve.reduce_max(m_cur[:, u, 0:1], bank(2 * u, 2), AX_X).then_inc(acc_step, 1)
                dve.wait_ge(acc_step, t + 1)
                dve.tensor_scalar(m_cur[:, u, 1:2], m_cur[:, u, 0:1], -scale_moe, None, ALU.mult).then_inc(nmax_set, 1)

            def pT_copy(t, u):
                dve.wait_ge(p_set, t + 3)
                dve.reciprocal(r_sum[:, bass.ds(t, 1)], m_cur[:, u, 2:3]).then_inc(fin_step, 1)
                dve.wait_ge(pt_ps, t + 2)
                dve.wait_ge(o_ps, t + 1)
                dve.tensor_copy(pT_cur[:, u, QN:2 * QN], bank(5)).then_inc(pt_sb, 1)

            row_max(0, 0)
            row_max(1, 1)
            pT_copy(0, 0)
            with dve.Fori(0, NT // 2 - 1) as i:
                for u in range(2):
                    t = 2 * i + u
                    row_max(t + 2, u)
                    pT_copy(t + 1, 1 - u)
            def divide(b):
                at = slice(b * KB, (b + 1) * KB)
                dve.wait_ge(fin_step, (b + 1) * KB)
                link(dve.tensor_tensor(w_rt[:, at], w_rt[:, at],
                                       r_sum[:, at].unsqueeze(2).broadcast_to([P, KB, E]), ALU.mult))
                dve.sem_inc(w_div, 1)

            dve.sem_inc(acc_step, 8)
            dve.sem_inc(y0_set, 4)
            divide(0)
            pT_copy(NT - 1, 1)
            divide(1)
            dve.sem_inc(fin_set, 2)
            dve.sem_inc(fin_std, 2)
            for u in range(2):
                dve.sem_inc(stored[u], 16)

            per = QUAD * (E - 4)

            with dve.Fori(0, NQ // 2) as i:
                for v in range(2):
                    q = 2 * i + v
                    weights(q, NQ)
                    for a in range(2):
                        for n in range(1, E // 4):
                            for j in range(4):
                                for u in range(2):
                                    t, e = 2 * a + u, 4 * n + j
                                    k = q * per + a * (per // 2) + 2 * (e - 4) + u
                                    z = bank((2 * (3 * a + n - 1) + u) % 4)[:, j * D:(j + 1) * D]
                                    if j == 0:
                                        dve.wait_ge(z_ps, q * 12 + a * 6 + 2 * (n - 1) + u + 1)
                                    if e == 4:
                                        dve.wait_ge(y0_set, q * QUAD + t + 5)
                                    else:
                                        dve.wait_ge(acc_step, NT + 8 + k - 1)
                                    dve.scalar_tensor_tensor(out=y_acc[:, v, t, :], in0=z, scalar=w_cur[:, t, e:e + 1],
                                                             in1=y_acc[:, v, t, :], op0=ALU.mult, op1=ALU.add)\
                                       .then_inc(acc_step, 1)
                    dve.wait_ge(acc_step, NT + 8 + (q + 1) * per)
                    for t in range(QUAD):
                        ins = dve.bn_stats(st[:, 0, t, :], y_acc[:, v, t, :])
                    ins.then_inc(fin_step, 1)
                    dve.wait_ge(fin_step, NT + 3 * q + 1)
                    dve.memset(tick[:, 0:1], 0.0).then_inc(fin_step, 1)
                    for t in range(QUAD):
                        ins = dve.bn_aggr(mv[:, 0, t, :], st[:, 0, t, :])
                    ins.then_inc(fin_step, 1)
                    dve.wait_ge(fin_step, NT + 3 * q + 3)
                    dve.wait_ge(fin_std, q + 1)
                    dve.tensor_scalar(nb[:, 2 + v, :], mv[:, 0, :, 0], -1.0, None, ALU.mult).then_inc(fin_var, 1)
                    dve.tensor_scalar(ve[:, v, :], mv[:, 0, :, 1], EPS, None, ALU.add).then_inc(fin_var, 1)


def constants():
    def bf16(a):
        a = np.asarray(a, np.float32).view(np.uint32).astype(np.uint64)
        return ((a + 0x7FFF + ((a >> 16) & 1)) >> 16).astype(np.uint16)

    def widen(a):
        return (a.astype(np.uint32) << 16).view(np.float32)

    n = np.arange(D)
    angle = 2.0 * np.pi * ((n[:, None] * n[None, :]) % D) / D
    start = 2.0 ** -0.5
    slope = np.array([start * start ** i for i in range(H)], np.float32)
    s1 = bf16(slope)
    s2 = bf16(slope - widen(s1))
    s3 = bf16(slope - widen(s1) - widen(s2))
    rows = np.stack([s1, s1, s2, s2, s3, s3])
    slopes = np.ascontiguousarray(np.broadcast_to(rows.reshape(N_BIAS, G, HG, 1).transpose(1, 0, 2, 3),
                                                  (G, N_BIAS, HG, S)).transpose(1, 0, 2, 3).reshape(N_BIAS, H * S))
    pos = np.arange(S) - (S - 1)
    hi = pos // 8 * 8
    kpos = np.stack([bf16(hi), bf16(pos - hi)] * PARTS)
    return {"ident": np.eye(P, dtype=np.float32), "c_cos": np.cos(angle).astype(np.float32),
            "c_sin": np.sin(angle).astype(np.float32), "c_nsin": (-np.sin(angle)).astype(np.float32),
            "slopes": slopes, "kpos": np.ascontiguousarray(kpos),
            "rank": np.ascontiguousarray(np.broadcast_to(np.arange(E, 0, -1, dtype=np.float32), (P, E)))}


_INS = ["L0_attn_x", "L0_attn_Wq", "L0_attn_Wk", "L0_attn_Wv", "L0_attn_Wo", "L0_ffn_w_freq_real",
        "L0_ffn_w_freq_imag", "L0_ffn_bias", "L1_attn_W_qkv", "L1_attn_W_out", "L1_ffn_sim_matrix", "L1_ffn_gates",
        "L1_ffn_q_proj", "L1_ffn_k_proj", "L1_ffn_v_proj", "L1_ffn_o_proj"]


def kernel(**inputs):
    import concourse.bacc as bacc
    from concourse.bass_utils import run_bass_kernel_spmd

    nc = bacc.Bacc("TRN2", target_bir_lowering=False, num_devices=1)
    arrays, args = {}, []
    for name in _INS:
        a = np.ascontiguousarray(inputs[name])
        arrays["in_" + name] = a
        args.append(nc.dram_tensor("in_" + name, a.shape, mybir.dt.from_np(a.dtype), kind="ExternalInput").ap())
    for name, a in constants().items():
        arrays["const_" + name] = a
        ap = nc.dram_tensor("const_" + name, a.shape, mybir.dt.from_np(a.dtype), kind="ExternalInput").ap()
        args.append(ap.bitcast(BF16) if a.dtype == np.uint16 else ap)
    args.append(nc.dram_tensor("out_x", (NB, S, D), F32, kind="ExternalOutput").ap())
    build(nc, *args)
    r = run_bass_kernel_spmd(nc, [arrays], core_ids=[0])
    return r.results[0]["out_x"]
```
